# Optimizing a Trainium2 kernel written in Bass

```python
import numpy as np
import jax
import jax.numpy as jnp

def _softmax(x, axis=-1):
    return jax.nn.softmax(x, axis=axis)

def _gelu(x):
    return jax.nn.gelu(x, approximate=True)

def _silu(x):
    return jax.nn.silu(x)

def _sigmoid(x):
    return jax.nn.sigmoid(x)

def _layernorm(x, axis=-1, eps=1e-05):
    m = jnp.mean(x, axis=axis, keepdims=True)
    v = jnp.var(x, axis=axis, keepdims=True)
    return (x - m) / jnp.sqrt(v + eps)

def _scatter_add(tgt, idx, src, axis=0):
    return tgt.at[idx].add(src)

def _segment_sum(src, seg, n):
    return jax.ops.segment_sum(src, seg, n)
kernel_name = 'mk_early_fusion_d1_tok_img1024_r4_37cdb2'

def setup_inputs(seed: int=0):
    np.random.seed(seed)
    _w = jnp.asarray

    def _rec_inputs():
        import jax
        import jax.numpy as jnp
        _rk = jax.random.key(seed)
        x = -0.00011082 + 0.999858 * jax.random.normal(jax.random.fold_in(_rk, 1), (4, 5, 128, 128), jnp.float32)
        txt = 1.3733e-10 + 0.999995 * jax.random.normal(jax.random.fold_in(_rk, 2), (4, 512, 256), jnp.float32)
        return (x, txt)
    x, txt = _rec_inputs()

    def _L0_tok_setup():
        import jax, jax.numpy as jnp
        import numpy as np
        PATCH = 8
        EPS = 1e-05

        def _patchify(x):
            B, C, H, Wd = x.shape
            p = PATCH
            x = x.reshape(B, C, H // p, p, Wd // p, p)
            x = x.transpose(0, 2, 4, 1, 3, 5)
            return x.reshape(B, H // p * (Wd // p), C * p * p)
        key = jax.random.key(seed)
        k1, k2 = jax.random.split(key)
        B, C, H, W_ = (32, 5, 128, 128)
        in_feat, embed_dim = (C * PATCH * PATCH, 256)
        x = jax.random.normal(k1, (B, C, H, W_), dtype=jnp.float32)
        W = jax.random.normal(k2, (in_feat, embed_dim), dtype=jnp.float32) * (1.0 / np.sqrt(in_feat))
        gamma = jnp.ones((embed_dim,), dtype=jnp.float32)
        return {'x': x, 'W': W, 'gamma': gamma}
    _L0_tok_all = _L0_tok_setup()
    _L0_tok_in = {k: v for k, v in _L0_tok_all.items() if k in ('W', 'gamma')}
    del _L0_tok_all

    def _L0_attn_setup():
        import jax, jax.numpy as jnp
        import numpy as np
        DIM = 256
        HEADS = 16
        DIM_HEAD = 64
        DIM_INNER = HEADS * DIM_HEAD
        SCALE = DIM_HEAD ** (-0.5)

        def rmsnorm(x, w):
            eps = jnp.asarray(jnp.finfo(x.dtype).eps, x.dtype)
            var = jnp.mean(jnp.square(x), axis=-1, keepdims=True)
            return x * jax.lax.rsqrt(var + eps) * w
        key = jax.random.key(seed)
        ks = jax.random.split(key, 6)
        tokens = jax.random.normal(ks[0], (2, 512, DIM), dtype=jnp.float32)
        norm_w = jnp.ones((DIM,), dtype=jnp.float32)
        Wq = jax.random.normal(ks[1], (DIM, DIM_INNER), dtype=jnp.float32) * 0.02
        Wkv = jax.random.normal(ks[2], (DIM, 2 * DIM_INNER), dtype=jnp.float32) * 0.02
        Wout = jax.random.normal(ks[3], (DIM_INNER, DIM), dtype=jnp.float32) * 0.02
        Wg = jax.random.normal(ks[4], (DIM, HEADS), dtype=jnp.float32) * 0.02
        return {'tokens': tokens, 'norm_w': norm_w, 'Wq': Wq, 'Wkv': Wkv, 'Wout': Wout, 'Wg': Wg}
    _L0_attn_all = _L0_attn_setup()
    _L0_attn_in = {k: v for k, v in _L0_attn_all.items() if k in ('norm_w', 'Wq', 'Wkv', 'Wout', 'Wg')}
    del _L0_attn_all

    def _L0_ffn_setup():
        import jax, jax.numpy as jnp
        import numpy as np
        NUM_EXPERTS = 8
        EXPERT_CAPACITY = 2.0
        key = jax.random.key(seed)
        k1, k2, k3, k4 = jax.random.split(key, 4)
        B, T, C, H, E = (4, 1024, 256, 1024, NUM_EXPERTS)
        x = jax.random.normal(k1, (B, T, C), jnp.float32)
        gate_w = jax.random.normal(k2, (C, E), jnp.float32) * 0.02
        w1 = jax.random.normal(k3, (E, C, H), jnp.float32) * 0.02
        w2 = jax.random.normal(k4, (E, H, C), jnp.float32) * 0.02
        return {'x': x, 'gate_w': gate_w, 'w1': w1, 'w2': w2}
    _L0_ffn_all = _L0_ffn_setup()
    _L0_ffn_in = {k: v for k, v in _L0_ffn_all.items() if k in ('gate_w', 'w1', 'w2')}
    del _L0_ffn_all
    return {'x': x, 'txt': txt, 'L0_tok_W': _L0_tok_in['W'], 'L0_tok_gamma': _L0_tok_in['gamma'], 'L0_attn_norm_w': _L0_attn_in['norm_w'], 'L0_attn_Wq': _L0_attn_in['Wq'], 'L0_attn_Wkv': _L0_attn_in['Wkv'], 'L0_attn_Wout': _L0_attn_in['Wout'], 'L0_attn_Wg': _L0_attn_in['Wg'], 'L0_ffn_gate_w': _L0_ffn_in['gate_w'], 'L0_ffn_w1': _L0_ffn_in['w1'], 'L0_ffn_w2': _L0_ffn_in['w2']}

def reference(x, txt, L0_tok_W, L0_tok_gamma, L0_attn_norm_w, L0_attn_Wq, L0_attn_Wkv, L0_attn_Wout, L0_attn_Wg, L0_ffn_gate_w, L0_ffn_w1, L0_ffn_w2):
    import jax
    import jax.numpy as jnp

    def _L0_tok_ref(x, W, gamma):
        import jax, jax.numpy as jnp
        import numpy as np
        PATCH = 8
        EPS = 1e-05

        def _patchify(x):
            B, C, H, Wd = x.shape
            p = PATCH
            x = x.reshape(B, C, H // p, p, Wd // p, p)
            x = x.transpose(0, 2, 4, 1, 3, 5)
            return x.reshape(B, H // p * (Wd // p), C * p * p)
        tokens = _patchify(x)
        h = jnp.einsum('bnf,fd->bnd', tokens, W)
        mu = jnp.mean(h, axis=-1, keepdims=True)
        var = jnp.mean(jnp.square(h - mu), axis=-1, keepdims=True)
        out = (h - mu) * jax.lax.rsqrt(var + EPS) * gamma
        return out

    def _L0_attn_ref(tokens, norm_w, Wq, Wkv, Wout, Wg):
        import jax, jax.numpy as jnp
        import numpy as np
        DIM = 256
        HEADS = 16
        DIM_HEAD = 64
        DIM_INNER = HEADS * DIM_HEAD
        SCALE = DIM_HEAD ** (-0.5)

        def rmsnorm(x, w):
            eps = jnp.asarray(jnp.finfo(x.dtype).eps, x.dtype)
            var = jnp.mean(jnp.square(x), axis=-1, keepdims=True)
            return x * jax.lax.rsqrt(var + eps) * w
        b, n, _ = tokens.shape
        x = rmsnorm(tokens, norm_w)
        q = x @ Wq
        kv = x @ Wkv
        k, v = jnp.split(kv, 2, axis=-1)

        def split_heads(t):
            return t.reshape(b, n, HEADS, DIM_HEAD).transpose(0, 2, 1, 3)
        q, k, v = map(split_heads, (q, k, v))
        sim = jnp.einsum('bhid,bhjd->bhij', q, k) * SCALE
        causal_mask = jnp.triu(jnp.ones((n, n), dtype=bool), k=1)
        sim = jnp.where(causal_mask, jnp.asarray(-jnp.finfo(sim.dtype).max, sim.dtype), sim)
        attn = jax.nn.softmax(sim, axis=-1)
        out = jnp.einsum('bhij,bhjd->bhid', attn, v)
        gates = jax.nn.sigmoid(x @ Wg)
        gates = gates.transpose(0, 2, 1)[..., None]
        out = gates * out
        out = out.transpose(0, 2, 1, 3).reshape(b, n, DIM_INNER)
        return out @ Wout

    def _L0_ffn_ref(x, gate_w, w1, w2):
        import jax, jax.numpy as jnp
        import numpy as np
        NUM_EXPERTS = 8
        EXPERT_CAPACITY = 2.0
        B, T, C = x.shape
        E = gate_w.shape[1]
        cap = int(EXPERT_CAPACITY * T / E)
        scores = jnp.einsum('BTC,CE->BTE', x, gate_w)
        probs = jax.nn.softmax(scores, axis=-1)
        probs_et = jnp.transpose(probs, (0, 2, 1))
        top_p, top_idx = jax.lax.top_k(probs_et, cap)
        xin = jnp.take_along_axis(x[:, None, :, :], top_idx[..., None], axis=2)
        h = jax.nn.gelu(jnp.einsum('BElC,ECH->BElH', xin, w1), approximate=False)
        y = jnp.einsum('BElH,EHC->BElC', h, w2)
        y = y * top_p[..., None]
        b_idx = jnp.arange(B)[:, None, None]
        out = jnp.zeros((B, T, C), x.dtype).at[b_idx, top_idx].add(y)
        return out
    h = _L0_tok_ref(x, L0_tok_W, L0_tok_gamma)
    h = jnp.concatenate([h, txt], axis=1)
    h = h + _L0_attn_ref(_layernorm(h, axis=-1), L0_attn_norm_w, L0_attn_Wq, L0_attn_Wkv, L0_attn_Wout, L0_attn_Wg)
    h = h + _L0_ffn_ref(_layernorm(h, axis=-1), L0_ffn_gate_w, L0_ffn_w1, L0_ffn_w2)
    return h

_drawn_inputs = setup_inputs


def setup_inputs(seed=0):
    import zlib

    import numpy as np

    out = dict(_drawn_inputs(seed))
    spreads = {'L0_tok_gamma': (1.0, 0.2), 'L0_attn_norm_w': (1.0, 0.6)}
    factors = {'L0_attn_Wq': 8.0,
     'L0_attn_Wkv': 5.487,
     'L0_attn_Wout': 5.486,
     'L0_attn_Wg': 8.0,
     'L0_ffn_gate_w': 8.0,
     'L0_ffn_w1': 8.0,
     'L0_ffn_w2': 8.0}
    for name, (base, spread) in spreads.items():
        noise = np.random.default_rng([zlib.crc32(name.encode()), seed]).standard_normal(out[name].shape)
        drawn = base * np.exp(spread * noise) if base else spread * noise
        out[name] = jnp.asarray(drawn.astype(out[name].dtype))
    for name, factor in factors.items():
        out[name] = (out[name] * factor).astype(out[name].dtype)
    return out
```

```python
from contextlib import ExitStack

import concourse.bass as bass
from concourse import mybir

F32 = mybir.dt.float32
F32R = mybir.dt.float32r
F16 = mybir.dt.float16
BF16 = mybir.dt.bfloat16
U32 = mybir.dt.uint32
ALU = mybir.AluOpType
ACT = mybir.ActivationFunctionType
AX = mybir.AxisListType
ds = bass.ds

P = 128
PATCH = 8
LN_EPS = 1e-5
RMS_EPS = 1.1920928955078125e-07
MASKED = -1e30
MAX_UNIT = 256.0

SCORE_PIECES = [
    [(0, 0, 512)],
    [(0, 512, 256), (4, 512, 256)],
    [(1, 128, 512)],
    [(1, 640, 128), (3, 384, 384)],
    [(2, 256, 512)],
    [(5, 640, 128)],
]
MAX_PIECES = [
    [(0, 0, 128, 0), (1, 0, 256, 1)],
    [(2, 0, 384, 2)],
    [(3, 0, 512, 3)],
    [(4, 0, 512, 4)],
    [(5, 0, 512, 5)],
    [(4, 512, 128, 6), (5, 512, 256, 7)],
]
NPIECE = len(SCORE_PIECES)


def piece_offsets():
    starts, where, at = [], {}, 0
    for piece in SCORE_PIECES:
        starts.append(at)
        for j, q0, w in piece:
            for q in range(q0, q0 + w, P):
                where[j, q // P] = at + q - q0
            at += w
    return starts, at, where


PIECE_START, PROB_COLS, PROB_AT = piece_offsets()


def fusion_block_kernel(nc, x, txt, tok_W, tok_gamma, norm_w, Wq, Wkv, Wout, Wg, gate_w, w1, w2, out):
    B, C_IN, IMG, _ = x.shape
    _, N_TXT, D = txt.shape
    GRID = IMG // PATCH
    N_IMG = GRID * GRID
    N = N_IMG + N_TXT
    NT = N // P
    NTI = N_IMG // P
    DC = D // P
    INNER = Wq.shape[1]
    HEADS = Wg.shape[1]
    DH = INNER // HEADS
    PAIRS = HEADS // 2
    COUPLES = PAIRS // 2
    E, _, HID = w1.shape
    HC = HID // P
    CAP = int(2.0 * N / E)
    SLOTS = B * CAP
    ST = SLOTS // P
    HALF = 384
    TH = HALF // P
    ROWS = C_IN * PATCH
    SHIFTS = 3
    TAPS = -(-PATCH // SHIFTS)
    VCOLS = INNER + HEADS
    V_PIECES = [(0, 5, 0), (5, 5, 0), (10, 6, HEADS)]
    SCALE = float(DH) ** -0.5
    assert (N, SLOTS, DC, NT, DH) == (2 * HALF, 2 * HALF, 2, 6, 64)

    x2_dram = nc.dram_tensor("ffn_rows", (B * N, D), F32, kind="Internal").ap()
    p_dram = nc.dram_tensor("router_probs", (B * E, N), F32, kind="Internal").ap()
    idx_dram = nc.dram_tensor("picked_rows", (E, B, CAP), U32, kind="Internal").ap()
    pv_dram = nc.dram_tensor("picked_probs", (E, B, CAP), F32, kind="Internal").ap()
    out_rows = out.rearrange("b n d -> (b n) d")

    top = ExitStack()
    with top:
        def sem(name):
            return top.enter_context(nc.semaphore(name))

        const_in = sem("const_in")
        qk_w_in = sem("qk_w_in")
        v_w_in = sem("v_w_in")
        o_w_in = sem("o_w_in")
        v_w_cut = sem("v_w_cut")
        o_w_cut = sem("o_w_cut")
        consts = sem("consts")
        img_in = sem("img_in")
        txt_in = sem("txt_in")
        pair_w = sem("pair_w")
        tok_full = sem("tok_full")
        ln = sem("ln")
        root_in = sem("root_in")
        root_out = sem("root_out")
        x_ready = sem("x_ready")
        xt_full = sem("xt_full")
        xt_hi = sem("xt_hi")
        xt_lo = sem("xt_lo")
        v_full = sem("v_full")
        v_hi_done = sem("v_hi_done")
        v_lo_done = sem("v_lo_done")
        gate_exp = sem("gate_exp")
        gate_ready = sem("gate_ready")
        pj_full = sem("pj_full")
        pj_hi = sem("pj_hi")
        pj_free = sem("pj_free")
        spread_q = sem("spread_q")
        spread_k = sem("spread_k")
        spread_m = [sem(f"spread_m_{hd}") for hd in range(2)]
        mx_full = sem("mx_full")
        mx_free = sem("mx_free")
        max_ready = sem("max_ready")
        mt_full = sem("mt_full")
        mt_copied = sem("mt_copied")
        st_full = sem("st_full")
        st_free = sem("st_free")
        p_lo_done = sem("p_lo_done")
        pv_done = sem("pv_done")
        normed = sem("normed")
        at_full = sem("at_full")
        at_hi = sem("at_hi")
        at_lo = sem("at_lo")
        op_full = sem("op_full")
        op_added = sem("op_added")
        x2_ready = sem("x2_ready")
        h_stored = sem("h_stored")
        x2t_full = sem("x2t_full")
        x2t_copied = sem("x2t_copied")
        logits_full = sem("logits_full")
        soft = sem("soft")
        logit_exp = sem("logit_exp")
        probs_ready = sem("probs_ready")
        pt_full = sem("pt_full")
        pt_copied = sem("pt_copied")
        p_stored = sem("p_stored")
        rows_in = sem("rows_in")
        pick = sem("pick")
        picks_stored = sem("picks_stored")
        picks_in = sem("picks_in")
        row_id = sem("row_id")
        w_raw_in = sem("w_raw_in")
        w_cut_hi = sem("w_cut_hi")
        w_cut_lo = sem("w_cut_lo")
        ids_copied = sem("ids_copied")
        gathered = [sem(f"gathered_{u}") for u in range(2)]
        scattered = sem("scattered")
        gt_full = sem("gt_full")
        gt_hi = sem("gt_hi")
        gt_lo = sem("gt_lo")
        h_full = sem("h_full")
        h_act = sem("h_act")
        h_lo_done = sem("h_lo_done")
        y_full = sem("y_full")
        y_ready = sem("y_ready")

        fence = sem("fence")

        def wait_apart(eng, s, value):
            eng.wait_ge(s, value)
            eng.sem_inc(fence, 1)

        PJ_CREDIT = 8
        PV_CREDIT = 2
        RING32 = 3
        LN_STEPS = 16
        SOFT_STEPS = 4
        IMG_DMAS = SHIFTS * C_IN
        H_CREDIT = 4

        small = ExitStack()
        with small:
            def sb_small(name, shape, dt):
                return small.enter_context(nc.sbuf_tensor(name, shape, dt))

            ident = sb_small("ident", [P, P], F32)

            attn = ExitStack()

            def sb(name, shape, dt):
                return attn.enter_context(nc.sbuf_tensor(name, shape, dt))

            wq_raw = sb("wq_raw", [P, DC, INNER], F32)
            wk_raw = sb("wk_raw", [P, DC, INNER], F32)
            stage = sb("stage", [P, DC * VCOLS], F32)
            wv = [sb(f"wv_{s}", [P, DC, VCOLS], F32R) for s in ("hi", "lo")]
            wo = [sb(f"wo_{s}", [P, PAIRS, D], F32R) for s in ("hi", "lo")]
            wp = [[sb(f"wp{u}_{s}", [P, 2, DC, P], F32R) for s in ("hi", "lo")] for u in range(2)]
            tok_w = sb("tok_w", [P, TAPS, D], F32)
            gamma = sb("gamma", [P, D], F32)
            nw = sb("nw", [P, DC], F32)
            gw = sb("gw", [P, DC, E], F32)
            ident_b = sb("ident_b", [P, P], BF16)
            mask_q = sb("mask_q", [P, P], BF16)
            mask_k = sb("mask_k", [P, P], BF16)
            img = sb("img", [P, GRID, IMG], F32)
            h = sb("h", [P, NT, D], F32)
            xn = sb("xn", [P, NT, D], F32)
            xT = [sb(f"xT_{s}", [P, DC, N], F32R) for s in ("hi", "lo")]
            cut = [[sb(f"cut_{w}_{s}", [P, N], F16) for s in ("hi", "lo")] for w in "qk"]
            key_both = sb("key_both", [P, 2, 2, N], F16)
            key_max = sb("key_max", [P, 2, 2, N], F16)
            query_both = sb("query_both", [P, 2, 2, N], F16)
            query_max = sb("query_max", [P, 2, 2, N], F16)
            v_hi = sb("v_hi", [P, NT, HEADS, DH + 1], F16)
            v_lo = sb("v_lo", [P, NT, HEADS, DH], F16)
            p32 = sb("p32", [P, RING32, 512], F32)
            p_hi = sb("p_hi", [P, 2, PROB_COLS], F16)
            p_lo = sb("p_lo", [P, 2, PROB_COLS], F16)
            heads_out = sb("heads_out", [P, NT, P], F32)
            aT = [sb(f"aT_{s}", [P, 2, N], F32R) for s in ("hi", "lo")]
            gate = sb("gate", [P, NT, HEADS], F32)
            stats = sb("stats", [P, NT, 6], F32)
            mv = sb("mv", [P, NT, 2], F32)
            rt = sb("rt", [P, 6, NT], F32)
            mx = sb("mx", [P, 2, 8], F32)
            m_row = sb("m_row", [NT, 2, P], F16)
            den = sb("den", [P, 2, NT], F32)
            probs = sb("probs", [P, NT, E], F32)
            rsm = sb("rsm", [P, 3, NT], F32)
            pT = sb("pT", [E, N], F32)
            x2T = stage[:, 0:DC * N].rearrange("p (c n) -> p c n", c=DC)

            psum = ExitStack()

            def ps(name, shape):
                return psum.enter_context(nc.psum_tensor(name, shape, F32))

            st_b = ps("st_b", [P, 2, 512])
            mx_b = ps("mx_b", [P, 2, 512])
            pj_b = ps("pj_b", [P, 2, 512])
            o_b = ps("o_b", [P, 512])
            tr_b = ps("tr_b", [P, 512])
            o_v = o_b[:, 0:NT * (DH + 1)].rearrange("p (t d) -> p t d", t=NT)
            four = [st_b[:, 0], st_b[:, 1], mx_b[:, 0], mx_b[:, 1]]
            turn = [pj_b[:, 0], pj_b[:, 1], mx_b[:, 0], mx_b[:, 1]]

            with nc.Block() as block:
                @block.sync
                def _(sp):
                    sp.dma_start(gamma[:], tok_gamma.rearrange("(a d) -> a d", a=1).broadcast_to([P, D])).then_inc(const_in, 16)
                    for k in range(PATCH):
                        g = k % SHIFTS
                        src = tok_W.rearrange("(r q) d -> r q d", q=PATCH)[:, k, :]
                        sp.dma_start(tok_w[ROWS * g:ROWS * g + ROWS, k // SHIFTS, :], src).then_inc(const_in, 16)
                    for c in range(DC):
                        sp.dma_start(nw[:, c:c + 1], norm_w.rearrange("(c p a) -> c p a", p=P, a=1)[c]).then_inc(const_in, 16)
                    sp.dma_start(gw[:], gate_w.rearrange("(c p) e -> p c e", p=P)).then_inc(const_in, 16)

                    stage_v = stage[:].rearrange("p (c n) -> p c n", c=DC)

                    def load_batch(b):
                        sp.wait_ge(tok_full, NTI * b)
                        for g in range(SHIFTS):
                            for c in range(C_IN):
                                r = ROWS * g + PATCH * c
                                src = x[ds(b, 1), c].rearrange("a (g q) w -> (a q) g w", q=PATCH)
                                sp.dma_start(img[r:r + PATCH, :, 0:IMG - g], src[:, :, g:IMG]).then_inc(img_in, 16)
                        sp.wait_ge(h_stored, 32 * b)
                        sp.wait_ge(x2_ready, b)
                        src = txt[ds(b, 1)].rearrange("a (t p) d -> (a p) t d", p=P)
                        sp.dma_start(h[:, NTI:NT, :], src).then_inc(txt_in, 16)

                    def spread(which, n, u):
                        sp.wait_ge(pj_free, PJ_CREDIT + 4 * n + 2 * which + 2)
                        both, one = (query_both, query_max) if which == 0 else (key_both, key_max)
                        hi, lo = cut[which]
                        done = spread_q if which == 0 else spread_k
                        for hd in range(2):
                            half = slice(64 * hd, 64 * hd + 64)
                            if which == 0:
                                moves = [(both[0:64, u, hd, :], hi), (both[64:128, u, hd, :], hi), (one[0:64, u, hd, :], lo)]
                            else:
                                moves = [(both[0:64, u, hd, :], hi), (both[64:128, u, hd, :], lo), (one[0:64, u, hd, :], hi)]
                            for dst, src in moves:
                                sp.dma_start(dst, src[half, :]).then_inc(done, 16)

                    def max_rows(n, u):
                        for hd in range(2):
                            sp.wait_ge(mt_copied, 2 * n + hd + 1)
                            sp.dma_start(query_max[64:65, u, hd, :], m_row[:, hd, :]).then_inc(spread_m[hd], 16)

                    def next_pair(n, u):
                        spread(0, n, u)
                        spread(1, n, u)
                        max_rows(n, u)

                    def store_batch(b):
                        sp.wait_ge(op_added, 3 * COUPLES * (b + 1))
                        dst = out_rows[ds(b * N, N), :].rearrange("(t p) d -> p t d", p=P)
                        sp.dma_start(dst, h[:]).then_inc(h_stored, 16)
                        sp.wait_ge(x2_ready, b + 1)
                        dst = x2_dram[ds(b * N, N), :].rearrange("(t p) d -> p t d", p=P)
                        sp.dma_start(dst, xn[:]).then_inc(h_stored, 16)
                        sp.wait_ge(pt_copied, 2 * (b + 1))
                        sp.dma_start(p_dram[ds(b * E, E), :], pT[:]).then_inc(p_stored, 16)

                    wv_src = Wkv.rearrange("(c p) n -> p c n", p=P)
                    sp.dma_start(stage_v[:, :, 0:INNER], wv_src[:, :, INNER:2 * INNER]).then_inc(v_w_in, 16)
                    sp.dma_start(stage_v[:, :, INNER:VCOLS], Wg.rearrange("(c p) n -> p c n", p=P)).then_inc(v_w_in, 16)
                    with sp.Fori(0, B) as b:
                        load_batch(b)
                        next_pair(PAIRS * b, 0)
                        with sp.Fori(0, COUPLES - 1) as c:
                            next_pair(PAIRS * b + 2 * c + 1, 1)
                            next_pair(PAIRS * b + 2 * c + 2, 0)
                        next_pair(PAIRS * b + PAIRS - 1, 1)
                        store_batch(b)

                @block.gpsimd
                def _(pool):
                    pool.dma_start(wq_raw[:], Wq.rearrange("(c p) n -> p c n", p=P)).then_inc(qk_w_in, 16)
                    pool.dma_start(wk_raw[:], Wkv.rearrange("(c p) n -> p c n", p=P)[:, :, 0:INNER]).then_inc(qk_w_in, 16)
                    pool.memset(ident[:], 0.0)
                    pool.memset(ident_b[:], 0.0)
                    pool.memset(mask_q[:], 0.0)
                    pool.memset(mask_k[:], 0.0)
                    pool.memset(v_hi[:, :, :, DH:DH + 1], 1.0).then_inc(consts, 1)
                    pool.wait_ge(consts, 2)
                    for m in (ident, ident_b):
                        pool.affine_select(out=m[:], in_=m[:], compare_op=ALU.not_equal, fill=1.0, base=0,
                                           pattern=[[-1, P]], channel_multiplier=1)
                    pool.affine_select(out=mask_q[:], in_=mask_q[:], compare_op=ALU.is_ge, fill=MASKED, base=0,
                                       pattern=[[-1, P]], channel_multiplier=1)
                    pool.affine_select(out=mask_k[:], in_=mask_k[:], compare_op=ALU.is_ge, fill=MASKED, base=0,
                                       pattern=[[1, P]], channel_multiplier=-1).then_inc(consts, 1)
                    pool.wait_ge(v_w_cut, 2)
                    pool.dma_start(stage[:, 0:PAIRS * D].rearrange("p (k n) -> p k n", k=PAIRS),
                                   Wout.rearrange("(k p) n -> p k n", p=P)).then_inc(o_w_in, 16)

                    def split_pair(n, p, u):
                        pool.wait_ge(pj_free, 4 * n + PJ_CREDIT - 4)
                        cols = ds(p * P, P)
                        for i, raw in enumerate((wq_raw, wk_raw)):
                            pool.tensor_copy(wp[u][0][:, i], raw[:, :, cols]).then_inc(pair_w, 1)
                        wait_apart(pool, pair_w, 4 * n + 2)
                        for i, raw in enumerate((wq_raw, wk_raw)):
                            pool.tensor_tensor(wp[u][1][:, i], raw[:, :, cols], wp[u][0][:, i],
                                               ALU.subtract).then_inc(pair_w, 1)

                    pool.wait_ge(qk_w_in, 32)
                    with pool.Fori(0, B) as b:
                        with pool.Fori(0, COUPLES) as c:
                            for u in range(2):
                                split_pair(PAIRS * b + 2 * c + u, 2 * c + u, u)

                @block.tensor
                def _(pe):
                    def three_terms(dst, lhs, rhs, first, last):
                        terms = [(0, 0), (1, 0), (0, 1)]
                        for i, (a, c) in enumerate(terms):
                            mm = pe.matmul(dst, lhs[a], rhs[c], start=first and i == 0, stop=last and i == 2)
                        return mm

                    def project(which, n, u, has_out):
                        if which == 0:
                            pe.wait_ge(pair_w, 4 * n + 4)
                        for half in range(2):
                            pe.wait_ge(pj_free, 4 * n + 2 * which + half + 1 + PJ_CREDIT - 2)
                            for c in range(DC):
                                mm = three_terms(
                                    pj_b[:, half, 0:HALF],
                                    [w[:, which, c, :] for w in wp[u]],
                                    [t[:, c, HALF * half:HALF * half + HALF] for t in xT],
                                    c == 0, c == DC - 1)
                            mm.then_inc(pj_full, 1)

                    def max_pass(n, u, hd):
                        if hd == 0:
                            pe.wait_ge(spread_q, 96 * (n + 1))
                            pe.wait_ge(spread_k, 96 * (n + 1))
                        for i, piece in enumerate(MAX_PIECES):
                            pe.wait_ge(mx_free, 12 * n + 6 * hd + i + 1)
                            at = 0
                            for q, k0, w, _ in piece:
                                dst = mx_b[:, i % 2, at:at + w]
                                diag = k0 <= q * P < k0 + w
                                mm = pe.matmul(dst, query_both[:, u, hd, q * P:q * P + P],
                                               key_both[:, u, hd, k0:k0 + w], start=True, stop=not diag)
                                if diag:
                                    d0 = at + q * P - k0
                                    mm = pe.matmul(mx_b[:, i % 2, d0:d0 + P], ident_b[:], mask_q[:],
                                                   start=False, stop=True)
                                at += w
                            mm.then_inc(mx_full, 1)

                    def max_turn(n, hd, turned):
                        pe.wait_ge(max_ready, 2 * n + hd + 1)
                        if hd == 0:
                            pe.wait_ge(at_lo, 2 * turned)
                        else:
                            pe.wait_ge(mt_copied, 2 * n + 1)
                        pe.transpose(tr_b[0:NT, 0:P], mx[:, hd, 0:NT], ident[:]).then_inc(mt_full, 1)

                    def scores(n, u, hd):
                        pe.wait_ge(spread_m[hd], 16 * (n + 1))
                        for i, piece in enumerate(SCORE_PIECES):
                            pe.wait_ge(st_free, 12 * n + 6 * hd + i + 1)
                            at = 0
                            for j, q0, w in piece:
                                dst = st_b[:, i % 2, at:at + w]
                                ks = slice(j * P, j * P + P)
                                diag = q0 == j * P
                                pe.matmul(dst, key_both[:, u, hd, ks], query_both[:, u, hd, q0:q0 + w],
                                          start=True, stop=False)
                                mm = pe.matmul(dst, key_max[0:65, u, hd, ks], query_max[0:65, u, hd, q0:q0 + w],
                                               start=False, stop=not diag)
                                if diag:
                                    mm = pe.matmul(st_b[:, i % 2, at:at + P], ident_b[:], mask_k[:],
                                                   start=False, stop=True)
                                at += w
                            mm.then_inc(st_full, 1)

                    def weigh_values(n, hd, head):
                        pe.wait_ge(p_lo_done, RING32 + 12 * n + 6 * hd + 6)
                        pe.wait_ge(normed, 3 * (2 * n + hd))
                        for q in range(NT):
                            for j in range(q + 1):
                                ps_ = slice(PROB_AT[j, q], PROB_AT[j, q] + P)
                                first, last = j == 0, j == q
                                pe.matmul(o_v[:, q, 0:DH + 1], p_hi[:, hd, ps_], v_hi[:, j, ds(head, 1), :],
                                          start=first, stop=False)
                                pe.matmul(o_v[:, q, 0:DH], p_hi[:, hd, ps_], v_lo[:, j, ds(head, 1), :],
                                          start=False, stop=False)
                                mm = pe.matmul(o_v[:, q, 0:DH + 1], p_lo[:, hd, ps_], v_hi[:, j, ds(head, 1), :],
                                               start=False, stop=last)
                        mm.then_inc(pv_done, 1)

                    def turn_outputs(n, last):
                        pe.wait_ge(normed, 3 * (2 * n + 2))
                        pe.wait_ge(mt_copied, 2 * n + 2 if last else 2 * n + 4)
                        for half in range(2):
                            if half:
                                pe.wait_ge(at_lo, 2 * n + 1)
                            for t in range(TH):
                                mm = pe.transpose(tr_b[:, t * P:t * P + P], heads_out[:, TH * half + t, :], ident[:])
                            mm.then_inc(at_full, 1)

                    def project_out(n, c, couple, last):
                        pe.wait_ge(at_lo, 2 * n + 2)
                        pe.wait_ge(pj_free, PJ_CREDIT + 4 * n + (4 if last else 8))
                        pe.wait_ge(o_w_cut, 2)
                        for k in range(NT // 2):
                            if k == 2:
                                pe.wait_ge(op_added, 3 * couple + 1)
                            for t in range(2):
                                tok = slice((2 * k + t) * P, (2 * k + t) * P + P)
                                for u in range(2):
                                    mm = three_terms(pj_b[:, k % 2, D * t:D * t + D],
                                                     [a[:, u, tok] for a in aT],
                                                     [w[:, ds(2 * c + u, 1), :] for w in wo],
                                                     u == 0, u == 1)
                            mm.then_inc(op_full, 1)

                    def pair_step(n, p, u, last):
                        scores(n, u, 0)
                        if not last:
                            if u == 0:
                                pe.wait_ge(op_added, 3 * couple_of(n, u))
                            project(0, n + 1, 1 - u, False)
                        scores(n, u, 1)
                        if not last:
                            project(1, n + 1, 1 - u, False)
                        weigh_values(n, 0, 2 * p)
                        if not last:
                            max_pass(n + 1, 1 - u, 0)
                        weigh_values(n, 1, 2 * p + 1)
                        if not last:
                            max_turn(n + 1, 0, n)
                            max_pass(n + 1, 1 - u, 1)
                            max_turn(n + 1, 1, n)
                        turn_outputs(n, last)

                    couple_now = [None]

                    def couple_of(n, u):
                        return couple_now[0]

                    def couple_step(b, c, last):
                        couple_now[0] = COUPLES * b + c
                        n = PAIRS * b + 2 * c
                        pair_step(n, 2 * c, 0, False)
                        pair_step(n + 1, 2 * c + 1, 1, last)
                        project_out(n + 1, c, couple_now[0], last)

                    pe.sem_inc(pv_done, PV_CREDIT)
                    pe.wait_ge(consts, 3)
                    pe.wait_ge(const_in, 16 * (1 + PATCH + DC + 1))
                    with pe.Fori(0, B) as b:
                        pe.wait_ge(img_in, 16 * IMG_DMAS * (b + 1))
                        pe.wait_ge(st_free, 2 + 12 * PAIRS * b)
                        for t in range(NTI):
                            for k in range(TAPS):
                                rows = ROWS * min(SHIFTS, PATCH - SHIFTS * k)
                                gr = GRID // NTI
                                lhs = img[0:rows, gr * t:gr * t + gr, SHIFTS * k:IMG:PATCH]
                                mm = pe.matmul(st_b[:, t, 0:D], lhs, tok_w[0:rows, k, :],
                                               start=k == 0, stop=k == TAPS - 1)
                            mm.then_inc(tok_full, 1)
                        pe.wait_ge(x_ready, b + 1)
                        for i in range(4):
                            c, half = i // 2, i % 2
                            for t in range(TH):
                                mm = pe.transpose(turn[i][:, t * P:t * P + P],
                                                  xn[:, TH * half + t, c * P:c * P + P], ident[:])
                            mm.then_inc(xt_full, 1)
                        pe.wait_ge(xt_lo, 4 * (b + 1))
                        pe.wait_ge(v_w_cut, 2)
                        i = 0
                        for t in range(NT):
                            for h0, nh, ng in V_PIECES:
                                w = nh * DH + ng
                                if i >= 4:
                                    pe.wait_ge(v_lo_done, NT * 3 * b + i - 3)
                                for c in range(DC):
                                    mm = three_terms(four[i % 4][:, 0:w],
                                                     [a[:, c, t * P:t * P + P] for a in xT],
                                                     [a[:, c, h0 * DH:h0 * DH + w] for a in wv],
                                                     c == 0, c == DC - 1)
                                mm.then_inc(v_full, 1)
                                i += 1
                        pe.wait_ge(op_added, 3 * COUPLES * b)
                        project(0, PAIRS * b, 0, False)
                        project(1, PAIRS * b, 0, False)
                        pe.wait_ge(v_lo_done, NT * 3 * (b + 1))
                        for hd in range(2):
                            max_pass(PAIRS * b, 0, hd)
                            max_turn(PAIRS * b, hd, PAIRS * b)
                        with pe.Fori(0, COUPLES - 1) as c:
                            couple_step(b, c, False)
                        couple_step(b, COUPLES - 1, True)
                        pe.wait_ge(x2_ready, b + 1)
                        for i in range(4):
                            c, half = i // 2, i % 2
                            for t in range(TH):
                                mm = pe.transpose(turn[i][:, t * P:t * P + P],
                                                  xn[:, TH * half + t, c * P:c * P + P], ident[:])
                            mm.then_inc(x2t_full, 1)
                        pe.wait_ge(x2t_copied, 4 * (b + 1))
                        for t in range(NT):
                            for c in range(DC):
                                mm = pe.matmul(tr_b[:, t * E:t * E + E], x2T[:, c, t * P:t * P + P], gw[:, c, :],
                                               start=c == 0, stop=c == DC - 1)
                        mm.then_inc(logits_full, 1)
                        pe.wait_ge(probs_ready, b + 1)
                        for half in range(2):
                            for t in range(TH):
                                mm = pe.transpose(pj_b[0:E, half, t * P:t * P + P], probs[:, TH * half + t, :], ident[:])
                            mm.then_inc(pt_full, 1)

                @block.scalar
                def _(act):
                    def split_projection(which, n):
                        act.wait_ge(spread_q if which == 0 else spread_k, 96 * n)
                        for half in range(2):
                            act.wait_ge(pj_full, 4 * n + 2 * which + half + 1)
                            act.activation(cut[which][0][:, HALF * half:HALF * half + HALF],
                                           pj_b[:, half, 0:HALF], ACT.Copy).then_inc(pj_hi, 1)

                    def exponentials(n, hd):
                        act.wait_ge(pv_done, 2 * n + hd + 1)
                        for i, piece in enumerate(SCORE_PIECES):
                            w = sum(q[2] for q in piece)
                            act.wait_ge(st_full, 12 * n + 6 * hd + i + 1)
                            act.wait_ge(p_lo_done, 12 * n + 6 * hd + i + 1)
                            at = PIECE_START[i]
                            act.activation(p32[:, i % RING32, 0:w], st_b[:, i % 2, 0:w], ACT.Exp, scale=SCALE)
                            act.activation(p_hi[:, hd, at:at + w], st_b[:, i % 2, 0:w], ACT.Exp,
                                           scale=SCALE).then_inc(st_free, 1)

                    def max_row(n, hd):
                        act.wait_ge(mt_full, 2 * n + hd + 1)
                        act.wait_ge(spread_m[hd], 16 * n)
                        act.activation(m_row[:, hd, :], tr_b[0:NT, 0:P], ACT.Copy,
                                       scale=-1.0 / MAX_UNIT).then_inc(mt_copied, 1)

                    def turned_outputs(n, u, couple):
                        act.wait_ge(op_full, 3 * couple)
                        for half in range(2):
                            act.wait_ge(at_full, 2 * n + half + 1)
                            act.activation(aT[0][:, u, HALF * half:HALF * half + HALF], tr_b[:, 0:HALF],
                                           ACT.Copy).then_inc(at_hi, 1)

                    def pair_step(n, u, couple, last):
                        exponentials(n, 0)
                        if not last:
                            split_projection(0, n + 1)
                        exponentials(n, 1)
                        if not last:
                            split_projection(1, n + 1)
                            max_row(n + 1, 0)
                            max_row(n + 1, 1)
                        turned_outputs(n, u, couple)

                    def couple_step(b, c, last):
                        n, couple = PAIRS * b + 2 * c, COUPLES * b + c
                        pair_step(n, 0, couple, False)
                        pair_step(n + 1, 1, couple, last)

                    def root(k, b, src, dst):
                        act.wait_ge(root_in, 4 * b + k + 1)
                        act.activation(dst, src, ACT.Sqrt).then_inc(root_out, 1)

                    act.sem_inc(st_free, 2)
                    with act.Fori(0, B) as b:
                        root(0, b, rt[:, 0, 0:NTI], rt[:, 1, 0:NTI])
                        root(1, b, rt[:, 0, :], rt[:, 1, :])
                        root(2, b, rt[:, 0, :], rt[:, 1, :])
                        for i in range(4):
                            c, half = i // 2, i % 2
                            act.wait_ge(xt_full, 4 * b + i + 1)
                            act.activation(xT[0][:, c, HALF * half:HALF * half + HALF], turn[i][:, 0:HALF], ACT.Copy,
                                           scale=nw[:, c:c + 1]).then_inc(xt_hi, 1)
                        i = 0
                        for t in range(NT):
                            for h0, nh, ng in V_PIECES:
                                act.wait_ge(v_full, NT * 3 * b + i + 1)
                                if ng:
                                    act.activation(gate[:, t, :], four[i % 4][:, nh * DH:nh * DH + ng], ACT.Exp,
                                                   scale=-1.0)
                                act.activation(v_hi[:, t, h0:h0 + nh, 0:DH],
                                               four[i % 4][:, 0:nh * DH].rearrange("p (h d) -> p h d", d=DH),
                                               ACT.Copy).then_inc(v_hi_done, 1)
                                i += 1
                        split_projection(0, PAIRS * b)
                        split_projection(1, PAIRS * b)
                        max_row(PAIRS * b, 0)
                        max_row(PAIRS * b, 1)
                        with act.Fori(0, COUPLES - 1) as c:
                            couple_step(b, c, False)
                        couple_step(b, COUPLES - 1, True)
                        root(3, b, rt[:, 0, :], rt[:, 1, :])
                        for i in range(4):
                            c, half = i // 2, i % 2
                            act.wait_ge(x2t_full, 4 * b + i + 1)
                            act.activation(x2T[:, c, HALF * half:HALF * half + HALF], turn[i][:, 0:HALF],
                                           ACT.Copy).then_inc(x2t_copied, 1)
                        act.wait_ge(soft, SOFT_STEPS * b + 2)
                        act.activation(probs[:], probs[:], ACT.Exp).then_inc(logit_exp, 1)

                @block.vector
                def _(dve):
                    def split_projection(which, n):
                        for half in range(2):
                            dve.wait_ge(pj_hi, 4 * n + 2 * which + half + 1)
                            cols = slice(HALF * half, HALF * half + HALF)
                            dve.tensor_tensor(cut[which][1][:, cols], pj_b[:, half, 0:HALF], cut[which][0][:, cols],
                                              ALU.subtract).then_inc(pj_free, 1)

                    def low_parts(n, hd):
                        for i, piece in enumerate(SCORE_PIECES):
                            w = sum(q[2] for q in piece)
                            at = PIECE_START[i]
                            dve.wait_ge(st_free, 2 + 12 * n + 6 * hd + i + 1)
                            dve.tensor_tensor(p_lo[:, hd, at:at + w], p32[:, i % RING32, 0:w],
                                              p_hi[:, hd, at:at + w], ALU.subtract).then_inc(p_lo_done, 1)

                    def maxima(n, hd):
                        dve.wait_ge(mt_full, 2 * n)
                        for i, piece in enumerate(MAX_PIECES):
                            dve.wait_ge(mx_full, 12 * n + 6 * hd + i + 1)
                            at = 0
                            for _, _, w, col in piece:
                                r = dve.tensor_reduce(mx[:, hd, col:col + 1], mx_b[:, i % 2, at:at + w], AX.X, ALU.max)
                                at += w
                            r.then_inc(mx_free, 1)
                        dve.wait_ge(mx_free, 2 + 12 * n + 6 * hd + 6)
                        dve.tensor_tensor(mx[:, hd, 4:6], mx[:, hd, 4:6], mx[:, hd, 6:8], ALU.max).then_inc(max_ready, 1)

                    def normalise(n, hd, head):
                        k = 2 * n + hd
                        dve.wait_ge(pv_done, PV_CREDIT + k + 1)
                        dve.tensor_tensor(den[:, 0, :], o_v[:, :, DH], gate[:, :, ds(head, 1)].rearrange("p t a -> p (t a)"),
                                          ALU.mult).then_inc(normed, 1)
                        dve.wait_ge(normed, 3 * k + 1)
                        dve.reciprocal(den[:, 1, :], den[:, 0, :]).then_inc(normed, 1)
                        dve.wait_ge(normed, 3 * k + 2)
                        if hd == 0:
                            dve.wait_ge(at_full, 2 * n)
                        scale = den[:, 1, :].rearrange("p (t a) -> p t a", a=1).broadcast_to([P, NT, DH])
                        dve.tensor_tensor(heads_out[:, :, DH * hd:DH * hd + DH], o_v[:, :, 0:DH], scale,
                                          ALU.mult).then_inc(normed, 1)

                    def turned_outputs(n, u):
                        for half in range(2):
                            dve.wait_ge(at_hi, 2 * n + half + 1)
                            cols = slice(HALF * half, HALF * half + HALF)
                            dve.tensor_tensor(aT[1][:, u, cols], tr_b[:, 0:HALF], aT[0][:, u, cols],
                                              ALU.subtract).then_inc(at_lo, 1)

                    def add_out(couple):
                        dve.wait_ge(op_added, 3 * couple)
                        for k in range(NT // 2):
                            dve.wait_ge(op_full, 3 * couple + k + 1)
                            rows = h[:, 2 * k:2 * k + 2, :].rearrange("p t d -> p (t d)")
                            dve.tensor_tensor(rows, rows, pj_b[:, k % 2, :], ALU.add).then_inc(op_added, 1)

                    def pair_step(n, p, u, last):
                        low_parts(n, 0)
                        if not last:
                            split_projection(0, n + 1)
                        low_parts(n, 1)
                        if not last:
                            split_projection(1, n + 1)
                        normalise(n, 0, 2 * p)
                        if not last:
                            maxima(n + 1, 0)
                        normalise(n, 1, 2 * p + 1)
                        if not last:
                            maxima(n + 1, 1)
                        turned_outputs(n, u)

                    def couple_step(b, c, last):
                        n = PAIRS * b + 2 * c
                        pair_step(n, 2 * c, 0, False)
                        pair_step(n + 1, 2 * c + 1, 1, last)
                        add_out(COUPLES * b + c)

                    steps = [0]

                    def chain(b, ins, per=LN_STEPS, sem_=ln):
                        steps[0] += 1
                        ins.then_inc(sem_, 1)
                        dve.wait_ge(sem_, per * b + steps[0])

                    dve.memset(key_max[64:65], MAX_UNIT).then_inc(consts, 1)
                    dve.sem_inc(pj_free, PJ_CREDIT)
                    dve.sem_inc(mx_free, 2)
                    dve.sem_inc(p_lo_done, RING32)
                    stage_v = stage[:].rearrange("p (c n) -> p c n", c=DC)
                    stage_o = stage[:, 0:PAIRS * D].rearrange("p (k n) -> p k n", k=PAIRS)
                    for w, src, arrived, bytes_, done in ((wv, stage_v, v_w_in, 32, v_w_cut), (wo, stage_o, o_w_in, 16, o_w_cut)):
                        dve.wait_ge(arrived, bytes_)
                        dve.tensor_copy(w[0][:], src).then_inc(done, 1)
                        dve.wait_ge(done, 1)
                        dve.tensor_tensor(w[1][:], src, w[0][:], ALU.subtract).then_inc(done, 1)
                    dve.wait_ge(const_in, 16 * (1 + PATCH + DC + 1))
                    with dve.Fori(0, B) as b:
                        steps[0] = 0
                        for t in range(NTI):
                            dve.wait_ge(tok_full, NTI * b + t + 1)
                            s = dve.bn_stats(stats[:, t, :], st_b[:, t, 0:D])
                        chain(b, s)
                        dve.sem_inc(fence, 1)
                        for t in range(NTI):
                            s = dve.bn_aggr(mv[:, t, :], stats[:, t, :])
                        chain(b, s)
                        dve.tensor_scalar(rt[:, 0, 0:NTI], mv[:, 0:NTI, 1], LN_EPS, None, ALU.add).then_inc(root_in, 1)
                        dve.wait_ge(root_out, 4 * b + 1)
                        chain(b, dve.reciprocal(rt[:, 2, 0:NTI], rt[:, 1, 0:NTI]))
                        dve.wait_ge(h_stored, 32 * b)
                        for t in range(NTI):
                            s = dve.tensor_scalar(xn[:, t, :], st_b[:, t, 0:D], mv[:, t, 0:1], rt[:, 2, t:t + 1],
                                                  ALU.subtract, ALU.mult)
                        chain(b, s)
                        for t in range(NTI):
                            s = dve.tensor_tensor(h[:, t, :], xn[:, t, :], gamma[:], ALU.mult)
                        chain(b, s)
                        dve.wait_ge(txt_in, 16 * (b + 1))
                        for t in range(NT):
                            s = dve.bn_stats(stats[:, t, :], h[:, t, :])
                        chain(b, s)
                        dve.sem_inc(fence, 1)
                        for t in range(NT):
                            s = dve.bn_aggr(mv[:, t, :], stats[:, t, :])
                        chain(b, s)
                        dve.tensor_scalar(rt[:, 0, :], mv[:, :, 1], LN_EPS, None, ALU.add).then_inc(root_in, 1)
                        dve.wait_ge(root_out, 4 * b + 2)
                        chain(b, dve.reciprocal(rt[:, 2, :], rt[:, 1, :]))
                        chain(b, dve.tensor_tensor(rt[:, 3, :], rt[:, 2, :], rt[:, 2, :], ALU.mult))
                        chain(b, dve.tensor_tensor(rt[:, 4, :], rt[:, 3, :], mv[:, :, 1], ALU.mult))
                        dve.tensor_scalar(rt[:, 0, :], rt[:, 4, :], RMS_EPS, None, ALU.add).then_inc(root_in, 1)
                        dve.wait_ge(root_out, 4 * b + 3)
                        chain(b, dve.reciprocal(rt[:, 3, :], rt[:, 1, :]))
                        chain(b, dve.tensor_tensor(rt[:, 5, :], rt[:, 3, :], rt[:, 2, :], ALU.mult))
                        for t in range(NT):
                            s = dve.tensor_scalar(xn[:, t, :], h[:, t, :], mv[:, t, 0:1], rt[:, 5, t:t + 1],
                                                  ALU.subtract, ALU.mult)
                        s.then_inc(x_ready, 1)
                        for i in range(4):
                            c, half = i // 2, i % 2
                            dve.wait_ge(xt_hi, 4 * b + i + 1)
                            cols = slice(HALF * half, HALF * half + HALF)
                            dve.scalar_tensor_tensor(out=xT[1][:, c, cols], in0=turn[i][:, 0:HALF], scalar=nw[:, c:c + 1],
                                                     in1=xT[0][:, c, cols], op0=ALU.mult,
                                                     op1=ALU.subtract).then_inc(xt_lo, 1)
                        i = 0
                        for t in range(NT):
                            for h0, nh, ng in V_PIECES:
                                dve.wait_ge(v_hi_done, NT * 3 * b + i + 1)
                                dve.tensor_tensor(v_lo[:, t, h0:h0 + nh, :],
                                                  four[i % 4][:, 0:nh * DH].rearrange("p (h d) -> p h d", d=DH),
                                                  v_hi[:, t, h0:h0 + nh, 0:DH], ALU.subtract).then_inc(v_lo_done, 1)
                                i += 1
                        chain(b, dve.tensor_scalar(gate[:], gate[:], 1.0, None, ALU.add))
                        split_projection(0, PAIRS * b)
                        split_projection(1, PAIRS * b)
                        maxima(PAIRS * b, 0)
                        maxima(PAIRS * b, 1)
                        with dve.Fori(0, COUPLES - 1) as c:
                            couple_step(b, c, False)
                        couple_step(b, COUPLES - 1, True)
                        dve.wait_ge(op_added, 3 * COUPLES * (b + 1))
                        for t in range(NT):
                            s = dve.bn_stats(stats[:, t, :], h[:, t, :])
                        chain(b, s)
                        dve.sem_inc(fence, 1)
                        for t in range(NT):
                            s = dve.bn_aggr(mv[:, t, :], stats[:, t, :])
                        chain(b, s)
                        dve.tensor_scalar(rt[:, 0, :], mv[:, :, 1], LN_EPS, None, ALU.add).then_inc(root_in, 1)
                        dve.wait_ge(root_out, 4 * b + 4)
                        chain(b, dve.reciprocal(rt[:, 2, :], rt[:, 1, :]))
                        for t in range(NT):
                            s = dve.tensor_scalar(xn[:, t, :], h[:, t, :], mv[:, t, 0:1], rt[:, 2, t:t + 1],
                                                  ALU.subtract, ALU.mult)
                        s.then_inc(x2_ready, 1)
                        total = steps[0]
                        steps[0] = 0
                        logits = tr_b[:, 0:NT * E].rearrange("p (t e) -> p t e", e=E)

                        def wide(v):
                            return v.rearrange("p (t a) -> p t a", a=1).broadcast_to([P, NT, E])

                        dve.wait_ge(logits_full, b + 1)
                        chain(b, dve.tensor_reduce(rsm[:, 0, :], logits, AX.X, ALU.max), SOFT_STEPS, soft)
                        chain(b, dve.tensor_tensor(probs[:], logits, wide(rsm[:, 0, :]), ALU.subtract), SOFT_STEPS, soft)
                        dve.wait_ge(logit_exp, b + 1)
                        chain(b, dve.tensor_reduce(rsm[:, 1, :], probs[:], AX.X, ALU.add), SOFT_STEPS, soft)
                        chain(b, dve.reciprocal(rsm[:, 2, :], rsm[:, 1, :]), SOFT_STEPS, soft)
                        assert steps[0] == SOFT_STEPS
                        dve.tensor_tensor(probs[:], probs[:], wide(rsm[:, 2, :]), ALU.mult).then_inc(probs_ready, 1)
                        dve.wait_ge(p_stored, 16 * b)
                        for half in range(2):
                            dve.wait_ge(pt_full, 2 * b + half + 1)
                            dve.tensor_copy(pT[:, HALF * half:HALF * half + HALF],
                                            pj_b[0:E, half, 0:HALF]).then_inc(pt_copied, 1)
                    assert total == LN_STEPS, total

            psum.close()
            attn.close()

            exp = ExitStack()
            with exp:
                def sbe(name, shape, dt):
                    return exp.enter_context(nc.sbuf_tensor(name, shape, dt))

                def pse(name, shape):
                    return exp.enter_context(nc.psum_tensor(name, shape, F32))

                R = B * E
                TOP = 8
                ROUNDS = CAP // TOP
                W_CUTS = 16
                W1C = DC * HID * 2 // W_CUTS
                router = [sbe(f"router_{i}", [R, N], F32) for i in range(2)]
                top_p = sbe("top_p", [R, CAP], F32)
                top_i = sbe("top_i", [R, CAP], U32)
                top_f = sbe("top_f", [R, CAP], F32)
                row_base = sbe("row_base", [R, 3], F32)
                row_u = sbe("row_u", [R, 2], U32)
                ids = sbe("ids", [P, E, ST], U32)
                pvs = sbe("pvs", [P, E, ST], F32)
                ids_now = [sbe(f"ids_now_{u}", [P, ST], U32) for u in range(2)]
                w1_raw = sbe("w1_raw", [P, DC * HID], F32)
                w2_raw = sbe("w2_raw", [P, HC * D], F32)
                w1s = [[sbe(f"w1_{u}_{s}", [P, DC * HID], F32R) for s in ("hi", "lo")] for u in range(2)]
                w2s = [[sbe(f"w2_{u}_{s}", [P, HC * D], F32R) for s in ("hi", "lo")] for u in range(2)]
                rows = [sbe(f"rows_{u}", [P, ST, D], F32) for u in range(2)]
                gT = [sbe(f"gT_{s}", [P, DC, SLOTS], F32R) for s in ("hi", "lo")]
                h32 = sbe("h32", [P, H_CREDIT, HALF], F32)
                hT = [[sbe(f"hT_{g}_{s}", [P, HC, HALF], F32R) for s in ("hi", "lo")] for g in range(2)]
                ys = sbe("ys", [P, ST, D], F32)
                gt_b = pse("gt_b", [P, 2, 512])
                h_b = pse("h_b", [P, H_CREDIT, 512])
                y_b = pse("y_b", [P, 2, 512])

                with nc.Block() as block:
                    @block.sync
                    def _(sp):
                        def load_weights(e):
                            sp.wait_ge(w_cut_lo, W_CUTS * e)
                            sp.dma_start(w1_raw[:].rearrange("p (c n) -> p c n", c=DC),
                                         w1[ds(e, 1)].rearrange("a (c p) n -> (a p) c n", p=P)).then_inc(w_raw_in, 16)
                            sp.dma_start(w2_raw[:].rearrange("p (k n) -> p k n", k=HC),
                                         w2[ds(e, 1)].rearrange("a (k p) n -> (a p) k n", p=P)).then_inc(w_raw_in, 16)

                        sp.wait_ge(p_stored, 16 * B)
                        sp.wait_ge(h_stored, 32 * B)
                        sp.dma_start(router[0][:], p_dram[:]).then_inc(rows_in, 16)
                        load_weights(0)
                        sp.wait_ge(pick, 3 * ROUNDS + 3)
                        for b in range(B):
                            r = slice(E * b, E * b + E)
                            sp.dma_start(idx_dram[:, b, :], top_i[r, :]).then_inc(picks_stored, 16)
                            sp.dma_start(pv_dram[:, b, :], top_p[r, :]).then_inc(picks_stored, 16)
                        sp.wait_ge(picks_stored, 32 * B)
                        sp.dma_start(ids[:], idx_dram.rearrange("e b s -> e (b s)").rearrange(
                            "e (p t) -> p e t", t=ST)).then_inc(picks_in, 16)
                        sp.dma_start(pvs[:], pv_dram.rearrange("e b s -> e (b s)").rearrange(
                            "e (p t) -> p e t", t=ST)).then_inc(picks_in, 16)
                        with sp.Fori(1, E) as e:
                            load_weights(e)

                    @block.gpsimd
                    def _(pool):
                        def fetch_rows(e, u):
                            if not isinstance(e, int) or e > 1:
                                pool.wait_ge(scattered, 16 * ST * (e - 1))
                            pool.tensor_copy(ids_now[u][:], ids[:, ds(e, 1), :].rearrange("p a t -> p (a t)")).then_inc(ids_copied, 1)
                            wait_apart(pool, ids_copied, e + 1)
                            for t in range(ST):
                                pool.indirect_dma_start(
                                    out=rows[u][:, t, :], out_offset=None, in_=x2_dram,
                                    in_offset=bass.IndirectOffsetOnAxis(ap=ids_now[u][:, t:t + 1], axis=0)).then_inc(gathered[u], 16)

                        def scatter_rows(e, u):
                            pool.wait_ge(scattered, 16 * ST * e)
                            for t in range(ST):
                                pool.wait_ge(scattered, 16 * (ST * e + t))
                                wait_apart(pool, y_ready, ST * e + t + 1)
                                pool.indirect_dma_start(
                                    out=out_rows, out_offset=bass.IndirectOffsetOnAxis(ap=ids_now[u][:, t:t + 1], axis=0),
                                    in_=ys[:, t, :], in_offset=None, compute_op=ALU.add).then_inc(scattered, 16)

                        pool.iota(row_u[:, 0:1], pattern=[[0, 1]], base=0, channel_multiplier=1).then_inc(row_id, 1)
                        pool.wait_ge(picks_in, 32)
                        fetch_rows(0, 0)
                        with pool.Fori(0, E // 2 - 1) as i:
                            fetch_rows(2 * i + 1, 1)
                            scatter_rows(2 * i, 0)
                            fetch_rows(2 * i + 2, 0)
                            scatter_rows(2 * i + 1, 1)
                        fetch_rows(E - 1, 1)
                        scatter_rows(E - 2, 0)
                        scatter_rows(E - 1, 1)
                        pool.wait_ge(scattered, 16 * ST * E)

                    @block.tensor
                    def _(pe):
                        def three_terms(dst, lhs, rhs, first, last):
                            terms = [(0, 0), (1, 0), (0, 1)]
                            for i, (a, c) in enumerate(terms):
                                mm = pe.matmul(dst, lhs[a], rhs[c], start=first and i == 0, stop=last and i == 2)
                            return mm

                        def turn_rows(e, u, i):
                            pe.wait_ge(gathered[u], 16 * ST * i)
                            for k in range(4):
                                c, half = k // 2, k % 2
                                pe.wait_ge(gt_lo, 4 * e + max(k - 1, 0))
                                for t in range(TH):
                                    mm = pe.transpose(gt_b[:, k % 2, t * P:t * P + P],
                                                      rows[u][:, TH * half + t, c * P:c * P + P], ident[:])
                                mm.then_inc(gt_full, 1)

                        def first_layer(e, u, g):
                            if g == 0:
                                pe.wait_ge(w_cut_lo, W_CUTS * (e + 1))
                                pe.wait_ge(gt_lo, 4 * (e + 1))
                            for k in range(HC):
                                i = HC * g + k
                                pe.wait_ge(h_lo_done, 2 * HC * e + i + 1)
                                for c in range(DC):
                                    mm = three_terms(h_b[:, i % H_CREDIT, 0:HALF],
                                                     [w[:, c * HID + k * P:c * HID + k * P + P] for w in w1s[u]],
                                                     [a[:, c, HALF * g:HALF * g + HALF] for a in gT],
                                                     c == 0, c == DC - 1)
                                mm.then_inc(h_full, 1)

                        def second_layer(e, u, g):
                            pe.wait_ge(h_lo_done, H_CREDIT + 2 * HC * e + HC * (g + 1))
                            for t in range(TH):
                                i = TH * g + t
                                pe.wait_ge(y_ready, ST * e + max(i - 1, 0))
                                for k in range(HC):
                                    mm = three_terms(y_b[:, i % 2, 0:D],
                                                     [a[:, k, t * P:t * P + P] for a in hT[g]],
                                                     [w[:, k * D:k * D + D] for w in w2s[u]],
                                                     k == 0, k == HC - 1)
                                mm.then_inc(y_full, 1)

                        def expert(i, u, last):
                            e = 2 * i + u
                            first_layer(e, u, 0)
                            first_layer(e, u, 1)
                            second_layer(e, u, 0)
                            if not last:
                                turn_rows(e + 1, 1 - u, i + 1 + u)
                            second_layer(e, u, 1)

                        pe.sem_inc(y_full, ST)
                        turn_rows(0, 0, 1)
                        with pe.Fori(0, E // 2 - 1) as i:
                            expert(i, 0, False)
                            expert(i, 1, False)
                        expert(E // 2 - 1, 0, False)
                        expert(E // 2 - 1, 1, True)

                    @block.scalar
                    def _(act):
                        def split_weights(e, u, i):
                            if i == 0:
                                act.wait_ge(w_raw_in, 32 * (e + 1))
                                act.wait_ge(y_full, ST * e)
                            raw, to = (w1_raw, w1s[u][0]) if i < W_CUTS // 2 else (w2_raw, w2s[u][0])
                            c = slice(W1C * (i % (W_CUTS // 2)), W1C * (i % (W_CUTS // 2)) + W1C)
                            act.activation(to[:, c], raw[:, c], ACT.Copy).then_inc(w_cut_hi, 1)

                        def turned_rows(e):
                            for i in range(4):
                                c, half = i // 2, i % 2
                                act.wait_ge(gt_full, 4 * e + i + 1)
                                if i == 0:
                                    act.wait_ge(h_full, 2 * HC * e)
                                act.activation(gT[0][:, c, HALF * half:HALF * half + HALF], gt_b[:, i % 2, 0:HALF],
                                               ACT.Copy).then_inc(gt_hi, 1)

                        def expert(e, u, last):
                            for i in range(2 * HC):
                                g, k = i // HC, i % HC
                                act.wait_ge(h_full, 2 * HC * e + i + 1)
                                act.wait_ge(h_lo_done, 2 * HC * e + i + 1)
                                if k == 0:
                                    act.wait_ge(y_full, ST * e + TH * (g + 1))
                                act.activation(h32[:, i % H_CREDIT, :], h_b[:, i % H_CREDIT, 0:HALF], ACT.Gelu)
                                act.activation(hT[g][0][:, k, :], h_b[:, i % H_CREDIT, 0:HALF], ACT.Gelu).then_inc(h_act, 1)
                                if not last:
                                    split_weights(e + 1, 1 - u, i)
                            if not last:
                                turned_rows(e + 1)

                        for i in range(W_CUTS):
                            split_weights(0, 0, i)
                        turned_rows(0)
                        with act.Fori(0, E // 2 - 1) as i:
                            expert(2 * i, 0, False)
                            expert(2 * i + 1, 1, False)
                        expert(E - 2, 0, False)
                        expert(E - 1, 1, True)

                    @block.vector
                    def _(dve):
                        def split_weights(e, u, i):
                            k = i % (W_CUTS // 2)
                            raw, to = (w1_raw, w1s[u]) if i < W_CUTS // 2 else (w2_raw, w2s[u])
                            c = slice(W1C * k, W1C * k + W1C)
                            dve.wait_ge(w_cut_hi, W_CUTS * e + i + 1)
                            dve.tensor_tensor(to[1][:, c], raw[:, c], to[0][:, c], ALU.subtract).then_inc(w_cut_lo, 1)

                        def turned_rows(e):
                            for i in range(4):
                                c, half = i // 2, i % 2
                                dve.wait_ge(gt_hi, 4 * e + i + 1)
                                cols = slice(HALF * half, HALF * half + HALF)
                                dve.tensor_tensor(gT[1][:, c, cols], gt_b[:, i % 2, 0:HALF], gT[0][:, c, cols],
                                                  ALU.subtract).then_inc(gt_lo, 1)

                        def outputs(e, g):
                            if g == 0:
                                dve.wait_ge(scattered, 16 * ST * e)
                            for t in range(TH):
                                i = TH * g + t
                                dve.wait_ge(y_full, ST * (e + 1) + i + 1)
                                dve.tensor_scalar(ys[:, i, :], y_b[:, i % 2, 0:D],
                                                  pvs[:, ds(e, 1), i:i + 1].rearrange("p a t -> p (a t)"), None,
                                                  ALU.mult).then_inc(y_ready, 1)

                        def expert(e, u, last):
                            for i in range(2 * HC):
                                g, k = i // HC, i % HC
                                dve.wait_ge(h_act, 2 * HC * e + i + 1)
                                dve.tensor_tensor(hT[g][1][:, k, :], h32[:, i % H_CREDIT, :], hT[g][0][:, k, :],
                                                  ALU.subtract).then_inc(h_lo_done, 1)
                                if not last:
                                    split_weights(e + 1, 1 - u, i)
                            outputs(e, 0)
                            if not last:
                                turned_rows(e + 1)
                            outputs(e, 1)

                        dve.sem_inc(h_lo_done, H_CREDIT)
                        for i in range(W_CUTS):
                            split_weights(0, 0, i)
                        dve.wait_ge(rows_in, 16)
                        for i in range(ROUNDS):
                            now, then = router[i % 2], router[(i + 1) % 2]
                            eight = slice(TOP * i, TOP * i + TOP)
                            dve.max(top_p[:, eight], now[:]).then_inc(pick, 1)
                            dve.wait_ge(pick, 3 * i + 1)
                            dve.max_index(top_i[:, eight], top_p[:, eight], now[:]).then_inc(pick, 1)
                            dve.match_replace(then[:], top_p[:, eight], now[:], -1.0).then_inc(pick, 1)
                            dve.wait_ge(pick, 3 * i + 3)
                        dve.wait_ge(row_id, 1)
                        dve.tensor_scalar(row_u[:, 1:2], row_u[:, 0:1], E.bit_length() - 1, None,
                                          ALU.logical_shift_right).then_inc(row_id, 1)
                        dve.wait_ge(row_id, 2)
                        dve.tensor_scalar(row_base[:, 0:1], row_u[:, 1:2], float(N), None, ALU.mult).then_inc(row_id, 1)
                        dve.tensor_copy(top_f[:], top_i[:]).then_inc(pick, 1)
                        dve.wait_ge(row_id, 3)
                        dve.wait_ge(pick, 3 * ROUNDS + 1)
                        dve.tensor_scalar(top_f[:], top_f[:], row_base[:, 0:1], None, ALU.add).then_inc(pick, 1)
                        dve.wait_ge(pick, 3 * ROUNDS + 2)
                        dve.tensor_copy(top_i[:], top_f[:]).then_inc(pick, 1)
                        dve.wait_ge(picks_in, 32)
                        turned_rows(0)
                        with dve.Fori(0, E // 2 - 1) as i:
                            expert(2 * i, 0, False)
                            expert(2 * i + 1, 1, False)
                        expert(E - 2, 0, False)
                        expert(E - 1, 1, True)


_INS = ["x", "txt", "L0_tok_W", "L0_tok_gamma", "L0_attn_norm_w", "L0_attn_Wq", "L0_attn_Wkv", "L0_attn_Wout",
        "L0_attn_Wg", "L0_ffn_gate_w", "L0_ffn_w1", "L0_ffn_w2"]


def kernel(**inputs):
    import numpy as _np
    import concourse.bacc as _bacc
    from concourse import mybir as _mybir
    from concourse.bass_utils import run_bass_kernel_spmd as _run

    nc = _bacc.Bacc("TRN2", target_bir_lowering=False, num_devices=1)
    arrays, args = {}, []
    for name in _INS:
        a = _np.ascontiguousarray(inputs[name])
        arrays[f"in_{name}"] = a
        args.append(nc.dram_tensor(f"in_{name}", a.shape, _mybir.dt.from_np(a.dtype), kind="ExternalInput").ap())
    B, _, img, _ = inputs["x"].shape
    _, n_txt, d = inputs["txt"].shape
    shape = (B, (img // PATCH) ** 2 + n_txt, d)
    args.append(nc.dram_tensor("out_0", shape, _mybir.dt.float32, kind="ExternalOutput").ap())
    fusion_block_kernel(nc, *args)
    r = _run(nc, [arrays], core_ids=[0])
    return r.results[0]["out_0"]
```

```python
from contextlib import ExitStack

import concourse.bass as bass
from concourse import mybir

F32 = mybir.dt.float32
F32R = mybir.dt.float32r
F16 = mybir.dt.float16
BF16 = mybir.dt.bfloat16
U32 = mybir.dt.uint32
ALU = mybir.AluOpType
ACT = mybir.ActivationFunctionType
AX = mybir.AxisListType
ds = bass.ds

P = 128
PATCH = 8
LN_EPS = 1e-5
RMS_EPS = 1.1920928955078125e-07
MASKED = -1e30
MAX_UNIT = 256.0

SCORE_PIECES = [
    [(0, 0, 512)],
    [(0, 512, 256), (4, 512, 256)],
    [(1, 128, 512)],
    [(1, 640, 128), (3, 384, 384)],
    [(2, 256, 512)],
    [(5, 640, 128)],
]
MAX_PIECES = [
    [(0, 0, 128, 0), (1, 0, 256, 1)],
    [(2, 0, 384, 2)],
    [(3, 0, 512, 3)],
    [(4, 0, 512, 4)],
    [(5, 0, 512, 5)],
    [(4, 512, 128, 6), (5, 512, 256, 7)],
]
NPIECE = len(SCORE_PIECES)


def piece_offsets():
    starts, where, at = [], {}, 0
    for piece in SCORE_PIECES:
        starts.append(at)
        for j, q0, w in piece:
            for q in range(q0, q0 + w, P):
                where[j, q // P] = at + q - q0
            at += w
    return starts, at, where


PIECE_START, PROB_COLS, PROB_AT = piece_offsets()


def fusion_block_kernel(nc, x, txt, tok_W, tok_gamma, norm_w, Wq, Wkv, Wout, Wg, gate_w, w1, w2, out):
    B, C_IN, IMG, _ = x.shape
    _, N_TXT, D = txt.shape
    GRID = IMG // PATCH
    N_IMG = GRID * GRID
    N = N_IMG + N_TXT
    NT = N // P
    NTI = N_IMG // P
    DC = D // P
    INNER = Wq.shape[1]
    HEADS = Wg.shape[1]
    DH = INNER // HEADS
    PAIRS = HEADS // 2
    COUPLES = PAIRS // 2
    E, _, HID = w1.shape
    HC = HID // P
    CAP = int(2.0 * N / E)
    SLOTS = B * CAP
    ST = SLOTS // P
    HALF = 384
    TH = HALF // P
    ROWS = C_IN * PATCH
    SHIFTS = 3
    TAPS = -(-PATCH // SHIFTS)
    VCOLS = INNER + HEADS
    V_PIECES = [(0, 5, 0), (5, 5, 0), (10, 6, HEADS)]
    SCALE = float(DH) ** -0.5
    assert (N, SLOTS, DC, NT, DH) == (2 * HALF, 2 * HALF, 2, 6, 64)

    x2_dram = nc.dram_tensor("ffn_rows", (B * N, D), F32, kind="Internal").ap()
    p_dram = nc.dram_tensor("router_probs", (B * E, N), F32, kind="Internal").ap()
    idx_dram = nc.dram_tensor("picked_rows", (E, B, CAP), U32, kind="Internal").ap()
    pv_dram = nc.dram_tensor("picked_probs", (E, B, CAP), F32, kind="Internal").ap()
    out_rows = out.rearrange("b n d -> (b n) d")

    top = ExitStack()
    with top:
        def sem(name):
            return top.enter_context(nc.semaphore(name))

        const_in = sem("const_in")
        qk_w_in = sem("qk_w_in")
        v_w_in = sem("v_w_in")
        o_w_in = sem("o_w_in")
        v_w_cut = sem("v_w_cut")
        o_w_cut = sem("o_w_cut")
        consts = sem("consts")
        img_in = sem("img_in")
        txt_in = sem("txt_in")
        pair_w = sem("pair_w")
        tok_full = sem("tok_full")
        ln = sem("ln")
        root_in = sem("root_in")
        root_out = sem("root_out")
        x_ready = sem("x_ready")
        xt_full = sem("xt_full")
        xt_hi = sem("xt_hi")
        xt_lo = sem("xt_lo")
        v_full = sem("v_full")
        v_hi_done = sem("v_hi_done")
        v_lo_done = sem("v_lo_done")
        gate_exp = sem("gate_exp")
        gate_ready = sem("gate_ready")
        pj_full = sem("pj_full")
        pj_hi = sem("pj_hi")
        pj_free = sem("pj_free")
        spread_q = sem("spread_q")
        spread_k = sem("spread_k")
        spread_m = [sem(f"spread_m_{hd}") for hd in range(2)]
        mx_full = sem("mx_full")
        mx_free = sem("mx_free")
        max_ready = sem("max_ready")
        mt_full = sem("mt_full")
        mt_copied = sem("mt_copied")
        st_full = sem("st_full")
        st_free = sem("st_free")
        p_lo_done = sem("p_lo_done")
        pv_done = sem("pv_done")
        normed = sem("normed")
        at_full = sem("at_full")
        at_hi = sem("at_hi")
        at_lo = sem("at_lo")
        op_full = sem("op_full")
        op_added = sem("op_added")
        x2_ready = sem("x2_ready")
        h_stored = sem("h_stored")
        x2t_full = sem("x2t_full")
        x2t_copied = sem("x2t_copied")
        logits_full = sem("logits_full")
        soft = sem("soft")
        logit_exp = sem("logit_exp")
        probs_ready = sem("probs_ready")
        pt_full = sem("pt_full")
        pt_copied = sem("pt_copied")
        p_stored = sem("p_stored")
        rows_in = sem("rows_in")
        pick = sem("pick")
        picks_stored = sem("picks_stored")
        picks_in = sem("picks_in")
        row_id = sem("row_id")
        w_raw_in = sem("w_raw_in")
        w_cut_hi = sem("w_cut_hi")
        w_cut_lo = sem("w_cut_lo")
        ids_copied = sem("ids_copied")
        gathered = [sem(f"gathered_{u}") for u in range(2)]
        scattered = sem("scattered")
        gt_full = sem("gt_full")
        gt_hi = sem("gt_hi")
        gt_lo = sem("gt_lo")
        h_full = sem("h_full")
        h_act = sem("h_act")
        h_lo_done = sem("h_lo_done")
        y_full = sem("y_full")
        y_ready = sem("y_ready")

        fence = sem("fence")

        def is_first_couple(c):
            return isinstance(c, int) and c == 0

        def is_last_couple(c):
            return isinstance(c, int) and c == COUPLES - 1

        def wait_apart(eng, s, value):
            eng.wait_ge(s, value)
            eng.sem_inc(fence, 1)

        PJ_CREDIT = 8
        PV_CREDIT = 2
        SPREAD = 6 * 16
        RING32 = 3
        LN_STEPS = 16
        SOFT_STEPS = 4
        IMG_DMAS = SHIFTS * C_IN
        H_CREDIT = 4

        small = ExitStack()
        with small:
            def sb_small(name, shape, dt):
                return small.enter_context(nc.sbuf_tensor(name, shape, dt))

            ident = sb_small("ident", [P, P], F32)

            attn = ExitStack()

            def sb(name, shape, dt):
                return attn.enter_context(nc.sbuf_tensor(name, shape, dt))

            wq_raw = sb("wq_raw", [P, DC, INNER], F32)
            wk_raw = sb("wk_raw", [P, DC, INNER], F32)
            stage = sb("stage", [P, DC * VCOLS], F32)
            wv = [sb(f"wv_{s}", [P, DC, VCOLS], F32R) for s in ("hi", "lo")]
            wo = [sb(f"wo_{s}", [P, PAIRS, D], F32R) for s in ("hi", "lo")]
            wp = [[sb(f"wp{u}_{s}", [P, 2, DC, P], F32R) for s in ("hi", "lo")] for u in range(2)]
            tok_w = sb("tok_w", [P, TAPS, D], F32)
            gamma = sb("gamma", [P, D], F32)
            nw = sb("nw", [P, DC], F32)
            gw = sb("gw", [P, DC, E], F32)
            ident_b = sb("ident_b", [P, P], BF16)
            mask_q = sb("mask_q", [P, P], BF16)
            mask_k = sb("mask_k", [P, P], BF16)
            img = sb("img", [P, GRID, IMG], F32)
            h = sb("h", [P, NT, D], F32)
            xn = sb("xn", [P, NT, D], F32)
            xT = [sb(f"xT_{s}", [P, DC, N], F32R) for s in ("hi", "lo")]
            cut = [[sb(f"cut_{w}_{s}", [P, N], F16) for s in ("hi", "lo")] for w in "qk"]
            key_both = sb("key_both", [P, 2, 2, N], F16)
            key_max = sb("key_max", [P, 2, 2, N], F16)
            query_both = sb("query_both", [P, 2, 2, N], F16)
            query_max = sb("query_max", [P, 2, 2, N], F16)
            v_hi = sb("v_hi", [P, NT, HEADS, DH + 1], F16)
            v_lo = sb("v_lo", [P, NT, HEADS, DH], F16)
            p32 = sb("p32", [P, RING32, 512], F32)
            p_hi = sb("p_hi", [P, 2, PROB_COLS], F16)
            p_lo = sb("p_lo", [P, 2, PROB_COLS], F16)
            heads_out = sb("heads_out", [P, NT, P], F32)
            aT = [sb(f"aT_{s}", [P, 2, N], F32R) for s in ("hi", "lo")]
            gate = sb("gate", [P, NT, HEADS], F32)
            stats = sb("stats", [P, NT, 6], F32)
            mv = sb("mv", [P, NT, 2], F32)
            rt = sb("rt", [P, 6, NT], F32)
            mx = sb("mx", [P, 2, 8], F32)
            m_row = sb("m_row", [NT, 2, P], F16)
            den = sb("den", [P, 2, NT], F32)
            probs = sb("probs", [P, NT, E], F32)
            rsm = sb("rsm", [P, 3, NT], F32)
            pT = sb("pT", [E, N], F32)
            x2T = stage[:, 0:DC * N].rearrange("p (c n) -> p c n", c=DC)

            psum = ExitStack()

            def ps(name, shape):
                return psum.enter_context(nc.psum_tensor(name, shape, F32))

            st_b = ps("st_b", [P, 2, 512])
            mx_b = ps("mx_b", [P, 2, 512])
            pj_b = ps("pj_b", [P, 2, 512])
            o_b = ps("o_b", [P, 512])
            tr_b = ps("tr_b", [P, 512])
            o_v = o_b[:, 0:NT * (DH + 1)].rearrange("p (t d) -> p t d", t=NT)
            four = [st_b[:, 0], st_b[:, 1], mx_b[:, 0], mx_b[:, 1]]
            turn = [pj_b[:, 0], pj_b[:, 1], mx_b[:, 0], mx_b[:, 1]]

            with nc.Block() as block:
                @block.sync
                def _(sp):
                    sp.dma_start(gamma[:], tok_gamma.rearrange("(a d) -> a d", a=1).broadcast_to([P, D])).then_inc(const_in, 16)
                    for k in range(PATCH):
                        g = k % SHIFTS
                        src = tok_W.rearrange("(r q) d -> r q d", q=PATCH)[:, k, :]
                        sp.dma_start(tok_w[ROWS * g:ROWS * g + ROWS, k // SHIFTS, :], src).then_inc(const_in, 16)
                    for c in range(DC):
                        sp.dma_start(nw[:, c:c + 1], norm_w.rearrange("(c p a) -> c p a", p=P, a=1)[c]).then_inc(const_in, 16)
                    sp.dma_start(gw[:], gate_w.rearrange("(c p) e -> p c e", p=P)).then_inc(const_in, 16)

                    stage_v = stage[:].rearrange("p (c n) -> p c n", c=DC)

                    def load_batch(b):
                        sp.wait_ge(tok_full, NTI * b)
                        for g in range(SHIFTS):
                            for c in range(C_IN):
                                r = ROWS * g + PATCH * c
                                src = x[ds(b, 1), c].rearrange("a (g q) w -> (a q) g w", q=PATCH)
                                sp.dma_start(img[r:r + PATCH, :, 0:IMG - g], src[:, :, g:IMG]).then_inc(img_in, 16)
                        sp.wait_ge(h_stored, 32 * b)
                        sp.wait_ge(x2_ready, b)
                        src = txt[ds(b, 1)].rearrange("a (t p) d -> (a p) t d", p=P)
                        sp.dma_start(h[:, NTI:NT, :], src).then_inc(txt_in, 16)

                    def spread(which, n, u):
                        sp.wait_ge(pj_free, PJ_CREDIT + 4 * n + 2 * which + 2)
                        both, one = (query_both, query_max) if which == 0 else (key_both, key_max)
                        hi, lo = cut[which]
                        done = spread_q if which == 0 else spread_k
                        for hd in range(2):
                            half = slice(DH * hd, DH * hd + DH)
                            if which == 0:
                                moves = [(both[0:64, u, hd], hi), (both[64:128, u, hd], hi), (one[0:64, u, hd], lo)]
                            else:
                                moves = [(both[0:64, u, hd], hi), (both[64:128, u, hd], lo), (one[0:64, u, hd], hi)]
                            for dst, src in moves:
                                sp.dma_start(dst, src[half, :]).then_inc(done, 16)

                    def max_row(n, u, hd):
                        sp.wait_ge(mt_copied, 2 * n + hd + 1)
                        sp.dma_start(query_max[64:65, u, hd, :], m_row[:, hd, :]).then_inc(spread_m[hd], 16)

                    def pair_step(n, u, last):
                        if not last:
                            sp.wait_ge(st_full, 12 * n)
                            spread(0, n + 1, 1 - u)
                            spread(1, n + 1, 1 - u)
                        max_row(n, u, 1)
                        if not last:
                            max_row(n + 1, 1 - u, 0)

                    def store_batch(b):
                        sp.wait_ge(op_added, 3 * COUPLES * (b + 1))
                        dst = out_rows[ds(b * N, N), :].rearrange("(t p) d -> p t d", p=P)
                        sp.dma_start(dst, h[:]).then_inc(h_stored, 16)
                        sp.wait_ge(x2_ready, b + 1)
                        dst = x2_dram[ds(b * N, N), :].rearrange("(t p) d -> p t d", p=P)
                        sp.dma_start(dst, xn[:]).then_inc(h_stored, 16)
                        sp.wait_ge(pt_copied, 2 * (b + 1))
                        sp.dma_start(p_dram[ds(b * E, E), :], pT[:]).then_inc(p_stored, 16)

                    wv_src = Wkv.rearrange("(c p) n -> p c n", p=P)
                    sp.dma_start(stage_v[:, :, 0:INNER], wv_src[:, :, INNER:2 * INNER]).then_inc(v_w_in, 16)
                    sp.dma_start(stage_v[:, :, INNER:VCOLS], Wg.rearrange("(c p) n -> p c n", p=P)).then_inc(v_w_in, 16)
                    with sp.Fori(0, B) as b:
                        load_batch(b)
                        spread(0, PAIRS * b, 0)
                        spread(1, PAIRS * b, 0)
                        max_row(PAIRS * b, 0, 0)
                        with sp.Fori(0, COUPLES - 1) as c:
                            pair_step(PAIRS * b + 2 * c, 0, False)
                            pair_step(PAIRS * b + 2 * c + 1, 1, False)
                        pair_step(PAIRS * b + PAIRS - 2, 0, False)
                        pair_step(PAIRS * b + PAIRS - 1, 1, True)
                        store_batch(b)

                @block.gpsimd
                def _(pool):
                    pool.dma_start(wq_raw[:], Wq.rearrange("(c p) n -> p c n", p=P)).then_inc(qk_w_in, 16)
                    pool.dma_start(wk_raw[:], Wkv.rearrange("(c p) n -> p c n", p=P)[:, :, 0:INNER]).then_inc(qk_w_in, 16)
                    pool.memset(ident[:], 0.0)
                    pool.memset(ident_b[:], 0.0)
                    pool.memset(mask_q[:], 0.0)
                    pool.memset(mask_k[:], 0.0)
                    pool.memset(v_hi[:, :, :, DH:DH + 1], 1.0).then_inc(consts, 1)
                    pool.wait_ge(consts, 2)
                    for m in (ident, ident_b):
                        pool.affine_select(out=m[:], in_=m[:], compare_op=ALU.not_equal, fill=1.0, base=0,
                                           pattern=[[-1, P]], channel_multiplier=1)
                    pool.affine_select(out=mask_q[:], in_=mask_q[:], compare_op=ALU.is_ge, fill=MASKED, base=0,
                                       pattern=[[-1, P]], channel_multiplier=1)
                    pool.affine_select(out=mask_k[:], in_=mask_k[:], compare_op=ALU.is_ge, fill=MASKED, base=0,
                                       pattern=[[1, P]], channel_multiplier=-1).then_inc(consts, 1)
                    pool.wait_ge(v_w_cut, 2)
                    pool.dma_start(stage[:, 0:PAIRS * D].rearrange("p (k n) -> p k n", k=PAIRS),
                                   Wout.rearrange("(k p) n -> p k n", p=P)).then_inc(o_w_in, 16)

                    def split_pair(n, p, u):
                        pool.wait_ge(pj_free, 4 * n + PJ_CREDIT - 4)
                        cols = ds(p * P, P)
                        for i, raw in enumerate((wq_raw, wk_raw)):
                            pool.tensor_copy(wp[u][0][:, i], raw[:, :, cols]).then_inc(pair_w, 1)
                        wait_apart(pool, pair_w, 4 * n + 2)
                        for i, raw in enumerate((wq_raw, wk_raw)):
                            pool.tensor_tensor(wp[u][1][:, i], raw[:, :, cols], wp[u][0][:, i],
                                               ALU.subtract).then_inc(pair_w, 1)

                    pool.wait_ge(qk_w_in, 32)
                    with pool.Fori(0, B) as b:
                        with pool.Fori(0, COUPLES) as c:
                            for u in range(2):
                                split_pair(PAIRS * b + 2 * c + u, 2 * c + u, u)

                @block.tensor
                def _(pe):
                    def three_terms(dst, lhs, rhs, first, last):
                        terms = [(0, 0), (1, 0), (0, 1)]
                        for i, (a, c) in enumerate(terms):
                            mm = pe.matmul(dst, lhs[a], rhs[c], start=first and i == 0, stop=last and i == 2)
                        return mm

                    def project(which, half, n, u):
                        pe.wait_ge(pj_free, 4 * n + 2 * which + half + 1 + PJ_CREDIT - 2)
                        for c in range(DC):
                            mm = three_terms(
                                pj_b[:, half, 0:HALF],
                                [w[:, which, c, :] for w in wp[u]],
                                [t[:, c, HALF * half:HALF * half + HALF] for t in xT],
                                c == 0, c == DC - 1)
                        mm.then_inc(pj_full, 1)

                    def max_piece(n, u, hd, i):
                        pe.wait_ge(mx_free, 12 * n + 6 * hd + i + 1)
                        at = 0
                        for q, k0, w, _ in MAX_PIECES[i]:
                            dst = mx_b[:, i % 2, at:at + w]
                            diag = k0 <= q * P < k0 + w
                            mm = pe.matmul(dst, query_both[:, u, hd, q * P:q * P + P],
                                           key_both[:, u, hd, k0:k0 + w], start=True, stop=not diag)
                            if diag:
                                d0 = at + q * P - k0
                                mm = pe.matmul(mx_b[:, i % 2, d0:d0 + P], ident_b[:], mask_q[:],
                                               start=False, stop=True)
                            at += w
                        mm.then_inc(mx_full, 1)

                    def turn_maxima(n, hd):
                        pe.wait_ge(max_ready, 2 * n + hd + 1)
                        pe.transpose(tr_b[0:NT, 0:P], mx[:, hd, 0:NT], ident[:]).then_inc(mt_full, 1)

                    def score_piece(n, u, hd, i):
                        pe.wait_ge(st_free, 12 * n + 6 * hd + i + 1)
                        at = 0
                        for j, q0, w in SCORE_PIECES[i]:
                            dst = st_b[:, i % 2, at:at + w]
                            ks = slice(j * P, j * P + P)
                            diag = q0 == j * P
                            pe.matmul(dst, key_both[:, u, hd, ks], query_both[:, u, hd, q0:q0 + w],
                                      start=True, stop=False)
                            mm = pe.matmul(dst, key_max[0:65, u, hd, ks], query_max[0:65, u, hd, q0:q0 + w],
                                           start=False, stop=not diag)
                            if diag:
                                mm = pe.matmul(st_b[:, i % 2, at:at + P], ident_b[:], mask_k[:],
                                               start=False, stop=True)
                            at += w
                        mm.then_inc(st_full, 1)

                    def weigh_values(n, hd, head, tiles):
                        if tiles[0] == 0:
                            pe.wait_ge(p_lo_done, RING32 + 12 * n + 6 * hd + 6)
                            pe.wait_ge(normed, 3 * (2 * n + hd))
                        for q in tiles:
                            for j in range(q + 1):
                                ps_ = slice(PROB_AT[j, q], PROB_AT[j, q] + P)
                                first, last = j == 0, j == q
                                pe.matmul(o_v[:, q, 0:DH + 1], p_hi[:, hd, ps_], v_hi[:, j, ds(head, 1), :],
                                          start=first, stop=False)
                                pe.matmul(o_v[:, q, 0:DH], p_hi[:, hd, ps_], v_lo[:, j, ds(head, 1), :],
                                          start=False, stop=False)
                                mm = pe.matmul(o_v[:, q, 0:DH + 1], p_lo[:, hd, ps_], v_hi[:, j, ds(head, 1), :],
                                               start=False, stop=last)
                        if tiles[-1] == NT - 1:
                            mm.then_inc(pv_done, 1)

                    def turn_outputs(n, half):
                        if half:
                            pe.wait_ge(at_lo, 2 * n + 1)
                        else:
                            pe.wait_ge(normed, 3 * (2 * n + 2))
                        for t in range(TH):
                            mm = pe.transpose(tr_b[:, t * P:t * P + P], heads_out[:, TH * half + t, :], ident[:])
                        mm.then_inc(at_full, 1)

                    def project_out(c, couple, k):
                        if k == 0:
                            pe.wait_ge(at_lo, 4 * (couple + 1))
                            pe.wait_ge(o_w_cut, 2)
                        if k == 2:
                            pe.wait_ge(op_added, 3 * couple + 1)
                        for t in range(2):
                            tok = slice((2 * k + t) * P, (2 * k + t) * P + P)
                            for u in range(2):
                                mm = three_terms(pj_b[:, k % 2, D * t:D * t + D],
                                                 [a[:, u, tok] for a in aT],
                                                 [w[:, ds(2 * c + u, 1), :] for w in wo],
                                                 u == 0, u == 1)
                        mm.then_inc(op_full, 1)

                    def first_head(b, c, u, first, last):
                        p = 2 * c + u
                        n = PAIRS * b + p
                        out_now = u == 1 and not is_first_couple(c)
                        couple = COUPLES * b + c - 1
                        pe.wait_ge(spread_m[0], 16 * (n + 1))
                        score_piece(n, u, 0, 0)
                        if first:
                            project_next(n + 1, 1 - u, 0, 3 * COUPLES * b)
                        max_piece(n, u, 1, 0)
                        max_piece(n, u, 1, 1)
                        if first:
                            project(0, 1, n + 1, 1 - u)
                        score_piece(n, u, 0, 1)
                        max_piece(n, u, 1, 2)
                        max_piece(n, u, 1, 3)
                        if first:
                            project(1, 0, n + 1, 1 - u)
                        else:
                            weigh_values(n - 1, 1, 2 * p - 1, (0, 1, 2))
                        score_piece(n, u, 0, 2)
                        if first:
                            project(1, 1, n + 1, 1 - u)
                        max_piece(n, u, 1, 4)
                        max_piece(n, u, 1, 5)
                        if not first:
                            weigh_values(n - 1, 1, 2 * p - 1, (3,))
                        score_piece(n, u, 0, 3)
                        if out_now:
                            pe.wait_ge(pj_free, PJ_CREDIT + (4 * (n + 1) if last else 4 * (n + 2)))
                            project_out(c - 1, couple, 0)
                        if not first:
                            weigh_values(n - 1, 1, 2 * p - 1, (4,))
                        pe.wait_ge(mt_copied, 2 * n + 1)
                        pe.wait_ge(at_lo, 2 * n if first else 2 * (n - 1))
                        turn_maxima(n, 1)
                        score_piece(n, u, 0, 4)
                        if not first:
                            weigh_values(n - 1, 1, 2 * p - 1, (5,))
                        if out_now:
                            project_out(c - 1, couple, 1)
                        score_piece(n, u, 0, 5)
                        if out_now:
                            project_out(c - 1, couple, 2)

                    def second_head(b, c, u, first, last):
                        p = 2 * c + u
                        n = PAIRS * b + p
                        ahead = not is_last_couple(c)
                        pe.wait_ge(spread_m[1], 16 * (n + 1))
                        score_piece(n, u, 1, 0)
                        if not last:
                            pe.wait_ge(spread_q, SPREAD * (n + 2))
                            pe.wait_ge(spread_k, SPREAD * (n + 2))
                            max_piece(n + 1, 1 - u, 0, 0)
                            max_piece(n + 1, 1 - u, 0, 1)
                        score_piece(n, u, 1, 1)
                        if not last:
                            max_piece(n + 1, 1 - u, 0, 2)
                            max_piece(n + 1, 1 - u, 0, 3)
                        if not first:
                            pe.wait_ge(mt_copied, 2 * n + 2)
                            turn_outputs(n - 1, 0)
                        weigh_values(n, 0, 2 * p, (0, 1, 2))
                        score_piece(n, u, 1, 2)
                        if not last:
                            max_piece(n + 1, 1 - u, 0, 4)
                            max_piece(n + 1, 1 - u, 0, 5)
                        if not first:
                            turn_outputs(n - 1, 1)
                        if ahead:
                            done = 3 * (COUPLES * b + c)
                            project_next(n + 2, u, 0, done if u == 1 or is_first_couple(c) else done - 3)
                        score_piece(n, u, 1, 3)
                        weigh_values(n, 0, 2 * p, (3,))
                        if not last:
                            pe.wait_ge(mt_copied, 2 * n + 2)
                            if not first:
                                pe.wait_ge(at_lo, 2 * n)
                            turn_maxima(n + 1, 0)
                        if ahead:
                            project(0, 1, n + 2, u)
                        score_piece(n, u, 1, 4)
                        weigh_values(n, 0, 2 * p, (4,))
                        if ahead:
                            project(1, 0, n + 2, u)
                        score_piece(n, u, 1, 5)
                        weigh_values(n, 0, 2 * p, (5,))
                        if ahead:
                            project(1, 1, n + 2, u)

                    def project_next(n, u, half, added):
                        pe.wait_ge(pair_w, 4 * n + 4)
                        pe.wait_ge(op_added, added)
                        project(0, half, n, u)

                    def couple_step(b, c, first, last):
                        for u in range(2):
                            first_head(b, c, u, first and u == 0, last and u == 1)
                            second_head(b, c, u, first and u == 0, last and u == 1)

                    def finish(b):
                        n = PAIRS * b + PAIRS - 1
                        weigh_values(n, 1, HEADS - 1, tuple(range(NT)))
                        pe.wait_ge(mt_copied, 2 * n + 2)
                        pe.wait_ge(at_lo, 2 * n)
                        turn_outputs(n, 0)
                        turn_outputs(n, 1)
                        pe.wait_ge(pj_free, PJ_CREDIT + 4 * (n + 1))
                        for k in range(NT // 2):
                            project_out(COUPLES - 1, COUPLES * b + COUPLES - 1, k)

                    pe.sem_inc(pv_done, PV_CREDIT)
                    pe.wait_ge(consts, 3)
                    pe.wait_ge(const_in, 16 * (1 + PATCH + DC + 1))
                    with pe.Fori(0, B) as b:
                        pe.wait_ge(img_in, 16 * IMG_DMAS * (b + 1))
                        pe.wait_ge(st_free, 2 + 12 * PAIRS * b)
                        for t in range(NTI):
                            for k in range(TAPS):
                                rows = ROWS * min(SHIFTS, PATCH - SHIFTS * k)
                                gr = GRID // NTI
                                lhs = img[0:rows, gr * t:gr * t + gr, SHIFTS * k:IMG:PATCH]
                                mm = pe.matmul(st_b[:, t, 0:D], lhs, tok_w[0:rows, k, :],
                                               start=k == 0, stop=k == TAPS - 1)
                            mm.then_inc(tok_full, 1)
                        pe.wait_ge(x_ready, b + 1)
                        for i in range(4):
                            c, half = i // 2, i % 2
                            for t in range(TH):
                                mm = pe.transpose(turn[i][:, t * P:t * P + P],
                                                  xn[:, TH * half + t, c * P:c * P + P], ident[:])
                            mm.then_inc(xt_full, 1)
                        pe.wait_ge(xt_lo, 4 * (b + 1))
                        pe.wait_ge(v_w_cut, 2)
                        i = 0
                        for t in range(NT):
                            for h0, nh, ng in V_PIECES:
                                w = nh * DH + ng
                                if i >= 4:
                                    pe.wait_ge(v_lo_done, NT * 3 * b + i - 3)
                                for c in range(DC):
                                    mm = three_terms(four[i % 4][:, 0:w],
                                                     [a[:, c, t * P:t * P + P] for a in xT],
                                                     [a[:, c, h0 * DH:h0 * DH + w] for a in wv],
                                                     c == 0, c == DC - 1)
                                mm.then_inc(v_full, 1)
                                i += 1
                        pe.wait_ge(op_added, 3 * COUPLES * b)
                        pe.wait_ge(pair_w, 4 * PAIRS * b + 4)
                        for which in range(2):
                            for half in range(2):
                                project(which, half, PAIRS * b, 0)
                        pe.wait_ge(v_lo_done, NT * 3 * (b + 1))
                        pe.wait_ge(spread_q, SPREAD * (PAIRS * b + 1))
                        pe.wait_ge(spread_k, SPREAD * (PAIRS * b + 1))
                        for i in range(NPIECE):
                            max_piece(PAIRS * b, 0, 0, i)
                        pe.wait_ge(at_lo, 2 * PAIRS * b)
                        turn_maxima(PAIRS * b, 0)
                        couple_step(b, 0, True, False)
                        with pe.Fori(1, COUPLES - 1) as c:
                            couple_step(b, c, False, False)
                        couple_step(b, COUPLES - 1, False, True)
                        finish(b)
                        pe.wait_ge(x2_ready, b + 1)
                        for i in range(4):
                            c, half = i // 2, i % 2
                            for t in range(TH):
                                mm = pe.transpose(turn[i][:, t * P:t * P + P],
                                                  xn[:, TH * half + t, c * P:c * P + P], ident[:])
                            mm.then_inc(x2t_full, 1)
                        pe.wait_ge(x2t_copied, 4 * (b + 1))
                        for t in range(NT):
                            for c in range(DC):
                                mm = pe.matmul(tr_b[:, t * E:t * E + E], x2T[:, c, t * P:t * P + P], gw[:, c, :],
                                               start=c == 0, stop=c == DC - 1)
                        mm.then_inc(logits_full, 1)
                        pe.wait_ge(probs_ready, b + 1)
                        for half in range(2):
                            for t in range(TH):
                                mm = pe.transpose(pj_b[0:E, half, t * P:t * P + P], probs[:, TH * half + t, :], ident[:])
                            mm.then_inc(pt_full, 1)

                @block.scalar
                def _(act):
                    def split_projection(which, half, n):
                        if half == 0:
                            act.wait_ge(spread_q if which == 0 else spread_k, SPREAD * n)
                        act.wait_ge(pj_full, 4 * n + 2 * which + half + 1)
                        act.activation(cut[which][0][:, HALF * half:HALF * half + HALF],
                                       pj_b[:, half, 0:HALF], ACT.Copy).then_inc(pj_hi, 1)

                    def exponentials(n, hd, i):
                        if i == 0:
                            act.wait_ge(pv_done, 2 * n + hd + 1)
                        w = sum(q[2] for q in SCORE_PIECES[i])
                        act.wait_ge(st_full, 12 * n + 6 * hd + i + 1)
                        act.wait_ge(p_lo_done, 12 * n + 6 * hd + i + 1)
                        at = PIECE_START[i]
                        act.activation(p32[:, i % RING32, 0:w], st_b[:, i % 2, 0:w], ACT.Exp, scale=SCALE)
                        act.activation(p_hi[:, hd, at:at + w], st_b[:, i % 2, 0:w], ACT.Exp,
                                       scale=SCALE).then_inc(st_free, 1)

                    def max_row(n, hd):
                        act.wait_ge(mt_full, 2 * n + hd + 1)
                        act.wait_ge(spread_m[hd], 16 * n)
                        act.activation(m_row[:, hd, :], tr_b[0:NT, 0:P], ACT.Copy,
                                       scale=-1.0 / MAX_UNIT).then_inc(mt_copied, 1)

                    def turned_outputs(n, u, couple, half):
                        if half == 0:
                            act.wait_ge(op_full, 3 * couple)
                        act.wait_ge(at_full, 2 * n + half + 1)
                        act.activation(aT[0][:, u, HALF * half:HALF * half + HALF], tr_b[:, 0:HALF],
                                       ACT.Copy).then_inc(at_hi, 1)

                    def first_head(b, c, u, first, last):
                        n = PAIRS * b + 2 * c + u
                        exponentials(n, 0, 0)
                        if first:
                            split_projection(0, 0, n + 1)
                            split_projection(0, 1, n + 1)
                        exponentials(n, 0, 1)
                        if first:
                            split_projection(1, 0, n + 1)
                        exponentials(n, 0, 2)
                        if first:
                            split_projection(1, 1, n + 1)
                        exponentials(n, 0, 3)
                        max_row(n, 1)
                        exponentials(n, 0, 4)
                        exponentials(n, 0, 5)

                    def second_head(b, c, u, first, last):
                        n = PAIRS * b + 2 * c + u
                        before = COUPLES * b + c - (1 if u == 0 else 0)
                        ahead = not is_last_couple(c)
                        exponentials(n, 1, 0)
                        exponentials(n, 1, 1)
                        if not first:
                            turned_outputs(n - 1, 1 - u, before, 0)
                        exponentials(n, 1, 2)
                        if not first:
                            turned_outputs(n - 1, 1 - u, before, 1)
                        if ahead:
                            split_projection(0, 0, n + 2)
                        exponentials(n, 1, 3)
                        if not last:
                            max_row(n + 1, 0)
                        if ahead:
                            split_projection(0, 1, n + 2)
                        exponentials(n, 1, 4)
                        if ahead:
                            split_projection(1, 0, n + 2)
                        exponentials(n, 1, 5)
                        if ahead:
                            split_projection(1, 1, n + 2)

                    def couple_step(b, c, first, last):
                        for u in range(2):
                            first_head(b, c, u, first and u == 0, last and u == 1)
                            second_head(b, c, u, first and u == 0, last and u == 1)

                    def root(k, b, src, dst):
                        act.wait_ge(root_in, 4 * b + k + 1)
                        act.activation(dst, src, ACT.Sqrt).then_inc(root_out, 1)

                    act.sem_inc(st_free, 2)
                    with act.Fori(0, B) as b:
                        root(0, b, rt[:, 0, 0:NTI], rt[:, 1, 0:NTI])
                        root(1, b, rt[:, 0, :], rt[:, 1, :])
                        root(2, b, rt[:, 0, :], rt[:, 1, :])
                        for i in range(4):
                            c, half = i // 2, i % 2
                            act.wait_ge(xt_full, 4 * b + i + 1)
                            act.activation(xT[0][:, c, HALF * half:HALF * half + HALF], turn[i][:, 0:HALF], ACT.Copy,
                                           scale=nw[:, c:c + 1]).then_inc(xt_hi, 1)
                        i = 0
                        for t in range(NT):
                            for h0, nh, ng in V_PIECES:
                                act.wait_ge(v_full, NT * 3 * b + i + 1)
                                if ng:
                                    act.activation(gate[:, t, :], four[i % 4][:, nh * DH:nh * DH + ng], ACT.Exp,
                                                   scale=-1.0)
                                act.activation(v_hi[:, t, h0:h0 + nh, 0:DH],
                                               four[i % 4][:, 0:nh * DH].rearrange("p (h d) -> p h d", d=DH),
                                               ACT.Copy).then_inc(v_hi_done, 1)
                                i += 1
                        for which in range(2):
                            for half in range(2):
                                split_projection(which, half, PAIRS * b)
                        max_row(PAIRS * b, 0)
                        couple_step(b, 0, True, False)
                        with act.Fori(1, COUPLES - 1) as c:
                            couple_step(b, c, False, False)
                        couple_step(b, COUPLES - 1, False, True)
                        for half in range(2):
                            turned_outputs(PAIRS * b + PAIRS - 1, 1, COUPLES * b + COUPLES - 1, half)
                        root(3, b, rt[:, 0, :], rt[:, 1, :])
                        for i in range(4):
                            c, half = i // 2, i % 2
                            act.wait_ge(x2t_full, 4 * b + i + 1)
                            act.activation(x2T[:, c, HALF * half:HALF * half + HALF], turn[i][:, 0:HALF],
                                           ACT.Copy).then_inc(x2t_copied, 1)
                        act.wait_ge(soft, SOFT_STEPS * b + 2)
                        act.activation(probs[:], probs[:], ACT.Exp).then_inc(logit_exp, 1)

                @block.vector
                def _(dve):
                    def split_projection(which, half, n):
                        dve.wait_ge(pj_hi, 4 * n + 2 * which + half + 1)
                        cols = slice(HALF * half, HALF * half + HALF)
                        dve.tensor_tensor(cut[which][1][:, cols], pj_b[:, half, 0:HALF], cut[which][0][:, cols],
                                          ALU.subtract).then_inc(pj_free, 1)

                    def low_part(n, hd, i):
                        w = sum(q[2] for q in SCORE_PIECES[i])
                        at = PIECE_START[i]
                        dve.wait_ge(st_free, 2 + 12 * n + 6 * hd + i + 1)
                        dve.tensor_tensor(p_lo[:, hd, at:at + w], p32[:, i % RING32, 0:w],
                                          p_hi[:, hd, at:at + w], ALU.subtract).then_inc(p_lo_done, 1)

                    def max_piece(n, hd, i):
                        if i == 0:
                            dve.wait_ge(mt_full, 2 * n)
                        dve.wait_ge(mx_full, 12 * n + 6 * hd + i + 1)
                        at = 0
                        for _, _, w, col in MAX_PIECES[i]:
                            r = dve.tensor_reduce(mx[:, hd, col:col + 1], mx_b[:, i % 2, at:at + w], AX.X, ALU.max)
                            at += w
                        r.then_inc(mx_free, 1)

                    def join_maxima(n, hd):
                        dve.wait_ge(mx_free, 2 + 12 * n + 6 * hd + 6)
                        dve.tensor_tensor(mx[:, hd, 4:6], mx[:, hd, 4:6], mx[:, hd, 6:8], ALU.max).then_inc(max_ready, 1)

                    def normalise(n, hd, head):
                        k = 2 * n + hd
                        dve.wait_ge(pv_done, PV_CREDIT + k + 1)
                        dve.tensor_tensor(den[:, 0, :], o_v[:, :, DH], gate[:, :, ds(head, 1)].rearrange("p t a -> p (t a)"),
                                          ALU.mult).then_inc(normed, 1)
                        dve.wait_ge(normed, 3 * k + 1)
                        dve.reciprocal(den[:, 1, :], den[:, 0, :]).then_inc(normed, 1)
                        dve.wait_ge(normed, 3 * k + 2)
                        if hd == 0:
                            dve.wait_ge(at_full, 2 * n)
                        scale = den[:, 1, :].rearrange("p (t a) -> p t a", a=1).broadcast_to([P, NT, DH])
                        dve.tensor_tensor(heads_out[:, :, DH * hd:DH * hd + DH], o_v[:, :, 0:DH], scale,
                                          ALU.mult).then_inc(normed, 1)

                    def turned_outputs(n, u, half):
                        dve.wait_ge(at_hi, 2 * n + half + 1)
                        cols = slice(HALF * half, HALF * half + HALF)
                        dve.tensor_tensor(aT[1][:, u, cols], tr_b[:, 0:HALF], aT[0][:, u, cols],
                                          ALU.subtract).then_inc(at_lo, 1)

                    def add_out(couple, k):
                        if k == 0:
                            dve.wait_ge(op_added, 3 * couple)
                        dve.wait_ge(op_full, 3 * couple + k + 1)
                        rows = h[:, 2 * k:2 * k + 2, :].rearrange("p t d -> p (t d)")
                        dve.tensor_tensor(rows, rows, pj_b[:, k % 2, :], ALU.add).then_inc(op_added, 1)

                    def first_head(b, c, u, first, last):
                        p = 2 * c + u
                        n = PAIRS * b + p
                        out_now = u == 1 and not is_first_couple(c)
                        couple = COUPLES * b + c - 1
                        max_piece(n, 1, 0)
                        if not first:
                            normalise(n - 1, 0, 2 * p - 2)
                        max_piece(n, 1, 1)
                        if first:
                            split_projection(0, 0, n + 1)
                        low_part(n, 0, 0)
                        if first:
                            split_projection(0, 1, n + 1)
                        max_piece(n, 1, 2)
                        max_piece(n, 1, 3)
                        low_part(n, 0, 1)
                        if first:
                            split_projection(1, 0, n + 1)
                        max_piece(n, 1, 4)
                        if first:
                            split_projection(1, 1, n + 1)
                        max_piece(n, 1, 5)
                        join_maxima(n, 1)
                        low_part(n, 0, 2)
                        low_part(n, 0, 3)
                        if out_now:
                            add_out(couple, 0)
                        low_part(n, 0, 4)
                        if out_now:
                            add_out(couple, 1)
                        low_part(n, 0, 5)
                        if out_now:
                            add_out(couple, 2)

                    def second_head(b, c, u, first, last):
                        p = 2 * c + u
                        n = PAIRS * b + p
                        ahead = not is_last_couple(c)
                        if not last:
                            max_piece(n + 1, 0, 0)
                        if not first:
                            normalise(n - 1, 1, 2 * p - 1)
                        if not last:
                            max_piece(n + 1, 0, 1)
                        low_part(n, 1, 0)
                        if not last:
                            max_piece(n + 1, 0, 2)
                            max_piece(n + 1, 0, 3)
                        low_part(n, 1, 1)
                        if not first:
                            turned_outputs(n - 1, 1 - u, 0)
                        if not last:
                            max_piece(n + 1, 0, 4)
                            max_piece(n + 1, 0, 5)
                            join_maxima(n + 1, 0)
                        low_part(n, 1, 2)
                        if not first:
                            turned_outputs(n - 1, 1 - u, 1)
                        if ahead:
                            split_projection(0, 0, n + 2)
                        low_part(n, 1, 3)
                        if ahead:
                            split_projection(0, 1, n + 2)
                        low_part(n, 1, 4)
                        if ahead:
                            split_projection(1, 0, n + 2)
                        low_part(n, 1, 5)
                        if ahead:
                            split_projection(1, 1, n + 2)

                    def couple_step(b, c, first, last):
                        for u in range(2):
                            first_head(b, c, u, first and u == 0, last and u == 1)
                            second_head(b, c, u, first and u == 0, last and u == 1)

                    def finish(b):
                        n = PAIRS * b + PAIRS - 1
                        normalise(n, 0, HEADS - 2)
                        normalise(n, 1, HEADS - 1)
                        for half in range(2):
                            turned_outputs(n, 1, half)
                        for k in range(NT // 2):
                            add_out(COUPLES * b + COUPLES - 1, k)

                    steps = [0]

                    def chain(b, ins, per=LN_STEPS, sem_=ln):
                        steps[0] += 1
                        ins.then_inc(sem_, 1)
                        dve.wait_ge(sem_, per * b + steps[0])

                    dve.memset(key_max[64:65], MAX_UNIT).then_inc(consts, 1)
                    dve.sem_inc(pj_free, PJ_CREDIT)
                    dve.sem_inc(mx_free, 2)
                    dve.sem_inc(p_lo_done, RING32)
                    stage_v = stage[:].rearrange("p (c n) -> p c n", c=DC)
                    stage_o = stage[:, 0:PAIRS * D].rearrange("p (k n) -> p k n", k=PAIRS)
                    for w, src, arrived, bytes_, done in ((wv, stage_v, v_w_in, 32, v_w_cut), (wo, stage_o, o_w_in, 16, o_w_cut)):
                        dve.wait_ge(arrived, bytes_)
                        dve.tensor_copy(w[0][:], src).then_inc(done, 1)
                        dve.wait_ge(done, 1)
                        dve.tensor_tensor(w[1][:], src, w[0][:], ALU.subtract).then_inc(done, 1)
                    dve.wait_ge(const_in, 16 * (1 + PATCH + DC + 1))
                    with dve.Fori(0, B) as b:
                        steps[0] = 0
                        for t in range(NTI):
                            dve.wait_ge(tok_full, NTI * b + t + 1)
                            s = dve.bn_stats(stats[:, t, :], st_b[:, t, 0:D])
                        chain(b, s)
                        dve.sem_inc(fence, 1)
                        for t in range(NTI):
                            s = dve.bn_aggr(mv[:, t, :], stats[:, t, :])
                        chain(b, s)
                        dve.tensor_scalar(rt[:, 0, 0:NTI], mv[:, 0:NTI, 1], LN_EPS, None, ALU.add).then_inc(root_in, 1)
                        dve.wait_ge(root_out, 4 * b + 1)
                        chain(b, dve.reciprocal(rt[:, 2, 0:NTI], rt[:, 1, 0:NTI]))
                        dve.wait_ge(h_stored, 32 * b)
                        for t in range(NTI):
                            s = dve.tensor_scalar(xn[:, t, :], st_b[:, t, 0:D], mv[:, t, 0:1], rt[:, 2, t:t + 1],
                                                  ALU.subtract, ALU.mult)
                        chain(b, s)
                        for t in range(NTI):
                            s = dve.tensor_tensor(h[:, t, :], xn[:, t, :], gamma[:], ALU.mult)
                        chain(b, s)
                        dve.wait_ge(txt_in, 16 * (b + 1))
                        for t in range(NT):
                            s = dve.bn_stats(stats[:, t, :], h[:, t, :])
                        chain(b, s)
                        dve.sem_inc(fence, 1)
                        for t in range(NT):
                            s = dve.bn_aggr(mv[:, t, :], stats[:, t, :])
                        chain(b, s)
                        dve.tensor_scalar(rt[:, 0, :], mv[:, :, 1], LN_EPS, None, ALU.add).then_inc(root_in, 1)
                        dve.wait_ge(root_out, 4 * b + 2)
                        chain(b, dve.reciprocal(rt[:, 2, :], rt[:, 1, :]))
                        chain(b, dve.tensor_tensor(rt[:, 3, :], rt[:, 2, :], rt[:, 2, :], ALU.mult))
                        chain(b, dve.tensor_tensor(rt[:, 4, :], rt[:, 3, :], mv[:, :, 1], ALU.mult))
                        dve.tensor_scalar(rt[:, 0, :], rt[:, 4, :], RMS_EPS, None, ALU.add).then_inc(root_in, 1)
                        dve.wait_ge(root_out, 4 * b + 3)
                        chain(b, dve.reciprocal(rt[:, 3, :], rt[:, 1, :]))
                        chain(b, dve.tensor_tensor(rt[:, 5, :], rt[:, 3, :], rt[:, 2, :], ALU.mult))
                        for t in range(NT):
                            s = dve.tensor_scalar(xn[:, t, :], h[:, t, :], mv[:, t, 0:1], rt[:, 5, t:t + 1],
                                                  ALU.subtract, ALU.mult)
                        s.then_inc(x_ready, 1)
                        for i in range(4):
                            c, half = i // 2, i % 2
                            dve.wait_ge(xt_hi, 4 * b + i + 1)
                            cols = slice(HALF * half, HALF * half + HALF)
                            dve.scalar_tensor_tensor(out=xT[1][:, c, cols], in0=turn[i][:, 0:HALF], scalar=nw[:, c:c + 1],
                                                     in1=xT[0][:, c, cols], op0=ALU.mult,
                                                     op1=ALU.subtract).then_inc(xt_lo, 1)
                        i = 0
                        for t in range(NT):
                            for h0, nh, ng in V_PIECES:
                                dve.wait_ge(v_hi_done, NT * 3 * b + i + 1)
                                dve.tensor_tensor(v_lo[:, t, h0:h0 + nh, :],
                                                  four[i % 4][:, 0:nh * DH].rearrange("p (h d) -> p h d", d=DH),
                                                  v_hi[:, t, h0:h0 + nh, 0:DH], ALU.subtract).then_inc(v_lo_done, 1)
                                i += 1
                        chain(b, dve.tensor_scalar(gate[:], gate[:], 1.0, None, ALU.add))
                        for which in range(2):
                            for half in range(2):
                                split_projection(which, half, PAIRS * b)
                        for i in range(NPIECE):
                            max_piece(PAIRS * b, 0, i)
                        join_maxima(PAIRS * b, 0)
                        couple_step(b, 0, True, False)
                        with dve.Fori(1, COUPLES - 1) as c:
                            couple_step(b, c, False, False)
                        couple_step(b, COUPLES - 1, False, True)
                        finish(b)
                        dve.wait_ge(op_added, 3 * COUPLES * (b + 1))
                        for t in range(NT):
                            s = dve.bn_stats(stats[:, t, :], h[:, t, :])
                        chain(b, s)
                        dve.sem_inc(fence, 1)
                        for t in range(NT):
                            s = dve.bn_aggr(mv[:, t, :], stats[:, t, :])
                        chain(b, s)
                        dve.tensor_scalar(rt[:, 0, :], mv[:, :, 1], LN_EPS, None, ALU.add).then_inc(root_in, 1)
                        dve.wait_ge(root_out, 4 * b + 4)
                        chain(b, dve.reciprocal(rt[:, 2, :], rt[:, 1, :]))
                        for t in range(NT):
                            s = dve.tensor_scalar(xn[:, t, :], h[:, t, :], mv[:, t, 0:1], rt[:, 2, t:t + 1],
                                                  ALU.subtract, ALU.mult)
                        s.then_inc(x2_ready, 1)
                        total = steps[0]
                        steps[0] = 0
                        logits = tr_b[:, 0:NT * E].rearrange("p (t e) -> p t e", e=E)

                        def wide(v):
                            return v.rearrange("p (t a) -> p t a", a=1).broadcast_to([P, NT, E])

                        dve.wait_ge(logits_full, b + 1)
                        chain(b, dve.tensor_reduce(rsm[:, 0, :], logits, AX.X, ALU.max), SOFT_STEPS, soft)
                        chain(b, dve.tensor_tensor(probs[:], logits, wide(rsm[:, 0, :]), ALU.subtract), SOFT_STEPS, soft)
                        dve.wait_ge(logit_exp, b + 1)
                        chain(b, dve.tensor_reduce(rsm[:, 1, :], probs[:], AX.X, ALU.add), SOFT_STEPS, soft)
                        chain(b, dve.reciprocal(rsm[:, 2, :], rsm[:, 1, :]), SOFT_STEPS, soft)
                        assert steps[0] == SOFT_STEPS
                        dve.tensor_tensor(probs[:], probs[:], wide(rsm[:, 2, :]), ALU.mult).then_inc(probs_ready, 1)
                        dve.wait_ge(p_stored, 16 * b)
                        for half in range(2):
                            dve.wait_ge(pt_full, 2 * b + half + 1)
                            dve.tensor_copy(pT[:, HALF * half:HALF * half + HALF],
                                            pj_b[0:E, half, 0:HALF]).then_inc(pt_copied, 1)
                    assert total == LN_STEPS, total

            psum.close()
            attn.close()

            exp = ExitStack()
            with exp:
                def sbe(name, shape, dt):
                    return exp.enter_context(nc.sbuf_tensor(name, shape, dt))

                def pse(name, shape):
                    return exp.enter_context(nc.psum_tensor(name, shape, F32))

                R = B * E
                TOP = 8
                ROUNDS = CAP // TOP
                W_CUTS = 16
                W1C = DC * HID * 2 // W_CUTS
                router = [sbe(f"router_{i}", [R, N], F32) for i in range(2)]
                top_p = sbe("top_p", [R, CAP], F32)
                top_i = sbe("top_i", [R, CAP], U32)
                top_f = sbe("top_f", [R, CAP], F32)
                row_base = sbe("row_base", [R, 3], F32)
                row_u = sbe("row_u", [R, 2], U32)
                ids = sbe("ids", [P, E, ST], U32)
                pvs = sbe("pvs", [P, E, ST], F32)
                ids_now = [sbe(f"ids_now_{u}", [P, ST], U32) for u in range(2)]
                w1_raw = sbe("w1_raw", [P, DC * HID], F32)
                w2_raw = sbe("w2_raw", [P, HC * D], F32)
                w1s = [[sbe(f"w1_{u}_{s}", [P, DC * HID], F32R) for s in ("hi", "lo")] for u in range(2)]
                w2s = [[sbe(f"w2_{u}_{s}", [P, HC * D], F32R) for s in ("hi", "lo")] for u in range(2)]
                rows = [sbe(f"rows_{u}", [P, ST, D], F32) for u in range(2)]
                gT = [sbe(f"gT_{s}", [P, DC, SLOTS], F32R) for s in ("hi", "lo")]
                h32 = sbe("h32", [P, H_CREDIT, HALF], F32)
                hT = [[sbe(f"hT_{g}_{s}", [P, HC, HALF], F32R) for s in ("hi", "lo")] for g in range(2)]
                ys = sbe("ys", [P, ST, D], F32)
                gt_b = pse("gt_b", [P, 2, 512])
                h_b = pse("h_b", [P, H_CREDIT, 512])
                y_b = pse("y_b", [P, 2, 512])

                with nc.Block() as block:
                    @block.sync
                    def _(sp):
                        def load_weights(e):
                            sp.wait_ge(w_cut_lo, W_CUTS * e)
                            sp.dma_start(w1_raw[:].rearrange("p (c n) -> p c n", c=DC),
                                         w1[ds(e, 1)].rearrange("a (c p) n -> (a p) c n", p=P)).then_inc(w_raw_in, 16)
                            sp.dma_start(w2_raw[:].rearrange("p (k n) -> p k n", k=HC),
                                         w2[ds(e, 1)].rearrange("a (k p) n -> (a p) k n", p=P)).then_inc(w_raw_in, 16)

                        sp.wait_ge(p_stored, 16 * B)
                        sp.wait_ge(h_stored, 32 * B)
                        sp.dma_start(router[0][:], p_dram[:]).then_inc(rows_in, 16)
                        load_weights(0)
                        sp.wait_ge(pick, 3 * ROUNDS + 3)
                        for b in range(B):
                            r = slice(E * b, E * b + E)
                            sp.dma_start(idx_dram[:, b, :], top_i[r, :]).then_inc(picks_stored, 16)
                            sp.dma_start(pv_dram[:, b, :], top_p[r, :]).then_inc(picks_stored, 16)
                        sp.wait_ge(picks_stored, 32 * B)
                        sp.dma_start(ids[:], idx_dram.rearrange("e b s -> e (b s)").rearrange(
                            "e (p t) -> p e t", t=ST)).then_inc(picks_in, 16)
                        sp.dma_start(pvs[:], pv_dram.rearrange("e b s -> e (b s)").rearrange(
                            "e (p t) -> p e t", t=ST)).then_inc(picks_in, 16)
                        with sp.Fori(1, E) as e:
                            load_weights(e)

                    @block.gpsimd
                    def _(pool):
                        def fetch_rows(e, u):
                            if not isinstance(e, int) or e > 1:
                                pool.wait_ge(scattered, 16 * ST * (e - 1))
                            pool.tensor_copy(ids_now[u][:], ids[:, ds(e, 1), :].rearrange("p a t -> p (a t)")).then_inc(ids_copied, 1)
                            wait_apart(pool, ids_copied, e + 1)
                            for t in range(ST):
                                pool.indirect_dma_start(
                                    out=rows[u][:, t, :], out_offset=None, in_=x2_dram,
                                    in_offset=bass.IndirectOffsetOnAxis(ap=ids_now[u][:, t:t + 1], axis=0)).then_inc(gathered[u], 16)

                        def scatter_rows(e, u):
                            pool.wait_ge(scattered, 16 * ST * e)
                            for t in range(ST):
                                pool.wait_ge(scattered, 16 * (ST * e + t))
                                wait_apart(pool, y_ready, ST * e + t + 1)
                                pool.indirect_dma_start(
                                    out=out_rows, out_offset=bass.IndirectOffsetOnAxis(ap=ids_now[u][:, t:t + 1], axis=0),
                                    in_=ys[:, t, :], in_offset=None, compute_op=ALU.add).then_inc(scattered, 16)

                        pool.iota(row_u[:, 0:1], pattern=[[0, 1]], base=0, channel_multiplier=1).then_inc(row_id, 1)
                        pool.wait_ge(picks_in, 32)
                        fetch_rows(0, 0)
                        with pool.Fori(0, E // 2 - 1) as i:
                            fetch_rows(2 * i + 1, 1)
                            scatter_rows(2 * i, 0)
                            fetch_rows(2 * i + 2, 0)
                            scatter_rows(2 * i + 1, 1)
                        fetch_rows(E - 1, 1)
                        scatter_rows(E - 2, 0)
                        scatter_rows(E - 1, 1)
                        pool.wait_ge(scattered, 16 * ST * E)

                    @block.tensor
                    def _(pe):
                        def three_terms(dst, lhs, rhs, first, last):
                            terms = [(0, 0), (1, 0), (0, 1)]
                            for i, (a, c) in enumerate(terms):
                                mm = pe.matmul(dst, lhs[a], rhs[c], start=first and i == 0, stop=last and i == 2)
                            return mm

                        def turn_rows(e, u, i):
                            pe.wait_ge(gathered[u], 16 * ST * i)
                            for k in range(4):
                                c, half = k // 2, k % 2
                                pe.wait_ge(gt_lo, 4 * e + max(k - 1, 0))
                                for t in range(TH):
                                    mm = pe.transpose(gt_b[:, k % 2, t * P:t * P + P],
                                                      rows[u][:, TH * half + t, c * P:c * P + P], ident[:])
                                mm.then_inc(gt_full, 1)

                        def first_layer(e, u, g):
                            if g == 0:
                                pe.wait_ge(w_cut_lo, W_CUTS * (e + 1))
                                pe.wait_ge(gt_lo, 4 * (e + 1))
                            for k in range(HC):
                                i = HC * g + k
                                pe.wait_ge(h_lo_done, 2 * HC * e + i + 1)
                                for c in range(DC):
                                    mm = three_terms(h_b[:, i % H_CREDIT, 0:HALF],
                                                     [w[:, c * HID + k * P:c * HID + k * P + P] for w in w1s[u]],
                                                     [a[:, c, HALF * g:HALF * g + HALF] for a in gT],
                                                     c == 0, c == DC - 1)
                                mm.then_inc(h_full, 1)

                        def second_layer(e, u, g):
                            pe.wait_ge(h_lo_done, H_CREDIT + 2 * HC * e + HC * (g + 1))
                            for t in range(TH):
                                i = TH * g + t
                                pe.wait_ge(y_ready, ST * e + max(i - 1, 0))
                                for k in range(HC):
                                    mm = three_terms(y_b[:, i % 2, 0:D],
                                                     [a[:, k, t * P:t * P + P] for a in hT[g]],
                                                     [w[:, k * D:k * D + D] for w in w2s[u]],
                                                     k == 0, k == HC - 1)
                                mm.then_inc(y_full, 1)

                        def expert(i, u, last):
                            e = 2 * i + u
                            first_layer(e, u, 0)
                            first_layer(e, u, 1)
                            second_layer(e, u, 0)
                            if not last:
                                turn_rows(e + 1, 1 - u, i + 1 + u)
                            second_layer(e, u, 1)

                        pe.sem_inc(y_full, ST)
                        turn_rows(0, 0, 1)
                        with pe.Fori(0, E // 2 - 1) as i:
                            expert(i, 0, False)
                            expert(i, 1, False)
                        expert(E // 2 - 1, 0, False)
                        expert(E // 2 - 1, 1, True)

                    @block.scalar
                    def _(act):
                        def split_weights(e, u, i):
                            if i == 0:
                                act.wait_ge(w_raw_in, 32 * (e + 1))
                                act.wait_ge(y_full, ST * e)
                            raw, to = (w1_raw, w1s[u][0]) if i < W_CUTS // 2 else (w2_raw, w2s[u][0])
                            c = slice(W1C * (i % (W_CUTS // 2)), W1C * (i % (W_CUTS // 2)) + W1C)
                            act.activation(to[:, c], raw[:, c], ACT.Copy).then_inc(w_cut_hi, 1)

                        def turned_rows(e):
                            for i in range(4):
                                c, half = i // 2, i % 2
                                act.wait_ge(gt_full, 4 * e + i + 1)
                                if i == 0:
                                    act.wait_ge(h_full, 2 * HC * e)
                                act.activation(gT[0][:, c, HALF * half:HALF * half + HALF], gt_b[:, i % 2, 0:HALF],
                                               ACT.Copy).then_inc(gt_hi, 1)

                        def expert(e, u, last):
                            for i in range(2 * HC):
                                g, k = i // HC, i % HC
                                act.wait_ge(h_full, 2 * HC * e + i + 1)
                                act.wait_ge(h_lo_done, 2 * HC * e + i + 1)
                                if k == 0:
                                    act.wait_ge(y_full, ST * e + TH * (g + 1))
                                act.activation(h32[:, i % H_CREDIT, :], h_b[:, i % H_CREDIT, 0:HALF], ACT.Gelu)
                                act.activation(hT[g][0][:, k, :], h_b[:, i % H_CREDIT, 0:HALF], ACT.Gelu).then_inc(h_act, 1)
                                if not last:
                                    split_weights(e + 1, 1 - u, i)
                            if not last:
                                turned_rows(e + 1)

                        for i in range(W_CUTS):
                            split_weights(0, 0, i)
                        turned_rows(0)
                        with act.Fori(0, E // 2 - 1) as i:
                            expert(2 * i, 0, False)
                            expert(2 * i + 1, 1, False)
                        expert(E - 2, 0, False)
                        expert(E - 1, 1, True)

                    @block.vector
                    def _(dve):
                        def split_weights(e, u, i):
                            k = i % (W_CUTS // 2)
                            raw, to = (w1_raw, w1s[u]) if i < W_CUTS // 2 else (w2_raw, w2s[u])
                            c = slice(W1C * k, W1C * k + W1C)
                            dve.wait_ge(w_cut_hi, W_CUTS * e + i + 1)
                            dve.tensor_tensor(to[1][:, c], raw[:, c], to[0][:, c], ALU.subtract).then_inc(w_cut_lo, 1)

                        def turned_rows(e):
                            for i in range(4):
                                c, half = i // 2, i % 2
                                dve.wait_ge(gt_hi, 4 * e + i + 1)
                                cols = slice(HALF * half, HALF * half + HALF)
                                dve.tensor_tensor(gT[1][:, c, cols], gt_b[:, i % 2, 0:HALF], gT[0][:, c, cols],
                                                  ALU.subtract).then_inc(gt_lo, 1)

                        def outputs(e, g):
                            if g == 0:
                                dve.wait_ge(scattered, 16 * ST * e)
                            for t in range(TH):
                                i = TH * g + t
                                dve.wait_ge(y_full, ST * (e + 1) + i + 1)
                                dve.tensor_scalar(ys[:, i, :], y_b[:, i % 2, 0:D],
                                                  pvs[:, ds(e, 1), i:i + 1].rearrange("p a t -> p (a t)"), None,
                                                  ALU.mult).then_inc(y_ready, 1)

                        def expert(e, u, last):
                            for i in range(2 * HC):
                                g, k = i // HC, i % HC
                                dve.wait_ge(h_act, 2 * HC * e + i + 1)
                                dve.tensor_tensor(hT[g][1][:, k, :], h32[:, i % H_CREDIT, :], hT[g][0][:, k, :],
                                                  ALU.subtract).then_inc(h_lo_done, 1)
                                if not last:
                                    split_weights(e + 1, 1 - u, i)
                            outputs(e, 0)
                            if not last:
                                turned_rows(e + 1)
                            outputs(e, 1)

                        dve.sem_inc(h_lo_done, H_CREDIT)
                        for i in range(W_CUTS):
                            split_weights(0, 0, i)
                        dve.wait_ge(rows_in, 16)
                        for i in range(ROUNDS):
                            now, then = router[i % 2], router[(i + 1) % 2]
                            eight = slice(TOP * i, TOP * i + TOP)
                            dve.max(top_p[:, eight], now[:]).then_inc(pick, 1)
                            dve.wait_ge(pick, 3 * i + 1)
                            dve.max_index(top_i[:, eight], top_p[:, eight], now[:]).then_inc(pick, 1)
                            dve.match_replace(then[:], top_p[:, eight], now[:], -1.0).then_inc(pick, 1)
                            dve.wait_ge(pick, 3 * i + 3)
                        dve.wait_ge(row_id, 1)
                        dve.tensor_scalar(row_u[:, 1:2], row_u[:, 0:1], E.bit_length() - 1, None,
                                          ALU.logical_shift_right).then_inc(row_id, 1)
                        dve.wait_ge(row_id, 2)
                        dve.tensor_scalar(row_base[:, 0:1], row_u[:, 1:2], float(N), None, ALU.mult).then_inc(row_id, 1)
                        dve.tensor_copy(top_f[:], top_i[:]).then_inc(pick, 1)
                        dve.wait_ge(row_id, 3)
                        dve.wait_ge(pick, 3 * ROUNDS + 1)
                        dve.tensor_scalar(top_f[:], top_f[:], row_base[:, 0:1], None, ALU.add).then_inc(pick, 1)
                        dve.wait_ge(pick, 3 * ROUNDS + 2)
                        dve.tensor_copy(top_i[:], top_f[:]).then_inc(pick, 1)
                        dve.wait_ge(picks_in, 32)
                        turned_rows(0)
                        with dve.Fori(0, E // 2 - 1) as i:
                            expert(2 * i, 0, False)
                            expert(2 * i + 1, 1, False)
                        expert(E - 2, 0, False)
                        expert(E - 1, 1, True)


_INS = ["x", "txt", "L0_tok_W", "L0_tok_gamma", "L0_attn_norm_w", "L0_attn_Wq", "L0_attn_Wkv", "L0_attn_Wout",
        "L0_attn_Wg", "L0_ffn_gate_w", "L0_ffn_w1", "L0_ffn_w2"]


def kernel(**inputs):
    import numpy as _np
    import concourse.bacc as _bacc
    from concourse import mybir as _mybir
    from concourse.bass_utils import run_bass_kernel_spmd as _run

    nc = _bacc.Bacc("TRN2", target_bir_lowering=False, num_devices=1)
    arrays, args = {}, []
    for name in _INS:
        a = _np.ascontiguousarray(inputs[name])
        arrays[f"in_{name}"] = a
        args.append(nc.dram_tensor(f"in_{name}", a.shape, _mybir.dt.from_np(a.dtype), kind="ExternalInput").ap())
    B, _, img, _ = inputs["x"].shape
    _, n_txt, d = inputs["txt"].shape
    shape = (B, (img // PATCH) ** 2 + n_txt, d)
    args.append(nc.dram_tensor("out_0", shape, _mybir.dt.float32, kind="ExternalOutput").ap())
    fusion_block_kernel(nc, *args)
    r = _run(nc, [arrays], core_ids=[0])
    return r.results[0]["out_0"]
```

```python
from contextlib import ExitStack

import concourse.bass as bass
from concourse import mybir

F32 = mybir.dt.float32
F32R = mybir.dt.float32r
F16 = mybir.dt.float16
BF16 = mybir.dt.bfloat16
U32 = mybir.dt.uint32
ALU = mybir.AluOpType
ACT = mybir.ActivationFunctionType
AX = mybir.AxisListType
ds = bass.ds

P = 128
PATCH = 8
LN_EPS = 1e-5
RMS_EPS = 1.1920928955078125e-07
MASKED = -1e30
MAX_UNIT = 256.0

SCORE_PIECES = [
    [(0, 0, 512)],
    [(0, 512, 256), (4, 512, 256)],
    [(1, 128, 512)],
    [(1, 640, 128), (3, 384, 384)],
    [(2, 256, 512)],
    [(5, 640, 128)],
]
MAX_PIECES = [
    [(0, 0, 128, 0), (1, 0, 256, 1)],
    [(2, 0, 384, 2)],
    [(3, 0, 512, 3)],
    [(4, 0, 512, 4)],
    [(5, 0, 512, 5)],
    [(4, 512, 128, 6), (5, 512, 256, 7)],
]
NPIECE = len(SCORE_PIECES)


def piece_offsets():
    starts, where, at = [], {}, 0
    for piece in SCORE_PIECES:
        starts.append(at)
        for j, q0, w in piece:
            for q in range(q0, q0 + w, P):
                where[j, q // P] = at + q - q0
            at += w
    return starts, at, where


PIECE_START, PROB_COLS, PROB_AT = piece_offsets()


def fusion_block_kernel(nc, x, txt, tok_W, tok_gamma, norm_w, Wq, Wkv, Wout, Wg, gate_w, w1, w2, out):
    B, C_IN, IMG, _ = x.shape
    _, N_TXT, D = txt.shape
    GRID = IMG // PATCH
    N_IMG = GRID * GRID
    N = N_IMG + N_TXT
    NT = N // P
    NTI = N_IMG // P
    DC = D // P
    INNER = Wq.shape[1]
    HEADS = Wg.shape[1]
    DH = INNER // HEADS
    PAIRS = HEADS // 2
    COUPLES = PAIRS // 2
    E, _, HID = w1.shape
    HC = HID // P
    CAP = int(2.0 * N / E)
    SLOTS = B * CAP
    ST = SLOTS // P
    HALF = 384
    TH = HALF // P
    ROWS = C_IN * PATCH
    SHIFTS = 3
    TAPS = -(-PATCH // SHIFTS)
    VCOLS = INNER + HEADS
    V_PIECES = [(t, h0, 5, 0) for t in range(NT) for h0 in (0, 5)] + [(t, 10, 6, HEADS) for t in range(NT)]
    NV, V_EARLY, V_INNER = len(V_PIECES), 2 * NT, 6
    SCALE = float(DH) ** -0.5
    assert (N, SLOTS, DC, NT, DH) == (2 * HALF, 2 * HALF, 2, 6, 64)

    x2_dram = nc.dram_tensor("ffn_rows", (B * N, D), F32, kind="Internal").ap()
    p_dram = nc.dram_tensor("router_probs", (B * E, N), F32, kind="Internal").ap()
    picks_dram = nc.dram_tensor("picked_tokens", (B * E, 2, CAP), F32, kind="Internal").ap()
    out_rows = out.rearrange("b n d -> (b n) d")

    top = ExitStack()
    with top:
        def sem(name):
            return top.enter_context(nc.semaphore(name))

        const_in = sem("const_in")
        qk_w_in = sem("qk_w_in")
        v_w_in = sem("v_w_in")
        o_w_in = sem("o_w_in")
        v_w_cut = sem("v_w_cut")
        o_w_cut = sem("o_w_cut")
        consts = sem("consts")
        img_in_0 = sem("img_in_0")
        img_in_last = sem("img_in_last")
        img_in = sem("img_in")
        txt_in_0 = sem("txt_in_0")
        txt_in = sem("txt_in")
        h_copied = sem("h_copied")
        pair_w = sem("pair_w")
        tok_full = sem("tok_full")
        ln = sem("ln")
        root_in = sem("root_in")
        root_out = sem("root_out")
        ln2 = sem("ln2")
        root2_in = sem("root2_in")
        root2_out = sem("root2_out")
        x_ready = sem("x_ready")
        xt_full = sem("xt_full")
        xt_hi = sem("xt_hi")
        xt_lo = sem("xt_lo")
        v_full = sem("v_full")
        v_hi_done = sem("v_hi_done")
        v_lo_done = sem("v_lo_done")
        gate_ready = sem("gate_ready")
        pj_full = sem("pj_full")
        pj_hi = sem("pj_hi")
        pj_free = sem("pj_free")
        spread_q = sem("spread_q")
        spread_k = sem("spread_k")
        spread_m = [sem(f"spread_m_{hd}") for hd in range(2)]
        mx_full = sem("mx_full")
        mx_free = sem("mx_free")
        max_ready = sem("max_ready")
        mt_full = sem("mt_full")
        mt_copied = sem("mt_copied")
        st_full = sem("st_full")
        st_free = sem("st_free")
        p_lo_done = sem("p_lo_done")
        pv_done = sem("pv_done")
        normed = sem("normed")
        at_full = sem("at_full")
        at_hi = sem("at_hi")
        at_lo = sem("at_lo")
        op_full = sem("op_full")
        op_added = sem("op_added")
        x2_ready = sem("x2_ready")
        h_stored = sem("h_stored")
        x2_stored = sem("x2_stored")
        x2t_full = sem("x2t_full")
        x2t_copied = sem("x2t_copied")
        logits_full = sem("logits_full")
        soft = sem("soft")
        logit_exp = sem("logit_exp")
        probs_ready = sem("probs_ready")
        pt_full = sem("pt_full")
        pt_copied = sem("pt_copied")
        p_stored = sem("p_stored")
        rows_in = sem("rows_in")
        pick = sem("pick")
        second_in = sem("second_in")
        picks_stored = sem("picks_stored")
        picks_in = sem("picks_in")
        row_id = sem("row_id")
        w_raw_in = sem("w_raw_in")
        w_cut_hi = sem("w_cut_hi")
        w_cut_lo = sem("w_cut_lo")
        ids_copied = sem("ids_copied")
        gathered = [[sem(f"gathered_{u}_{half}") for half in range(2)] for u in range(2)]
        scattered = sem("scattered")
        gt_full = sem("gt_full")
        gt_hi = sem("gt_hi")
        gt_lo = sem("gt_lo")
        h_full = sem("h_full")
        h_act = sem("h_act")
        h_lo_done = sem("h_lo_done")
        y_full = sem("y_full")
        y_ready = sem("y_ready")

        fence = sem("fence")

        def is_first_couple(c):
            return isinstance(c, int) and c == 0

        def is_last_couple(c):
            return isinstance(c, int) and c == COUPLES - 1

        def wait_apart(eng, s, value):
            eng.wait_ge(s, value)
            eng.sem_inc(fence, 1)

        PJ_CREDIT = 8
        PV_CREDIT = 2
        SPREAD = 6 * 16
        RING32 = 3
        LN_STEPS = 11
        LN2_STEPS = 3
        SOFT_STEPS = 4
        IMG_DMAS = SHIFTS * C_IN
        CONSTS_IN = 16 * (1 + SHIFTS + DC + 1)
        H_CREDIT = 4

        small = ExitStack()
        with small:
            def sb_small(name, shape, dt):
                return small.enter_context(nc.sbuf_tensor(name, shape, dt))

            ident = sb_small("ident", [P, P], F32)

            attn = ExitStack()

            def sb(name, shape, dt):
                return attn.enter_context(nc.sbuf_tensor(name, shape, dt))

            wq_raw = sb("wq_raw", [P, DC, INNER], F32)
            wk_raw = sb("wk_raw", [P, DC, INNER], F32)
            stage = sb("stage", [P, DC * VCOLS], F32)
            wv = [sb(f"wv_{s}", [P, DC, VCOLS], F32R) for s in ("hi", "lo")]
            wo = [sb(f"wo_{s}", [P, PAIRS, D], F32R) for s in ("hi", "lo")]
            wp = [[sb(f"wp{u}_{s}", [P, 2, DC, P], F32R) for s in ("hi", "lo")] for u in range(2)]
            tok_w = sb("tok_w", [P, TAPS, D], F32)
            gamma = sb("gamma", [P, D], F32)
            nw = sb("nw", [P, DC], F32)
            gw = sb("gw", [P, DC, E], F32)
            ident_b = sb("ident_b", [P, P], BF16)
            mask_q = sb("mask_q", [P, P], BF16)
            mask_k = sb("mask_k", [P, P], BF16)
            img = sb("img", [P, GRID, IMG], F32)
            h = sb("h", [P, NT, D], F32)
            xn = sb("xn", [P, NT, D], F32)
            xT = [sb(f"xT_{s}", [P, DC, N], F32R) for s in ("hi", "lo")]
            cut = [[sb(f"cut_{w}_{s}", [P, N], F16) for s in ("hi", "lo")] for w in "qk"]
            key_both = sb("key_both", [P, 2, 2, N], F16)
            key_max = sb("key_max", [P, 2, 2, N], F16)
            query_both = sb("query_both", [P, 2, 2, N], F16)
            query_max = sb("query_max", [P, 2, 2, N], F16)
            v_hi = sb("v_hi", [P, NT, HEADS, DH + 1], F16)
            v_lo = sb("v_lo", [P, NT, HEADS, DH], F16)
            p32 = sb("p32", [P, RING32, 512], F32)
            p_hi = sb("p_hi", [P, 2, PROB_COLS], F16)
            p_lo = sb("p_lo", [P, 2, PROB_COLS], F16)
            heads_out = sb("heads_out", [P, NT, P], F32)
            aT = [sb(f"aT_{s}", [P, 2, N], F32R) for s in ("hi", "lo")]
            gate = sb("gate", [P, NT, HEADS], F32)
            stats = sb("stats", [P, NT, 6], F32)
            mv = sb("mv", [P, NT, 2], F32)
            rt = sb("rt", [P, 6, NT], F32)
            mx = sb("mx", [P, 2, 8], F32)
            m_row = sb("m_row", [NT, 2, P], F16)
            den = sb("den", [P, 2, NT], F32)
            probs = sb("probs", [P, NT, E], F32)
            rsm = sb("rsm", [P, 3, NT], F32)
            pT = sb("pT", [E, N], F32)
            h_next = stage[:, 0:NT * D].rearrange("p (t d) -> p t d", t=NT)
            x2T = img[:].rearrange("p a b -> p (a b)")[:, 0:DC * N].rearrange("p (c n) -> p c n", c=DC)

            psum = ExitStack()

            def ps(name, shape):
                return psum.enter_context(nc.psum_tensor(name, shape, F32))

            st_b = ps("st_b", [P, 2, 512])
            mx_b = ps("mx_b", [P, 2, 512])
            pj_b = ps("pj_b", [P, 2, 512])
            o_b = ps("o_b", [P, 512])
            tr_b = ps("tr_b", [P, 512])
            o_v = o_b[:, 0:NT * (DH + 1)].rearrange("p (t d) -> p t d", t=NT)
            four = [st_b[:, 0], st_b[:, 1], mx_b[:, 0], mx_b[:, 1]]
            v_bank = [2 + i % 2 if i < V_INNER else (i - (V_INNER if i < V_EARLY else V_EARLY)) % 4
                      for i in range(NV)]

            def load_image(eng, b, g, done):
                for c in range(C_IN):
                    r = ROWS * g + PATCH * c
                    src = x[ds(b, 1), c].rearrange("a (g q) w -> (a q) g w", q=PATCH)
                    eng.dma_start(img[r:r + PATCH, :, 0:IMG - g], src[:, :, g:IMG]).then_inc(done, 16)

            def load_text(eng, b, to, done):
                src = txt[ds(b, 1)].rearrange("a (t p) d -> (a p) t d", p=P)
                eng.dma_start(to[:, NTI:NT, :], src).then_inc(done, 16)

            with nc.Block() as block:
                @block.sync
                def _(sp):
                    for g in range(SHIFTS - 1):
                        load_image(sp, 0, g, img_in_0)
                    load_text(sp, 0, h, txt_in_0)

                    def spread(which, n, u):
                        sp.wait_ge(pj_free, PJ_CREDIT + 4 * n + 2 * which + 2)
                        both, one = (query_both, query_max) if which == 0 else (key_both, key_max)
                        hi, lo = cut[which]
                        done = spread_q if which == 0 else spread_k
                        for hd in range(2):
                            half = slice(DH * hd, DH * hd + DH)
                            if which == 0:
                                moves = [(both[0:64, u, hd], hi), (both[64:128, u, hd], hi), (one[0:64, u, hd], lo)]
                            else:
                                moves = [(both[0:64, u, hd], hi), (both[64:128, u, hd], lo), (one[0:64, u, hd], hi)]
                            for dst, src in moves:
                                sp.dma_start(dst, src[half, :]).then_inc(done, 16)

                    def max_row(n, u, hd):
                        sp.wait_ge(mt_copied, 2 * n + hd + 1)
                        sp.dma_start(query_max[64:65, u, hd, :], m_row[:, hd, :]).then_inc(spread_m[hd], 16)

                    def pair_step(n, u):
                        sp.wait_ge(st_full, 12 * n)
                        spread(0, n + 1, 1 - u)
                        spread(1, n + 1, 1 - u)
                        max_row(n, u, 1)
                        max_row(n + 1, 1 - u, 0)

                    def batch(b, more):
                        with sp.Fori(0, COUPLES - 1) as c:
                            pair_step(PAIRS * b + 2 * c, 0)
                            pair_step(PAIRS * b + 2 * c + 1, 1)
                        n = PAIRS * b + PAIRS - 1
                        pair_step(n - 1, 0)
                        max_row(n, 1, 1)
                        if more:
                            sp.wait_ge(st_full, 12 * n)
                            spread(0, n + 1, 0)
                            spread(1, n + 1, 0)
                        sp.wait_ge(op_added, 3 * COUPLES * (b + 1))
                        dst = out_rows[ds(b * N, N), :].rearrange("(t p) d -> p t d", p=P)
                        sp.dma_start(dst, h[:]).then_inc(h_stored, 16)
                        if more:
                            max_row(n + 1, 0, 0)

                    spread(0, 0, 0)
                    spread(1, 0, 0)
                    max_row(0, 0, 0)
                    with sp.Fori(0, B - 1) as b:
                        batch(b, True)
                    batch(B - 1, False)

                @block.gpsimd
                def _(pool):
                    stage_v = stage[:].rearrange("p (c n) -> p c n", c=DC)
                    wv_src = Wkv.rearrange("(c p) n -> p c n", p=P)
                    pool.dma_start(stage_v[:, :, 0:INNER], wv_src[:, :, INNER:2 * INNER]).then_inc(v_w_in, 16)
                    pool.dma_start(stage_v[:, :, INNER:VCOLS], Wg.rearrange("(c p) n -> p c n", p=P)).then_inc(v_w_in, 16)
                    load_image(pool, 0, SHIFTS - 1, img_in_last)
                    pool.dma_start(wq_raw[:], Wq.rearrange("(c p) n -> p c n", p=P)).then_inc(qk_w_in, 16)
                    pool.dma_start(wk_raw[:], Wkv.rearrange("(c p) n -> p c n", p=P)[:, :, 0:INNER]).then_inc(qk_w_in, 16)
                    pool.memset(ident[:], 0.0)
                    pool.memset(ident_b[:], 0.0)
                    pool.memset(mask_q[:], 0.0)
                    pool.memset(mask_k[:], 0.0)
                    pool.memset(v_hi[:, :, :, DH:DH + 1], 1.0).then_inc(consts, 1)
                    pool.wait_ge(consts, 2)
                    for m in (ident, ident_b):
                        pool.affine_select(out=m[:], in_=m[:], compare_op=ALU.not_equal, fill=1.0, base=0,
                                           pattern=[[-1, P]], channel_multiplier=1)
                    pool.affine_select(out=mask_q[:], in_=mask_q[:], compare_op=ALU.is_ge, fill=MASKED, base=0,
                                       pattern=[[-1, P]], channel_multiplier=1)
                    pool.affine_select(out=mask_k[:], in_=mask_k[:], compare_op=ALU.is_ge, fill=MASKED, base=0,
                                       pattern=[[1, P]], channel_multiplier=-1).then_inc(consts, 1)
                    def split_pair(n, p, u):
                        wait_apart(pool, pj_free, 4 * n + PJ_CREDIT - 4)
                        cols = ds(p * P, P)
                        for i, raw in enumerate((wq_raw, wk_raw)):
                            pool.tensor_copy(wp[u][0][:, i], raw[:, :, cols]).then_inc(pair_w, 1)
                        wait_apart(pool, pair_w, 4 * n + 2)
                        for i, raw in enumerate((wq_raw, wk_raw)):
                            pool.tensor_tensor(wp[u][1][:, i], raw[:, :, cols], wp[u][0][:, i],
                                               ALU.subtract).then_inc(pair_w, 1)

                    def split_pairs(b, first_couple, couples):
                        with pool.Fori(first_couple, couples) as c:
                            for u in range(2):
                                split_pair(PAIRS * b + 2 * c + u, 2 * c + u, u)

                    def next_image(b):
                        pool.wait_ge(tok_full, NTI * (b + 1))
                        for g in range(SHIFTS):
                            load_image(pool, b + 1, g, img_in)

                    def store_x2(b):
                        pool.wait_ge(x2_ready, b + 1)
                        dst = x2_dram[ds(b * N, N), :].rearrange("(t p) d -> p t d", p=P)
                        pool.dma_start(dst, xn[:]).then_inc(x2_stored, 16)

                    def store_probs(b):
                        pool.wait_ge(pt_copied, 2 * (b + 1))
                        pool.dma_start(p_dram[ds(b * E, E), :], pT[:]).then_inc(p_stored, 16)

                    def batch(b, more):
                        split_pairs(b, 0, 2)
                        store_x2(b - 1)
                        wait_apart(pool, x_ready, b + 1)
                        wait_apart(pool, h_stored, 16 * b)
                        pool.tensor_copy(h[:], h_next).then_inc(h_copied, 1)
                        if more:
                            pool.wait_ge(h_copied, b)
                            load_text(pool, b + 1, h_next, txt_in)
                        store_probs(b - 1)
                        split_pairs(b, 2, COUPLES)
                        if more:
                            pool.wait_ge(logits_full, b)
                            next_image(b)

                    pool.wait_ge(qk_w_in, 32)
                    for u in range(2):
                        split_pair(u, u, u)
                    pool.wait_ge(v_w_cut, 2)
                    pool.dma_start(stage[:, 0:PAIRS * D].rearrange("p (k n) -> p k n", k=PAIRS),
                                   Wout.rearrange("(k p) n -> p k n", p=P)).then_inc(o_w_in, 16)
                    split_pairs(0, 1, COUPLES)
                    next_image(0)
                    pool.wait_ge(o_w_cut, 2)
                    load_text(pool, 1, h_next, txt_in)
                    with pool.Fori(1, B - 1) as b:
                        batch(b, True)
                    batch(B - 1, False)
                    store_x2(B - 1)
                    store_probs(B - 1)

                @block.tensor
                def _(pe):
                    def three_terms(dst, lhs, rhs, first, last):
                        terms = [(0, 0), (1, 0), (0, 1)]
                        for i, (a, c) in enumerate(terms):
                            mm = pe.matmul(dst, lhs[a], rhs[c], start=first and i == 0, stop=last and i == 2)
                        return mm

                    def project(which, half, n, u):
                        pe.wait_ge(pj_free, 4 * n + 2 * which + half + 1 + PJ_CREDIT - 2)
                        for c in range(DC):
                            mm = three_terms(
                                pj_b[:, half, 0:HALF],
                                [w[:, which, c, :] for w in wp[u]],
                                [t[:, c, HALF * half:HALF * half + HALF] for t in xT],
                                c == 0, c == DC - 1)
                        mm.then_inc(pj_full, 1)

                    def max_piece(n, u, hd, i):
                        pe.wait_ge(mx_free, 12 * n + 6 * hd + i + 1)
                        at = 0
                        for q, k0, w, _ in MAX_PIECES[i]:
                            dst = mx_b[:, i % 2, at:at + w]
                            diag = k0 <= q * P < k0 + w
                            mm = pe.matmul(dst, query_both[:, u, hd, q * P:q * P + P],
                                           key_both[:, u, hd, k0:k0 + w], start=True, stop=not diag)
                            if diag:
                                d0 = at + q * P - k0
                                mm = pe.matmul(mx_b[:, i % 2, d0:d0 + P], ident_b[:], mask_q[:],
                                               start=False, stop=True)
                            at += w
                        mm.then_inc(mx_full, 1)

                    def turn_maxima(n, hd):
                        pe.wait_ge(max_ready, 2 * n + hd + 1)
                        pe.transpose(tr_b[0:NT, 0:P], mx[:, hd, 0:NT], ident[:]).then_inc(mt_full, 1)

                    def score_piece(n, u, hd, i):
                        pe.wait_ge(st_free, 12 * n + 6 * hd + i + 1)
                        at = 0
                        for j, q0, w in SCORE_PIECES[i]:
                            dst = st_b[:, i % 2, at:at + w]
                            ks = slice(j * P, j * P + P)
                            diag = q0 == j * P
                            pe.matmul(dst, key_both[:, u, hd, ks], query_both[:, u, hd, q0:q0 + w],
                                      start=True, stop=False)
                            mm = pe.matmul(dst, key_max[0:65, u, hd, ks], query_max[0:65, u, hd, q0:q0 + w],
                                           start=False, stop=not diag)
                            if diag:
                                mm = pe.matmul(st_b[:, i % 2, at:at + P], ident_b[:], mask_k[:],
                                               start=False, stop=True)
                            at += w
                        mm.then_inc(st_full, 1)

                    def weigh_values(n, hd, head, tiles):
                        if tiles[0] == 0:
                            pe.wait_ge(p_lo_done, RING32 + 12 * n + 6 * hd + 6)
                            pe.wait_ge(normed, 3 * (2 * n + hd))
                        for q in tiles:
                            for j in range(q + 1):
                                ps_ = slice(PROB_AT[j, q], PROB_AT[j, q] + P)
                                first, last = j == 0, j == q
                                pe.matmul(o_v[:, q, 0:DH + 1], p_hi[:, hd, ps_], v_hi[:, j, ds(head, 1), :],
                                          start=first, stop=False)
                                pe.matmul(o_v[:, q, 0:DH], p_hi[:, hd, ps_], v_lo[:, j, ds(head, 1), :],
                                          start=False, stop=False)
                                mm = pe.matmul(o_v[:, q, 0:DH + 1], p_lo[:, hd, ps_], v_hi[:, j, ds(head, 1), :],
                                               start=False, stop=last)
                        if tiles[-1] == NT - 1:
                            mm.then_inc(pv_done, 1)

                    def turn_outputs(n, half):
                        if half:
                            pe.wait_ge(at_lo, 2 * n + 1)
                        else:
                            pe.wait_ge(normed, 3 * (2 * n + 2))
                        for t in range(TH):
                            mm = pe.transpose(tr_b[:, t * P:t * P + P], heads_out[:, TH * half + t, :], ident[:])
                        mm.then_inc(at_full, 1)

                    def project_out(c, couple, k):
                        if k == 0:
                            pe.wait_ge(at_lo, 4 * (couple + 1))
                            pe.wait_ge(o_w_cut, 2)
                        if k == 2:
                            pe.wait_ge(op_added, 3 * couple + 1)
                        for t in range(2):
                            tok = slice((2 * k + t) * P, (2 * k + t) * P + P)
                            for u in range(2):
                                mm = three_terms(pj_b[:, k % 2, D * t:D * t + D],
                                                 [a[:, u, tok] for a in aT],
                                                 [w[:, ds(2 * c + u, 1), :] for w in wo],
                                                 u == 0, u == 1)
                        mm.then_inc(op_full, 1)

                    def project_tokens(b, t, arrived, count):
                        pe.wait_ge(arrived, count)
                        for k in range(TAPS):
                            rows = ROWS * min(SHIFTS, PATCH - SHIFTS * k)
                            gr = GRID // NTI
                            lhs = img[0:rows, gr * t:gr * t + gr, SHIFTS * k:IMG:PATCH]
                            mm = pe.matmul(pj_b[:, t, 0:D], lhs, tok_w[0:rows, k, :],
                                           start=k == 0, stop=k == TAPS - 1)
                        mm.then_inc(tok_full, 1)

                    def turn_x(b, i):
                        c, half = i // 2, i % 2
                        pe.wait_ge(x_ready, b + 1)
                        if i >= 2:
                            pe.wait_ge(xt_lo, 4 * b + i - 1)
                        for t in range(TH):
                            mm = pe.transpose(pj_b[:, half, t * P:t * P + P],
                                              xn[:, TH * half + t, c * P:c * P + P], ident[:])
                        mm.then_inc(xt_full, 1)

                    def first_head(b, c, u, first, more, router):
                        p = 2 * c + u
                        n = PAIRS * b + p
                        out_now = u == 1 and not is_first_couple(c)
                        last = is_last_couple(c) and u == 1
                        front = is_last_couple(c) and u == 0 and more
                        turn = last and more
                        couple = COUPLES * b + c - 1
                        if first:
                            pe.wait_ge(v_lo_done, NV * (b + 1))
                        max_piece(n, u, 1, 0)
                        max_piece(n, u, 1, 1)
                        pe.wait_ge(spread_m[0], 16 * (n + 1))
                        score_piece(n, u, 0, 0)
                        score_piece(n, u, 0, 1)
                        if front:
                            pe.wait_ge(pj_free, PJ_CREDIT + 4 * (n + 2))
                            pe.wait_ge(op_added, 3 * couple)
                            project_tokens(b + 1, 0, img_in, 16 * IMG_DMAS * (b + 1))
                        max_piece(n, u, 1, 2)
                        if out_now and not turn:
                            pe.wait_ge(pj_free, PJ_CREDIT + (4 * (n + 1) if last else 4 * (n + 2)))
                            project_out(c - 1, couple, 0)
                        max_piece(n, u, 1, 3)
                        score_piece(n, u, 0, 2)
                        if router:
                            turn_x2(b - 1, 0)
                        if not first:
                            weigh_values(n - 1, 1, 2 * p - 1, (0, 1, 2))
                        max_piece(n, u, 1, 4)
                        score_piece(n, u, 0, 3)
                        if turn:
                            turn_x(b + 1, 0)
                            turn_x(b + 1, 1)
                        if router:
                            turn_x2(b - 1, 1)
                        max_piece(n, u, 1, 5)
                        if front:
                            project_tokens(b + 1, 1, img_in, 16 * IMG_DMAS * (b + 1))
                        if out_now and not turn:
                            project_out(c - 1, couple, 1)
                        score_piece(n, u, 0, 4)
                        if turn:
                            turn_x(b + 1, 2)
                            turn_x(b + 1, 3)
                        if router:
                            turn_x2(b - 1, 2)
                        pe.wait_ge(mt_copied, 2 * n + 1)
                        pe.wait_ge(at_lo, 2 * n if first else 2 * (n - 1))
                        turn_maxima(n, 1)
                        score_piece(n, u, 0, 5)
                        if router:
                            turn_x2(b - 1, 3)
                        if out_now and not turn:
                            project_out(c - 1, couple, 2)
                        if not first:
                            weigh_values(n - 1, 1, 2 * p - 1, (3, 4, 5))
                        if turn:
                            pe.wait_ge(pj_free, PJ_CREDIT + 4 * (n + 1))
                            pe.wait_ge(xt_lo, 4 * (b + 2))
                            for k in range(NT // 2):
                                project_out(c - 1, couple, k)

                    def second_head(b, c, u, first, more, router):
                        p = 2 * c + u
                        n = PAIRS * b + p
                        last = is_last_couple(c) and u == 1
                        ahead = not is_last_couple(c) or (last and more)
                        to = n + 1 if last else n + 2
                        par = 0 if last else u
                        if not last:
                            pe.wait_ge(spread_q, SPREAD * (n + 2))
                            pe.wait_ge(spread_k, SPREAD * (n + 2))
                            max_piece(n + 1, 1 - u, 0, 0)
                            max_piece(n + 1, 1 - u, 0, 1)
                        pe.wait_ge(spread_m[1], 16 * (n + 1))
                        score_piece(n, u, 1, 0)
                        if router:
                            logits(b - 1)
                        score_piece(n, u, 1, 1)
                        if last and more:
                            value_piece(b + 1, 0)
                        if router:
                            pe.wait_ge(soft, SOFT_STEPS * (b - 1) + 2)
                        weigh_values(n, 0, 2 * p, (0, 1, 2))
                        if not last:
                            max_piece(n + 1, 1 - u, 0, 2)
                        if not first:
                            pe.wait_ge(mt_copied, 2 * n + 2)
                            turn_outputs(n - 1, 0)
                        if not last:
                            max_piece(n + 1, 1 - u, 0, 3)
                        score_piece(n, u, 1, 2)
                        if router:
                            turn_probs(b - 1)
                        if last and more:
                            value_piece(b + 1, 1)
                        done = 3 * (COUPLES * b + c)
                        if ahead and not router:
                            project_next(to, par, 0, done if u == 1 or is_first_couple(c) else done - 3)
                        if not last:
                            max_piece(n + 1, 1 - u, 0, 4)
                        score_piece(n, u, 1, 3)
                        if router:
                            pe.wait_ge(pt_copied, 2 * b)
                            project_next(to, par, 0, done)
                        if last and more:
                            value_piece(b + 1, 2)
                        if not last:
                            max_piece(n + 1, 1 - u, 0, 5)
                        if not first:
                            turn_outputs(n - 1, 1)
                        if ahead:
                            project(0, 1, to, par)
                        score_piece(n, u, 1, 4)
                        if last and more:
                            value_piece(b + 1, 3)
                        weigh_values(n, 0, 2 * p, (3,))
                        if not last:
                            pe.wait_ge(mt_copied, 2 * n + 2)
                            if not first:
                                pe.wait_ge(at_lo, 2 * n)
                            turn_maxima(n + 1, 0)
                        if ahead:
                            project(1, 0, to, par)
                        score_piece(n, u, 1, 5)
                        if last and more:
                            value_piece(b + 1, 4)
                        if ahead:
                            project(1, 1, to, par)
                        weigh_values(n, 0, 2 * p, (4, 5))
                        if last and more:
                            value_piece(b + 1, 5)

                    def project_next(n, u, half, added):
                        pe.wait_ge(pair_w, 4 * n + 4)
                        pe.wait_ge(op_added, added)
                        project(0, half, n, u)

                    def couple_step(b, c, more, router=False):
                        for u in range(2):
                            first = is_first_couple(c) and u == 0
                            first_head(b, c, u, first, more, router and u == 0)
                            second_head(b, c, u, first, more, router and u == 0)

                    def finish(b, more):
                        n = PAIRS * b + PAIRS - 1
                        weigh_values(n, 1, HEADS - 1, tuple(range(NT)))
                        if more:
                            for i in range(V_INNER, V_INNER + 3):
                                value_piece(b + 1, i)
                        pe.wait_ge(mt_copied, 2 * n + 2)
                        pe.wait_ge(at_lo, 2 * n)
                        turn_outputs(n, 0)
                        if more:
                            value_piece(b + 1, V_INNER + 3)
                        turn_outputs(n, 1)
                        if more:
                            for i in range(V_INNER + 4, V_EARLY):
                                value_piece(b + 1, i)
                        pe.wait_ge(pj_free, PJ_CREDIT + 4 * (n + (2 if more else 1)))
                        for k in range(NT // 2):
                            project_out(COUPLES - 1, COUPLES * b + COUPLES - 1, k)

                    def value_piece(b, i):
                        if i == 0:
                            pe.wait_ge(xt_lo, 4 * (b + 1))
                            pe.wait_ge(v_w_cut, 2)
                            pe.wait_ge(mx_free, 2 + 12 * PAIRS * b)
                        if i == V_INNER:
                            pe.wait_ge(st_free, 2 + 12 * PAIRS * b)
                        if i == V_EARLY + 2:
                            pe.wait_ge(mx_free, 2 + 12 * PAIRS * b + 6)
                        before = [j for j in range(i) if v_bank[j] == v_bank[i]]
                        if before:
                            pe.wait_ge(v_lo_done, NV * b + before[-1] + 1)
                        t, h0, nh, ng = V_PIECES[i]
                        w = nh * DH + ng
                        for c in range(DC):
                            mm = three_terms(four[v_bank[i]][:, 0:w],
                                             [a[:, c, t * P:t * P + P] for a in xT],
                                             [a[:, c, h0 * DH:h0 * DH + w] for a in wv],
                                             c == 0, c == DC - 1)
                        mm.then_inc(v_full, 1)

                    def first_maxima(b):
                        pe.wait_ge(v_lo_done, NV * b + V_EARLY)
                        pe.wait_ge(spread_q, SPREAD * (PAIRS * b + 1))
                        pe.wait_ge(spread_k, SPREAD * (PAIRS * b + 1))
                        for i in range(NPIECE):
                            max_piece(PAIRS * b, 0, 0, i)

                    def project_second(b, i):
                        if i == 0:
                            project_next(PAIRS * b + 1, 1, 0, 3 * COUPLES * b)
                        else:
                            project(i // 2, i % 2, PAIRS * b + 1, 1)

                    def turn_first_maxima(b):
                        pe.wait_ge(at_lo, 2 * PAIRS * b)
                        turn_maxima(PAIRS * b, 0)

                    def turn_x2(b, i, bank=None):
                        c, half = i // 2, i % 2
                        if i == 0:
                            pe.wait_ge(x2_ready, b + 1)
                            pe.wait_ge(normed, 3 * HEADS * (b + 1))
                        elif bank is None:
                            pe.wait_ge(x2t_copied, 4 * b + i)
                        to = o_b if bank is None else bank
                        for t in range(TH):
                            mm = pe.transpose(to[:, t * P:t * P + P], xn[:, TH * half + t, c * P:c * P + P], ident[:])
                        mm.then_inc(x2t_full, 1)

                    def logits(b):
                        pe.wait_ge(x2t_copied, 4 * (b + 1))
                        for t in range(NT):
                            for c in range(DC):
                                mm = pe.matmul(o_b[:, t * E:t * E + E], x2T[:, c, t * P:t * P + P], gw[:, c, :],
                                               start=c == 0, stop=c == DC - 1)
                        mm.then_inc(logits_full, 1)

                    def turn_probs(b):
                        pe.wait_ge(probs_ready, b + 1)
                        for half in range(2):
                            for t in range(TH):
                                mm = pe.transpose(pj_b[0:E, half, t * P:t * P + P], probs[:, TH * half + t, :], ident[:])
                            mm.then_inc(pt_full, 1)

                    def batch(b, more):
                        with pe.Fori(1, COUPLES - 1) as c:
                            couple_step(b, c, more)
                        couple_step(b, COUPLES - 1, more)
                        finish(b, more)
                        if more:
                            first_maxima(b + 1)
                            value_piece(b + 1, V_EARLY)
                            value_piece(b + 1, V_EARLY + 1)
                            turn_first_maxima(b + 1)
                            for i in range(4):
                                value_piece(b + 1, V_EARLY + 2 + i)
                                project_second(b + 1, i)
                            couple_step(b + 1, 0, True, True)
                        else:
                            pe.wait_ge(st_free, 2 + 12 * PAIRS * (b + 1))
                            pe.wait_ge(mx_free, 2 + 12 * PAIRS * (b + 1))
                            for i in range(4):
                                turn_x2(b, i, four[i])
                            logits(b)
                            turn_probs(b)

                    pe.sem_inc(pv_done, PV_CREDIT)
                    pe.wait_ge(consts, 3)
                    pe.wait_ge(const_in, CONSTS_IN)
                    pe.wait_ge(img_in_last, 16 * C_IN)
                    for t in range(NTI):
                        project_tokens(0, t, img_in_0, 16 * C_IN * (SHIFTS - 1))
                    for i in range(4):
                        turn_x(0, i)
                    pe.wait_ge(xt_lo, 4)
                    project_next(0, 0, 0, 0)
                    project(0, 1, 0, 0)
                    project(1, 0, 0, 0)
                    project(1, 1, 0, 0)
                    for i in range(V_EARLY):
                        value_piece(0, i)
                    first_maxima(0)
                    value_piece(0, V_EARLY)
                    value_piece(0, V_EARLY + 1)
                    turn_first_maxima(0)
                    for i in range(4):
                        value_piece(0, V_EARLY + 2 + i)
                        project_second(0, i)
                    couple_step(0, 0, True)
                    with pe.Fori(0, B - 1) as b:
                        batch(b, True)
                    batch(B - 1, False)

                @block.scalar
                def _(act):
                    def split_projection(which, half, n):
                        if half == 0:
                            act.wait_ge(spread_q if which == 0 else spread_k, SPREAD * n)
                        act.wait_ge(pj_full, 4 * n + 2 * which + half + 1)
                        act.activation(cut[which][0][:, HALF * half:HALF * half + HALF],
                                       pj_b[:, half, 0:HALF], ACT.Copy).then_inc(pj_hi, 1)

                    def exponentials(n, hd, i):
                        if i == 0:
                            act.wait_ge(pv_done, 2 * n + hd + 1)
                        w = sum(q[2] for q in SCORE_PIECES[i])
                        act.wait_ge(st_full, 12 * n + 6 * hd + i + 1)
                        act.wait_ge(p_lo_done, 12 * n + 6 * hd + i + 1)
                        at = PIECE_START[i]
                        act.activation(p32[:, i % RING32, 0:w], st_b[:, i % 2, 0:w], ACT.Exp, scale=SCALE)
                        act.activation(p_hi[:, hd, at:at + w], st_b[:, i % 2, 0:w], ACT.Exp,
                                       scale=SCALE).then_inc(st_free, 1)

                    def max_row(n, hd):
                        act.wait_ge(mt_full, 2 * n + hd + 1)
                        act.wait_ge(spread_m[hd], 16 * n)
                        act.activation(m_row[:, hd, :], tr_b[0:NT, 0:P], ACT.Copy,
                                       scale=-1.0 / MAX_UNIT).then_inc(mt_copied, 1)

                    def turned_outputs(n, u, couple, half):
                        if half == 0:
                            act.wait_ge(op_full, 3 * couple)
                        act.wait_ge(at_full, 2 * n + half + 1)
                        act.activation(aT[0][:, u, HALF * half:HALF * half + HALF], tr_b[:, 0:HALF],
                                       ACT.Copy).then_inc(at_hi, 1)

                    def root(k, src, dst):
                        act.wait_ge(root_in, k + 1)
                        act.activation(dst, src, ACT.Sqrt).then_inc(root_out, 1)

                    def turned_x(b, i):
                        c, half = i // 2, i % 2
                        act.wait_ge(xt_full, 4 * b + i + 1)
                        act.activation(xT[0][:, c, HALF * half:HALF * half + HALF], pj_b[:, half, 0:HALF], ACT.Copy,
                                       scale=nw[:, c:c + 1]).then_inc(xt_hi, 1)

                    def first_head(b, c, u, first, more, router):
                        n = PAIRS * b + 2 * c + u
                        front = is_last_couple(c) and u == 0 and more
                        turn = is_last_couple(c) and u == 1 and more
                        exponentials(n, 0, 0)
                        exponentials(n, 0, 1)
                        exponentials(n, 0, 2)
                        if turn:
                            turned_x(b + 1, 0)
                            turned_x(b + 1, 1)
                        if router:
                            turned_x2(b - 1, 0)
                        exponentials(n, 0, 3)
                        if turn:
                            turned_x(b + 1, 2)
                            turned_x(b + 1, 3)
                        if router:
                            turned_x2(b - 1, 1)
                        max_row(n, 1)
                        exponentials(n, 0, 4)
                        if router:
                            turned_x2(b - 1, 2)
                        exponentials(n, 0, 5)
                        if router:
                            turned_x2(b - 1, 3)
                        if front:
                            root(2 * (b + 1), rt[:, 0, 0:NTI], rt[:, 1, 0:NTI])

                    def second_head(b, c, u, first, more, router):
                        n = PAIRS * b + 2 * c + u
                        before = COUPLES * b + c - (1 if u == 0 else 0)
                        last = is_last_couple(c) and u == 1
                        front = is_last_couple(c) and u == 0 and more
                        ahead = not is_last_couple(c) or (last and more)
                        to = n + 1 if last else n + 2
                        exponentials(n, 1, 0)
                        exponentials(n, 1, 1)
                        if router:
                            exp_logits(b - 1)
                        if last and more:
                            value_piece(b + 1, 0)
                        if not first:
                            turned_outputs(n - 1, 1 - u, before, 0)
                        exponentials(n, 1, 2)
                        if last and more:
                            value_piece(b + 1, 1)
                        if ahead:
                            split_projection(0, 0, to)
                        if not first:
                            turned_outputs(n - 1, 1 - u, before, 1)
                        exponentials(n, 1, 3)
                        if last and more:
                            value_piece(b + 1, 2)
                        if ahead:
                            split_projection(0, 1, to)
                        if not last:
                            max_row(n + 1, 0)
                        exponentials(n, 1, 4)
                        if last and more:
                            value_piece(b + 1, 3)
                        if ahead:
                            split_projection(1, 0, to)
                            split_projection(1, 1, to)
                        exponentials(n, 1, 5)
                        if last and more:
                            value_piece(b + 1, 4)
                            value_piece(b + 1, 5)
                        if front:
                            root(2 * (b + 1) + 1, rt[:, 0, :], rt[:, 1, :])

                    def couple_step(b, c, more, router=False):
                        for u in range(2):
                            first = is_first_couple(c) and u == 0
                            first_head(b, c, u, first, more, router and u == 0)
                            second_head(b, c, u, first, more, router and u == 0)

                    def value_piece(b, i):
                        t, h0, nh, ng = V_PIECES[i]
                        act.wait_ge(v_full, NV * b + i + 1)
                        if ng:
                            act.activation(gate[:, t, :], four[v_bank[i]][:, nh * DH:nh * DH + ng], ACT.Exp, scale=-1.0)
                        act.activation(v_hi[:, t, h0:h0 + nh, 0:DH],
                                       four[v_bank[i]][:, 0:nh * DH].rearrange("p (h d) -> p h d", d=DH),
                                       ACT.Copy).then_inc(v_hi_done, 1)

                    def batch(b, more):
                        with act.Fori(1, COUPLES - 1) as c:
                            couple_step(b, c, more)
                        couple_step(b, COUPLES - 1, more)
                        for half in range(2):
                            if more:
                                for i in ((V_INNER, V_INNER + 1, V_INNER + 2), (V_INNER + 3,))[half]:
                                    value_piece(b + 1, i)
                            turned_outputs(PAIRS * b + PAIRS - 1, 1, COUPLES * b + COUPLES - 1, half)
                        if more:
                            for i in range(V_INNER + 4, V_EARLY + 2):
                                value_piece(b + 1, i)
                            max_row(PAIRS * (b + 1), 0)
                            for i in range(4):
                                value_piece(b + 1, V_EARLY + 2 + i)
                                split_projection(i // 2, i % 2, PAIRS * (b + 1) + 1)
                        act.wait_ge(root2_in, b + 1)
                        act.activation(rt[:, 1, :], rt[:, 0, :], ACT.Sqrt).then_inc(root2_out, 1)
                        if more:
                            couple_step(b + 1, 0, True, True)
                        else:
                            for i in range(4):
                                turned_x2(b, i, four[i])
                            exp_logits(b)

                    def turned_x2(b, i, bank=None):
                        c, half = i // 2, i % 2
                        act.wait_ge(x2t_full, 4 * b + i + 1)
                        act.activation(x2T[:, c, HALF * half:HALF * half + HALF],
                                       (o_b if bank is None else bank)[:, 0:HALF],
                                       ACT.Copy).then_inc(x2t_copied, 1)

                    def exp_logits(b):
                        act.wait_ge(soft, SOFT_STEPS * b + 2)
                        act.activation(probs[:], probs[:], ACT.Exp).then_inc(logit_exp, 1)

                    gamma_row = tok_gamma.rearrange("(a d) -> a d", a=1)
                    act.dma_start(gamma[:], gamma_row.broadcast_to([P, D])).then_inc(const_in, 16)
                    for g in range(SHIFTS):
                        taps = len(range(g, PATCH, SHIFTS))
                        src = tok_W.rearrange("(r q) d -> r q d", q=PATCH)[:, g:PATCH:SHIFTS, :]
                        act.dma_start(tok_w[ROWS * g:ROWS * g + ROWS, 0:taps, :], src).then_inc(const_in, 16)
                    for c in range(DC):
                        src = norm_w.rearrange("(c p a) -> c p a", p=P, a=1)[c]
                        act.dma_start(nw[:, c:c + 1], src).then_inc(const_in, 16)
                    act.dma_start(gw[:], gate_w.rearrange("(c p) e -> p c e", p=P)).then_inc(const_in, 16)
                    act.sem_inc(st_free, 2)
                    act.wait_ge(const_in, CONSTS_IN)
                    root(0, rt[:, 0, 0:NTI], rt[:, 1, 0:NTI])
                    root(1, rt[:, 0, :], rt[:, 1, :])
                    for i in range(4):
                        turned_x(0, i)
                    for which in range(2):
                        for half in range(2):
                            split_projection(which, half, 0)
                    for i in range(V_EARLY + 2):
                        value_piece(0, i)
                    max_row(0, 0)
                    for i in range(4):
                        value_piece(0, V_EARLY + 2 + i)
                        split_projection(i // 2, i % 2, 1)
                    couple_step(0, 0, True)
                    with act.Fori(0, B - 1) as b:
                        batch(b, True)
                    batch(B - 1, False)

                @block.vector
                def _(dve):
                    def split_projection(which, half, n):
                        dve.wait_ge(pj_hi, 4 * n + 2 * which + half + 1)
                        cols = slice(HALF * half, HALF * half + HALF)
                        dve.tensor_tensor(cut[which][1][:, cols], pj_b[:, half, 0:HALF], cut[which][0][:, cols],
                                          ALU.subtract).then_inc(pj_free, 1)

                    def low_part(n, hd, i):
                        w = sum(q[2] for q in SCORE_PIECES[i])
                        at = PIECE_START[i]
                        dve.wait_ge(st_free, 2 + 12 * n + 6 * hd + i + 1)
                        dve.tensor_tensor(p_lo[:, hd, at:at + w], p32[:, i % RING32, 0:w],
                                          p_hi[:, hd, at:at + w], ALU.subtract).then_inc(p_lo_done, 1)

                    def max_piece(n, hd, i):
                        if i == 0:
                            dve.wait_ge(mt_full, 2 * n)
                        dve.wait_ge(mx_full, 12 * n + 6 * hd + i + 1)
                        at = 0
                        for _, _, w, col in MAX_PIECES[i]:
                            r = dve.tensor_reduce(mx[:, hd, col:col + 1], mx_b[:, i % 2, at:at + w], AX.X, ALU.max)
                            at += w
                        r.then_inc(mx_free, 1)

                    def join_maxima(n, hd):
                        dve.wait_ge(mx_free, 2 + 12 * n + 6 * hd + 6)
                        dve.tensor_tensor(mx[:, hd, 4:6], mx[:, hd, 4:6], mx[:, hd, 6:8], ALU.max).then_inc(max_ready, 1)

                    def denominators(n, hd, head):
                        dve.wait_ge(pv_done, PV_CREDIT + 2 * n + hd + 1)
                        dve.tensor_tensor(den[:, 0, :], o_v[:, :, DH], gate[:, :, ds(head, 1)].rearrange("p t a -> p (t a)"),
                                          ALU.mult).then_inc(normed, 1)

                    def inverses(n, hd):
                        dve.wait_ge(normed, 3 * (2 * n + hd) + 1)
                        dve.reciprocal(den[:, 1, :], den[:, 0, :]).then_inc(normed, 1)

                    def scale_head(n, hd):
                        dve.wait_ge(normed, 3 * (2 * n + hd) + 2)
                        if hd == 0:
                            dve.wait_ge(at_full, 2 * n)
                        scale = den[:, 1, :].rearrange("p (t a) -> p t a", a=1).broadcast_to([P, NT, DH])
                        dve.tensor_tensor(heads_out[:, :, DH * hd:DH * hd + DH], o_v[:, :, 0:DH], scale,
                                          ALU.mult).then_inc(normed, 1)

                    def normalise(n, hd, head):
                        denominators(n, hd, head)
                        inverses(n, hd)
                        scale_head(n, hd)

                    def turned_outputs(n, u, half):
                        dve.wait_ge(at_hi, 2 * n + half + 1)
                        cols = slice(HALF * half, HALF * half + HALF)
                        dve.tensor_tensor(aT[1][:, u, cols], tr_b[:, 0:HALF], aT[0][:, u, cols],
                                          ALU.subtract).then_inc(at_lo, 1)

                    def add_out(b, couple, k):
                        if k == 0:
                            dve.wait_ge(op_added, 3 * couple)
                            dve.wait_ge(h_copied, b)
                        dve.wait_ge(op_full, 3 * couple + k + 1)
                        rows = h[:, 2 * k:2 * k + 2, :].rearrange("p t d -> p (t d)")
                        dve.tensor_tensor(rows, rows, pj_b[:, k % 2, :], ALU.add).then_inc(op_added, 1)

                    def chain(ins, k, s, count):
                        ins.then_inc(s, 1)
                        dve.wait_ge(s, count + k)

                    def token_moments(b):
                        for t in range(NTI):
                            dve.wait_ge(tok_full, NTI * b + t + 1)
                            s = dve.bn_stats(stats[:, t, :], pj_b[:, t, 0:D])
                        s.then_inc(ln, 1)

                    def token_variance(b):
                        dve.wait_ge(ln, LN_STEPS * b + 1)
                        dve.sem_inc(fence, 1)
                        for t in range(NTI):
                            s = dve.bn_aggr(mv[:, t, :], stats[:, t, :])
                        chain(s, 2, ln, LN_STEPS * b)
                        dve.tensor_scalar(rt[:, 0, 0:NTI], mv[:, 0:NTI, 1], LN_EPS, None, ALU.add).then_inc(root_in, 1)

                    def token_inverse(b):
                        dve.wait_ge(root_out, 2 * b + 1)
                        dve.reciprocal(rt[:, 2, 0:NTI], rt[:, 1, 0:NTI]).then_inc(ln, 1)

                    def normed_tokens(b, to):
                        dve.wait_ge(ln, LN_STEPS * b + 3)
                        if not isinstance(b, int):
                            dve.wait_ge(x2_stored, 16 * (b - 1))
                            dve.wait_ge(x2t_full, 4 * (b - 1))
                            dve.wait_ge(h_copied, b - 1)
                        for t in range(NTI):
                            s = dve.tensor_scalar(xn[:, t, :], pj_b[:, t, 0:D], mv[:, t, 0:1], rt[:, 2, t:t + 1],
                                                  ALU.subtract, ALU.mult)
                        chain(s, 4, ln, LN_STEPS * b)
                        for t in range(NTI):
                            s = dve.tensor_tensor(to[:, t, :], xn[:, t, :], gamma[:], ALU.mult)
                        s.then_inc(ln, 1)

                    def moments(b, src, arrived, count):
                        dve.wait_ge(arrived, count)
                        dve.wait_ge(ln, LN_STEPS * b + 5)
                        for t in range(NT):
                            s = dve.bn_stats(stats[:, t, :], src[:, t, :])
                        s.then_inc(ln, 1)

                    def variance(b):
                        dve.wait_ge(ln, LN_STEPS * b + 6)
                        dve.sem_inc(fence, 1)
                        for t in range(NT):
                            s = dve.bn_aggr(mv[:, t, :], stats[:, t, :])
                        chain(s, 7, ln, LN_STEPS * b)
                        dve.tensor_scalar(rt[:, 0, :], mv[:, :, 1], 1.0 + RMS_EPS, RMS_EPS * LN_EPS, ALU.mult,
                                          ALU.add).then_inc(root_in, 1)

                    def normed_x(b, src):
                        dve.wait_ge(root_out, 2 * b + 2)
                        chain(dve.reciprocal(rt[:, 2, :], rt[:, 1, :]), 8, ln, LN_STEPS * b)
                        chain(dve.tensor_tensor(rt[:, 3, :], rt[:, 2, :], rt[:, 2, :], ALU.mult), 9, ln, LN_STEPS * b)
                        chain(dve.scalar_tensor_tensor(out=rt[:, 4, :], in0=rt[:, 3, :], scalar=-0.5, in1=rt[:, 0, :],
                                                       op0=ALU.mult, op1=ALU.mult), 10, ln, LN_STEPS * b)
                        chain(dve.scalar_tensor_tensor(out=rt[:, 3, :], in0=rt[:, 4, :], scalar=1.5, in1=rt[:, 2, :],
                                                       op0=ALU.add, op1=ALU.mult), 11, ln, LN_STEPS * b)
                        for t in range(NT):
                            s = dve.tensor_scalar(xn[:, t, :], src[:, t, :], mv[:, t, 0:1], rt[:, 3, t:t + 1],
                                                  ALU.subtract, ALU.mult)
                        s.then_inc(x_ready, 1)

                    def turned_x(b, i):
                        c, half = i // 2, i % 2
                        dve.wait_ge(xt_hi, 4 * b + i + 1)
                        cols = slice(HALF * half, HALF * half + HALF)
                        dve.scalar_tensor_tensor(out=xT[1][:, c, cols], in0=pj_b[:, half, 0:HALF], scalar=nw[:, c:c + 1],
                                                 in1=xT[0][:, c, cols], op0=ALU.mult,
                                                 op1=ALU.subtract).then_inc(xt_lo, 1)

                    def first_head(b, c, u, first, more, router):
                        p = 2 * c + u
                        n = PAIRS * b + p
                        out_now = u == 1 and not is_first_couple(c)
                        front = is_last_couple(c) and u == 0 and more
                        turn = is_last_couple(c) and u == 1 and more
                        couple = COUPLES * b + c - 1
                        max_piece(n, 1, 0)
                        max_piece(n, 1, 1)
                        if not first:
                            normalise(n - 1, 0, 2 * p - 2)
                        if router:
                            normed_x2(b - 1, True)
                        if turn:
                            normed_x(b + 1, h_next)
                        max_piece(n, 1, 2)
                        if out_now and not turn:
                            add_out(b, couple, 0)
                        max_piece(n, 1, 3)
                        low_part(n, 0, 0)
                        max_piece(n, 1, 4)
                        max_piece(n, 1, 5)
                        join_maxima(n, 1)
                        low_part(n, 0, 1)
                        if turn:
                            turned_x(b + 1, 0)
                            turned_x(b + 1, 1)
                        low_part(n, 0, 2)
                        if turn:
                            turned_x(b + 1, 2)
                            turned_x(b + 1, 3)
                        if out_now and not turn:
                            add_out(b, couple, 1)
                        if front:
                            token_moments(b + 1)
                        low_part(n, 0, 3)
                        if front:
                            token_variance(b + 1)
                        low_part(n, 0, 4)
                        if out_now and not turn:
                            add_out(b, couple, 2)
                        low_part(n, 0, 5)
                        if turn:
                            for k in range(NT // 2):
                                add_out(b, couple, k)

                    def second_head(b, c, u, first, more, router):
                        p = 2 * c + u
                        n = PAIRS * b + p
                        last = is_last_couple(c) and u == 1
                        front = is_last_couple(c) and u == 0 and more
                        ahead = not is_last_couple(c) or (last and more)
                        to = n + 1 if last else n + 2
                        if not first:
                            normalise(n - 1, 1, 2 * p - 1)
                        if not last:
                            max_piece(n + 1, 0, 0)
                        if not last:
                            max_piece(n + 1, 0, 1)
                        if router:
                            shift_logits(b - 1)
                        if front:
                            token_inverse(b + 1)
                        if not last:
                            max_piece(n + 1, 0, 2)
                            max_piece(n + 1, 0, 3)
                        low_part(n, 1, 0)
                        if router:
                            divide_logits(b - 1)
                        if last and more:
                            value_piece(b + 1, 0)
                        if not first:
                            turned_outputs(n - 1, 1 - u, 0)
                        if front:
                            normed_tokens(b + 1, h_next)
                        if not last:
                            max_piece(n + 1, 0, 4)
                        if router:
                            turned_probs(b - 1)
                        if not last:
                            max_piece(n + 1, 0, 5)
                        if ahead:
                            split_projection(0, 0, to)
                        if not last:
                            join_maxima(n + 1, 0)
                        if not first:
                            turned_outputs(n - 1, 1 - u, 1)
                        low_part(n, 1, 1)
                        if last and more:
                            value_piece(b + 1, 1)
                        if ahead:
                            split_projection(0, 1, to)
                        if front:
                            moments(b + 1, h_next, txt_in, 16 * (b + 1))
                        low_part(n, 1, 2)
                        if last and more:
                            value_piece(b + 1, 2)
                        low_part(n, 1, 3)
                        if front:
                            variance(b + 1)
                        low_part(n, 1, 4)
                        if last and more:
                            value_piece(b + 1, 3)
                        if ahead:
                            split_projection(1, 0, to)
                            split_projection(1, 1, to)
                        low_part(n, 1, 5)
                        if last and more:
                            value_piece(b + 1, 4)
                            value_piece(b + 1, 5)

                    def couple_step(b, c, more, router=False):
                        for u in range(2):
                            first = is_first_couple(c) and u == 0
                            first_head(b, c, u, first, more, router and u == 0)
                            second_head(b, c, u, first, more, router and u == 0)

                    def value_piece(b, i):
                        t, h0, nh, ng = V_PIECES[i]
                        dve.wait_ge(v_hi_done, NV * b + i + 1)
                        dve.tensor_tensor(v_lo[:, t, h0:h0 + nh, :],
                                          four[v_bank[i]][:, 0:nh * DH].rearrange("p (h d) -> p h d", d=DH),
                                          v_hi[:, t, h0:h0 + nh, 0:DH], ALU.subtract).then_inc(v_lo_done, 1)
                        if i == NV - 1:
                            dve.tensor_scalar(gate[:], gate[:], 1.0, None, ALU.add).then_inc(gate_ready, 1)

                    def finish(b, more):
                        n = PAIRS * b + PAIRS - 1
                        normalise(n, 0, HEADS - 2)
                        normalise(n, 1, HEADS - 1)
                        for half in range(2):
                            if more:
                                for i in ((V_INNER, V_INNER + 1, V_INNER + 2), (V_INNER + 3,))[half]:
                                    value_piece(b + 1, i)
                            turned_outputs(n, 1, half)
                        if more:
                            for i in range(V_INNER + 4, V_EARLY):
                                value_piece(b + 1, i)
                        for k in range(NT // 2):
                            add_out(b, COUPLES * b + COUPLES - 1, k)
                            if not more and k > 0:
                                x2_moments(b, (2 * k - 2, 2 * k - 1))

                    def x2_moments(b, tiles):
                        dve.wait_ge(op_added, 3 * COUPLES * (b + 1) - 2 + tiles[-1] // 2)
                        for t in tiles:
                            s = dve.bn_stats(stats[:, t, :], h[:, t, :])
                        if tiles[-1] == NT - 1:
                            s.then_inc(ln2, 1)

                    def x2_variance(b):
                        dve.wait_ge(ln2, LN2_STEPS * b + 1)
                        dve.sem_inc(fence, 1)
                        for t in range(NT):
                            s = dve.bn_aggr(mv[:, t, :], stats[:, t, :])
                        chain(s, 2, ln2, LN2_STEPS * b)
                        dve.tensor_scalar(rt[:, 0, :], mv[:, :, 1], LN_EPS, None, ALU.add).then_inc(root2_in, 1)

                    def normed_x2(b, more):
                        dve.wait_ge(root2_out, b + 1)
                        chain(dve.reciprocal(rt[:, 2, :], rt[:, 1, :]), 3, ln2, LN2_STEPS * b)
                        dve.wait_ge(x2_stored, 16 * b)
                        if more:
                            dve.wait_ge(xt_full, 4 * (b + 2))
                        for t in range(NT):
                            s = dve.tensor_scalar(xn[:, t, :], h[:, t, :], mv[:, t, 0:1], rt[:, 2, t:t + 1],
                                                  ALU.subtract, ALU.mult)
                        s.then_inc(x2_ready, 1)

                    def first_maxima(b):
                        for i in range(NPIECE):
                            max_piece(PAIRS * b, 0, i)
                        join_maxima(PAIRS * b, 0)

                    def over_experts(v):
                        return v.rearrange("p (t a) -> p t a", a=1).broadcast_to([P, NT, E])

                    def shift_logits(b):
                        scores = o_b[:, 0:NT * E].rearrange("p (t e) -> p t e", e=E)
                        dve.wait_ge(logits_full, b + 1)
                        chain(dve.tensor_reduce(rsm[:, 0, :], scores, AX.X, ALU.max), 1, soft, SOFT_STEPS * b)
                        dve.tensor_tensor(probs[:], scores, over_experts(rsm[:, 0, :]), ALU.subtract).then_inc(soft, 1)

                    def divide_logits(b):
                        dve.wait_ge(logit_exp, b + 1)
                        chain(dve.tensor_reduce(rsm[:, 1, :], probs[:], AX.X, ALU.add), 3, soft, SOFT_STEPS * b)
                        chain(dve.reciprocal(rsm[:, 2, :], rsm[:, 1, :]), 4, soft, SOFT_STEPS * b)
                        dve.tensor_tensor(probs[:], probs[:], over_experts(rsm[:, 2, :]), ALU.mult).then_inc(probs_ready, 1)

                    def turned_probs(b):
                        dve.wait_ge(p_stored, 16 * b)
                        for half in range(2):
                            dve.wait_ge(pt_full, 2 * b + half + 1)
                            dve.tensor_copy(pT[:, HALF * half:HALF * half + HALF],
                                            pj_b[0:E, half, 0:HALF]).then_inc(pt_copied, 1)

                    def batch(b, more):
                        with dve.Fori(1, COUPLES - 1) as c:
                            couple_step(b, c, more)
                        couple_step(b, COUPLES - 1, more)
                        finish(b, more)
                        if more:
                            first_maxima(b + 1)
                            value_piece(b + 1, V_EARLY)
                            value_piece(b + 1, V_EARLY + 1)
                            x2_moments(b, (0, 1, 2))
                            for i in range(4):
                                value_piece(b + 1, V_EARLY + 2 + i)
                                split_projection(i // 2, i % 2, PAIRS * (b + 1) + 1)
                                if i == 1:
                                    x2_moments(b, (3, 4, 5))
                            x2_variance(b)
                            dve.wait_ge(gate_ready, b + 2)
                            couple_step(b + 1, 0, True, True)
                        else:
                            x2_moments(b, (NT - 2, NT - 1))
                            x2_variance(b)
                            normed_x2(b, False)
                            shift_logits(b)
                            divide_logits(b)
                            turned_probs(b)

                    dve.memset(key_max[64:65], MAX_UNIT).then_inc(consts, 1)
                    dve.sem_inc(pj_free, PJ_CREDIT)
                    dve.sem_inc(mx_free, 2)
                    dve.sem_inc(p_lo_done, RING32)
                    stage_v = stage[:].rearrange("p (c n) -> p c n", c=DC)
                    stage_o = stage[:, 0:PAIRS * D].rearrange("p (k n) -> p k n", k=PAIRS)

                    def split_staged(w, src, arrived, bytes_, done):
                        dve.wait_ge(arrived, bytes_)
                        dve.tensor_copy(w[0][:], src).then_inc(done, 1)
                        dve.wait_ge(done, 1)
                        dve.tensor_tensor(w[1][:], src, w[0][:], ALU.subtract).then_inc(done, 1)

                    split_staged(wv, stage_v, v_w_in, 32, v_w_cut)
                    dve.wait_ge(const_in, CONSTS_IN)
                    token_moments(0)
                    token_variance(0)
                    token_inverse(0)
                    normed_tokens(0, h)
                    moments(0, h, txt_in_0, 16)
                    variance(0)
                    normed_x(0, h)
                    for i in range(4):
                        turned_x(0, i)
                    split_staged(wo, stage_o, o_w_in, 16, o_w_cut)
                    for which in range(2):
                        for half in range(2):
                            split_projection(which, half, 0)
                    for i in range(V_EARLY):
                        value_piece(0, i)
                    first_maxima(0)
                    value_piece(0, V_EARLY)
                    value_piece(0, V_EARLY + 1)
                    for i in range(4):
                        value_piece(0, V_EARLY + 2 + i)
                        split_projection(i // 2, i % 2, 1)
                    dve.wait_ge(gate_ready, 1)
                    couple_step(0, 0, True)
                    with dve.Fori(0, B - 1) as b:
                        batch(b, True)
                    batch(B - 1, False)

            psum.close()
            attn.close()

            exp = ExitStack()
            with exp:
                def sbe(name, shape, dt):
                    return exp.enter_context(nc.sbuf_tensor(name, shape, dt))

                def pse(name, shape):
                    return exp.enter_context(nc.psum_tensor(name, shape, F32))

                R = B * E
                TOP = 8
                ROUNDS = CAP // TOP
                W_CUTS = 16
                W1C = DC * HID * 2 // W_CUTS
                router = [sbe(f"router_{i}", [2 * R, HALF], F32) for i in range(2)]
                halves = sbe("halves", [2 * R, 2, CAP], F32)
                second = sbe("second", [R, 2, CAP], F32)
                best = sbe("best", [R, 2, CAP], F32)
                keep = sbe("keep", [R, 2, CAP], F32)
                top_i = sbe("top_i", [2 * R, CAP], U32)
                row_base = sbe("row_base", [2 * R, 3], F32)
                row_u = sbe("row_u", [2 * R, 2], U32)
                picks = sbe("picks", [P, E, 2, ST], F32)
                ids_now = [sbe(f"ids_now_{u}", [P, ST], U32) for u in range(2)]
                w1_raw = sbe("w1_raw", [P, DC * HID], F32)
                w2_raw = sbe("w2_raw", [P, HC * D], F32)
                w1s = [[sbe(f"w1_{u}_{s}", [P, DC * HID], F32R) for s in ("hi", "lo")] for u in range(2)]
                w2s = [[sbe(f"w2_{u}_{s}", [P, HC * D], F32R) for s in ("hi", "lo")] for u in range(2)]
                rows = [sbe(f"rows_{u}", [P, ST, D], F32) for u in range(2)]
                gT = [sbe(f"gT_{s}", [P, DC, SLOTS], F32R) for s in ("hi", "lo")]
                h32 = sbe("h32", [P, H_CREDIT, HALF], F32)
                hT = [[sbe(f"hT_{g}_{s}", [P, HC, HALF], F32R) for s in ("hi", "lo")] for g in range(2)]
                ys = sbe("ys", [P, ST, D], F32)
                gt_b = pse("gt_b", [P, 2, 512])
                h_b = pse("h_b", [P, H_CREDIT, 512])
                y_b = pse("y_b", [P, 2, 512])

                PICKED = 3 * ROUNDS - 1
                MERGED = PICKED + 7

                def load_picks(eng, entries):
                    eng.wait_ge(picks_stored, 16)
                    rows_of = P // B
                    for b in entries:
                        src = picks_dram[E * b:E * b + E].rearrange("e k (p t) -> p (e k) t", t=ST)
                        dst = picks[rows_of * b:rows_of * b + rows_of].rearrange("p e k t -> p (e k) t")
                        eng.dma_start(dst, src).then_inc(picks_in, 16)

                with nc.Block() as block:
                    @block.sync
                    def _(sp):
                        def load_weights(e):
                            sp.wait_ge(w_cut_lo, W_CUTS * e)
                            sp.dma_start(w1_raw[:].rearrange("p (c n) -> p c n", c=DC),
                                         w1[ds(e, 1)].rearrange("a (c p) n -> (a p) c n", p=P)).then_inc(w_raw_in, 16)
                            sp.dma_start(w2_raw[:].rearrange("p (k n) -> p k n", k=HC),
                                         w2[ds(e, 1)].rearrange("a (k p) n -> (a p) k n", p=P)).then_inc(w_raw_in, 16)

                        sp.wait_ge(p_stored, 16 * B)
                        sp.wait_ge(h_stored, 16 * B)
                        sp.wait_ge(x2_stored, 16 * B)
                        for half in range(2):
                            sp.dma_start(router[0][R * half:R * half + R, :],
                                         p_dram[:, HALF * half:HALF * half + HALF]).then_inc(rows_in, 16)
                        load_weights(0)
                        sp.wait_ge(pick, PICKED + 2)
                        sp.dma_start(second[:], halves[R:2 * R]).then_inc(second_in, 16)
                        sp.wait_ge(pick, MERGED)
                        sp.dma_start(picks_dram[:], best[:]).then_inc(picks_stored, 16)
                        load_picks(sp, (0, 1))
                        with sp.Fori(1, E) as e:
                            load_weights(e)

                    @block.gpsimd
                    def _(pool):
                        def fetch_rows(e, u):
                            if not isinstance(e, int) or e > 1:
                                pool.wait_ge(scattered, 16 * ST * (e - 1))
                            ids = picks[:, ds(e, 1), 1, :].rearrange("p a t -> p (a t)")
                            pool.tensor_copy(ids_now[u][:], ids).then_inc(ids_copied, 1)
                            wait_apart(pool, ids_copied, e + 1)
                            for t in range(ST):
                                pool.indirect_dma_start(
                                    out=rows[u][:, t, :], out_offset=None, in_=x2_dram,
                                    in_offset=bass.IndirectOffsetOnAxis(ap=ids_now[u][:, t:t + 1], axis=0)
                                ).then_inc(gathered[u][t // TH], 16)

                        def scatter_rows(e, u):
                            pool.wait_ge(scattered, 16 * ST * e)
                            for t in range(ST):
                                pool.wait_ge(scattered, 16 * (ST * e + t))
                                wait_apart(pool, y_ready, ST * e + t + 1)
                                pool.indirect_dma_start(
                                    out=out_rows, out_offset=bass.IndirectOffsetOnAxis(ap=ids_now[u][:, t:t + 1], axis=0),
                                    in_=ys[:, t, :], in_offset=None, compute_op=ALU.add).then_inc(scattered, 16)

                        for half in range(2):
                            of = slice(R * half, R * half + R)
                            pool.iota(row_u[of, 0:1], pattern=[[0, 1]], base=0, channel_multiplier=1).then_inc(row_id, 1)
                            pool.wait_ge(row_id, 2 * half + 1)
                            pool.memset(row_base[of, 2:3], float(HALF * half)).then_inc(row_id, 1)
                            pool.wait_ge(row_id, 2 * half + 2)
                        for i in range(W_CUTS):
                            k = i % (W_CUTS // 2)
                            raw, to = (w1_raw, w1s[0]) if i < W_CUTS // 2 else (w2_raw, w2s[0])
                            c = slice(W1C * k, W1C * k + W1C)
                            pool.wait_ge(w_cut_hi, i + 1)
                            pool.tensor_tensor(to[1][:, c], raw[:, c], to[0][:, c], ALU.subtract).then_inc(w_cut_lo, 1)
                        pool.wait_ge(picks_in, 16 * B)
                        fetch_rows(0, 0)
                        with pool.Fori(0, E // 2 - 1) as i:
                            fetch_rows(2 * i + 1, 1)
                            scatter_rows(2 * i, 0)
                            fetch_rows(2 * i + 2, 0)
                            scatter_rows(2 * i + 1, 1)
                        fetch_rows(E - 1, 1)
                        scatter_rows(E - 2, 0)
                        scatter_rows(E - 1, 1)
                        pool.wait_ge(scattered, 16 * ST * E)

                    @block.tensor
                    def _(pe):
                        def three_terms(dst, lhs, rhs, first, last):
                            terms = [(0, 0), (1, 0), (0, 1)]
                            for i, (a, c) in enumerate(terms):
                                mm = pe.matmul(dst, lhs[a], rhs[c], start=first and i == 0, stop=last and i == 2)
                            return mm

                        def turn_rows(e, u, i, quarters):
                            for k in quarters:
                                half, c = k // 2, k % 2
                                if c == 0:
                                    pe.wait_ge(gathered[u][half], 16 * TH * i)
                                pe.wait_ge(gt_lo, 4 * e + max(k - 1, 0))
                                for t in range(TH):
                                    mm = pe.transpose(gt_b[:, k % 2, t * P:t * P + P],
                                                      rows[u][:, TH * half + t, c * P:c * P + P], ident[:])
                                mm.then_inc(gt_full, 1)

                        def first_layer(e, u, g):
                            if g == 0:
                                pe.wait_ge(w_cut_lo, W_CUTS * (e + 1))
                                pe.wait_ge(gt_lo, 4 * e + 2)
                            elif g == 1:
                                pe.wait_ge(gt_lo, 4 * e + 4)
                            for k in range(HC):
                                i = HC * g + k
                                pe.wait_ge(h_lo_done, 2 * HC * e + i + 1)
                                for c in range(DC):
                                    mm = three_terms(h_b[:, i % H_CREDIT, 0:HALF],
                                                     [w[:, c * HID + k * P:c * HID + k * P + P] for w in w1s[u]],
                                                     [a[:, c, HALF * g:HALF * g + HALF] for a in gT],
                                                     c == 0, c == DC - 1)
                                mm.then_inc(h_full, 1)

                        def second_layer(e, u, g, tiles):
                            pe.wait_ge(h_lo_done, H_CREDIT + 2 * HC * e + HC * (g + 1))
                            for t in tiles:
                                i = TH * g + t
                                pe.wait_ge(y_ready, ST * e + max(i - 1, 0))
                                for k in range(HC):
                                    mm = three_terms(y_b[:, i % 2, 0:D],
                                                     [a[:, k, t * P:t * P + P] for a in hT[g]],
                                                     [w[:, k * D:k * D + D] for w in w2s[u]],
                                                     k == 0, k == HC - 1)
                                mm.then_inc(y_full, 1)

                        def expert(i, u, last):
                            e = 2 * i + u
                            first_layer(e, u, 0)
                            first_layer(e, u, 1)
                            second_layer(e, u, 0, (0, 1, 2))
                            if not last:
                                turn_rows(e + 1, 1 - u, i + 1 + u, (0, 1))
                            second_layer(e, u, 1, (0,))
                            if not last:
                                turn_rows(e + 1, 1 - u, i + 1 + u, (2, 3))
                            second_layer(e, u, 1, (1, 2))

                        pe.sem_inc(y_full, ST)
                        turn_rows(0, 0, 1, range(4))
                        with pe.Fori(0, E // 2 - 1) as i:
                            expert(i, 0, False)
                            expert(i, 1, False)
                        expert(E // 2 - 1, 0, False)
                        expert(E // 2 - 1, 1, True)

                    @block.scalar
                    def _(act):
                        def split_weights(e, u, i):
                            if i == 0:
                                act.wait_ge(w_raw_in, 32 * (e + 1))
                                act.wait_ge(y_full, ST * e)
                            raw, to = (w1_raw, w1s[u][0]) if i < W_CUTS // 2 else (w2_raw, w2s[u][0])
                            c = slice(W1C * (i % (W_CUTS // 2)), W1C * (i % (W_CUTS // 2)) + W1C)
                            act.activation(to[:, c], raw[:, c], ACT.Copy).then_inc(w_cut_hi, 1)

                        def turned_rows(e):
                            for i in range(4):
                                half, c = i // 2, i % 2
                                act.wait_ge(gt_full, 4 * e + i + 1)
                                if i == 0:
                                    act.wait_ge(h_full, 2 * HC * e)
                                act.activation(gT[0][:, c, HALF * half:HALF * half + HALF], gt_b[:, i % 2, 0:HALF],
                                               ACT.Copy).then_inc(gt_hi, 1)

                        def expert(e, u, last):
                            for i in range(2 * HC):
                                g, k = i // HC, i % HC
                                act.wait_ge(h_full, 2 * HC * e + i + 1)
                                act.wait_ge(h_lo_done, 2 * HC * e + i + 1)
                                if k == 0:
                                    act.wait_ge(y_full, ST * e + TH * (g + 1))
                                act.activation(h32[:, i % H_CREDIT, :], h_b[:, i % H_CREDIT, 0:HALF], ACT.Gelu)
                                act.activation(hT[g][0][:, k, :], h_b[:, i % H_CREDIT, 0:HALF], ACT.Gelu).then_inc(h_act, 1)
                            if not last:
                                for i in range(W_CUTS // 2):
                                    split_weights(e + 1, 1 - u, i)
                                turned_rows(e + 1)
                                for i in range(W_CUTS // 2, W_CUTS):
                                    split_weights(e + 1, 1 - u, i)

                        for i in range(W_CUTS):
                            split_weights(0, 0, i)
                        load_picks(act, (2, 3))
                        turned_rows(0)
                        with act.Fori(0, E // 2 - 1) as i:
                            expert(2 * i, 0, False)
                            expert(2 * i + 1, 1, False)
                        expert(E - 2, 0, False)
                        expert(E - 1, 1, True)

                    @block.vector
                    def _(dve):
                        def split_weights(e, u, i):
                            k = i % (W_CUTS // 2)
                            raw, to = (w1_raw, w1s[u]) if i < W_CUTS // 2 else (w2_raw, w2s[u])
                            c = slice(W1C * k, W1C * k + W1C)
                            dve.wait_ge(w_cut_hi, W_CUTS * e + i + 1)
                            dve.tensor_tensor(to[1][:, c], raw[:, c], to[0][:, c], ALU.subtract).then_inc(w_cut_lo, 1)

                        def turned_rows(e, quarters):
                            for i in quarters:
                                half, c = i // 2, i % 2
                                dve.wait_ge(gt_hi, 4 * e + i + 1)
                                cols = slice(HALF * half, HALF * half + HALF)
                                dve.tensor_tensor(gT[1][:, c, cols], gt_b[:, i % 2, 0:HALF], gT[0][:, c, cols],
                                                  ALU.subtract).then_inc(gt_lo, 1)

                        def outputs(e, g, tiles):
                            if g == 0 and 0 in tiles:
                                dve.wait_ge(scattered, 16 * ST * e)
                            for t in tiles:
                                i = TH * g + t
                                dve.wait_ge(y_full, ST * (e + 1) + i + 1)
                                dve.tensor_scalar(ys[:, i, :], y_b[:, i % 2, 0:D],
                                                  picks[:, ds(e, 1), 0, i:i + 1].rearrange("p a t -> p (a t)"), None,
                                                  ALU.mult).then_inc(y_ready, 1)

                        def expert(e, u, last):
                            for i in range(2 * HC):
                                g, k = i // HC, i % HC
                                dve.wait_ge(h_act, 2 * HC * e + i + 1)
                                dve.tensor_tensor(hT[g][1][:, k, :], h32[:, i % H_CREDIT, :], hT[g][0][:, k, :],
                                                  ALU.subtract).then_inc(h_lo_done, 1)
                            for t in range(TH):
                                outputs(e, 0, (t,))
                                if not last and t < TH - 1:
                                    for i in range(4):
                                        split_weights(e + 1, 1 - u, 4 * t + i)
                            if not last:
                                turned_rows(e + 1, (0, 1))
                            outputs(e, 1, (0,))
                            if not last:
                                turned_rows(e + 1, (2, 3))
                            for t in (1, 2):
                                if not last:
                                    for i in range(4):
                                        split_weights(e + 1, 1 - u, W_CUTS // 2 + 4 * (t - 1) + i)
                                outputs(e, 1, (t,))

                        dve.sem_inc(h_lo_done, H_CREDIT)
                        dve.wait_ge(row_id, 4)
                        dve.tensor_scalar(row_u[:, 1:2], row_u[:, 0:1], E.bit_length() - 1, None,
                                          ALU.logical_shift_right).then_inc(row_id, 1)
                        dve.wait_ge(row_id, 5)
                        dve.tensor_scalar(row_base[:, 0:1], row_u[:, 1:2], float(N), None, ALU.mult).then_inc(row_id, 1)
                        dve.wait_ge(row_id, 6)
                        dve.tensor_tensor(row_base[:, 1:2], row_base[:, 0:1], row_base[:, 2:3], ALU.add).then_inc(row_id, 1)
                        dve.wait_ge(rows_in, 32)
                        for i in range(ROUNDS):
                            now, then = router[i % 2], router[(i + 1) % 2]
                            eight = slice(TOP * i, TOP * i + TOP)
                            dve.max(halves[:, 0, eight], now[:]).then_inc(pick, 1)
                            dve.wait_ge(pick, 3 * i + 1)
                            dve.max_index(top_i[:, eight], halves[:, 0, eight], now[:]).then_inc(pick, 1)
                            if i < ROUNDS - 1:
                                dve.match_replace(then[:], halves[:, 0, eight], now[:], -1.0).then_inc(pick, 1)
                                dve.wait_ge(pick, 3 * i + 3)
                        dve.wait_ge(pick, PICKED)
                        dve.tensor_copy(halves[:, 1, :], top_i[:]).then_inc(pick, 1)
                        dve.wait_ge(row_id, 7)
                        dve.wait_ge(pick, PICKED + 1)
                        dve.tensor_scalar(halves[:, 1, :], halves[:, 1, :], row_base[:, 1:2], None, ALU.add).then_inc(pick, 1)
                        dve.wait_ge(pick, PICKED + 2)
                        dve.wait_ge(second_in, 16)
                        first_p, first_i = halves[0:R, 0, :], halves[0:R, 1, :]
                        second_p, second_i = second[:, 0, ::-1], second[:, 1, ::-1]
                        dve.tensor_tensor(keep[:, 0, :], first_p, second_p, ALU.is_ge).then_inc(pick, 1)
                        dve.tensor_tensor(keep[:, 1, :], first_i, second_i, ALU.subtract).then_inc(pick, 1)
                        dve.tensor_tensor(best[:, 0, :], first_p, second_p, ALU.max).then_inc(pick, 1)
                        dve.wait_ge(pick, PICKED + 4)
                        dve.tensor_tensor(best[:, 1, :], keep[:, 0, :], keep[:, 1, :], ALU.mult).then_inc(pick, 1)
                        dve.wait_ge(pick, PICKED + 6)
                        dve.tensor_tensor(best[:, 1, :], best[:, 1, :], second_i, ALU.add).then_inc(pick, 1)
                        dve.wait_ge(picks_in, 16 * B)
                        turned_rows(0, range(4))
                        with dve.Fori(0, E // 2 - 1) as i:
                            expert(2 * i, 0, False)
                            expert(2 * i + 1, 1, False)
                        expert(E - 2, 0, False)
                        expert(E - 1, 1, True)


_INS = ["x", "txt", "L0_tok_W", "L0_tok_gamma", "L0_attn_norm_w", "L0_attn_Wq", "L0_attn_Wkv", "L0_attn_Wout",
        "L0_attn_Wg", "L0_ffn_gate_w", "L0_ffn_w1", "L0_ffn_w2"]


def kernel(**inputs):
    import numpy as _np
    import concourse.bacc as _bacc
    from concourse import mybir as _mybir
    from concourse.bass_utils import run_bass_kernel_spmd as _run

    nc = _bacc.Bacc("TRN2", target_bir_lowering=False, num_devices=1)
    arrays, args = {}, []
    for name in _INS:
        a = _np.ascontiguousarray(inputs[name])
        arrays[f"in_{name}"] = a
        args.append(nc.dram_tensor(f"in_{name}", a.shape, _mybir.dt.from_np(a.dtype), kind="ExternalInput").ap())
    B, _, img, _ = inputs["x"].shape
    _, n_txt, d = inputs["txt"].shape
    shape = (B, (img // PATCH) ** 2 + n_txt, d)
    args.append(nc.dram_tensor("out_0", shape, _mybir.dt.float32, kind="ExternalOutput").ap())
    fusion_block_kernel(nc, *args)
    r = _run(nc, [arrays], core_ids=[0])
    return r.results[0]["out_0"]
```
